# Optimizing a Trainium2 kernel written in Bass

```python
import numpy as np
import jax
import jax.numpy as jnp

def _softmax(x, axis=-1):
    return jax.nn.softmax(x, axis=axis)

def _gelu(x):
    return jax.nn.gelu(x, approximate=True)

def _silu(x):
    return jax.nn.silu(x)

def _sigmoid(x):
    return jax.nn.sigmoid(x)

def _layernorm(x, axis=-1, eps=1e-05):
    m = jnp.mean(x, axis=axis, keepdims=True)
    v = jnp.var(x, axis=axis, keepdims=True)
    return (x - m) / jnp.sqrt(v + eps)

def _scatter_add(tgt, idx, src, axis=0):
    return tgt.at[idx].add(src)

def _segment_sum(src, seg, n):
    return jax.ops.segment_sum(src, seg, n)
kernel_name = 'mk_decoder_preln_d1_seqx_r8_833931'

def setup_inputs(seed: int=0):
    np.random.seed(seed)
    _w = jnp.asarray

    def _rec_inputs():
        import jax
        import jax.numpy as jnp
        _rk = jax.random.key(seed)
        x = 7.22e-05 + 1 * jax.random.normal(jax.random.fold_in(_rk, 1), (8, 256, 128), jnp.float32)
        _lenS = 256 - jax.random.randint(jax.random.fold_in(_rk, 7), (8,), 0, max(1, 256 // 4) + 1, jnp.int32)
        _lenS2 = 1601 - jax.random.randint(jax.random.fold_in(_rk, 8), (8,), 0, max(1, 1601 // 4) + 1, jnp.int32)
        _ctx_768P = jax.random.normal(jax.random.fold_in(_rk, 11), (8, 16, 96), jnp.float32)
        _ctx_768c = jax.random.dirichlet(jax.random.fold_in(_rk, 511), 0.3 * jnp.ones((16,), jnp.float32), (8, 1601))
        _ctx_768t = jnp.einsum('bsk,bkd->bsd', _ctx_768c, _ctx_768P)
        _ctx_768t = _ctx_768t * jax.lax.rsqrt(jnp.mean(jnp.square(_ctx_768t)) + 1e-12) * 0.953939
        ctx_768 = 2.09791e-05 + 1.00001 * (_ctx_768t + 0.3 * jax.random.normal(jax.random.fold_in(_rk, 611), (8, 1601, 96), jnp.float32))
        return (x, ctx_768)
    x, ctx_768 = _rec_inputs()

    def _L0_attn_setup():
        import jax, jax.numpy as jnp
        import numpy as np
        N_HEADS = 16
        EPS = 1e-06
        key = jax.random.key(seed)
        ks = jax.random.split(key, 10)
        B, T, D = (2, 256, 128)
        x = jax.random.normal(ks[0], (B, T, D), dtype=jnp.float32)
        norm_w = jnp.ones((D,), dtype=jnp.float32)
        bound = float(np.sqrt(6.0 / (D + D)))

        def lin(k):
            return jax.random.uniform(k, (D, D), dtype=jnp.float32, minval=-bound, maxval=bound)
        Wq, Wk, Wv, Wo = (lin(ks[1]), lin(ks[2]), lin(ks[3]), lin(ks[4]))
        bq = jnp.zeros((D,), dtype=jnp.float32)
        bk = jnp.zeros((D,), dtype=jnp.float32)
        bv = jnp.zeros((D,), dtype=jnp.float32)
        bo = jnp.zeros((D,), dtype=jnp.float32)
        return {'x': x, 'norm_w': norm_w, 'Wq': Wq, 'bq': bq, 'Wk': Wk, 'bk': bk, 'Wv': Wv, 'bv': bv, 'Wo': Wo, 'bo': bo}
    _L0_attn_all = _L0_attn_setup()
    _L0_attn_in = {k: v for k, v in _L0_attn_all.items() if k in ('norm_w', 'Wq', 'bq', 'Wk', 'bk', 'Wv', 'bv', 'Wo', 'bo')}
    del _L0_attn_all

    def _L0_xattn_setup():
        import jax, jax.numpy as jnp
        import numpy as np
        N_HEAD = 16
        D_EMBED = 128
        D_CROSS = 96
        D_HEAD = D_EMBED // N_HEAD
        key = jax.random.key(seed)
        ks = jax.random.split(key, 8)
        B, SQ, SKV = (2, 512, 256)
        s_q = 1.0 / np.sqrt(D_EMBED)
        s_kv = 1.0 / np.sqrt(D_CROSS)
        return {'x': jax.random.normal(ks[0], (B, SQ, D_EMBED), jnp.float32), 'y': jax.random.normal(ks[1], (B, SKV, D_CROSS), jnp.float32), 'Wq': jax.random.normal(ks[2], (D_EMBED, D_EMBED), jnp.float32) * s_q, 'bq': jnp.zeros((D_EMBED,), jnp.float32), 'Wkv': jax.random.normal(ks[3], (D_CROSS, 2 * D_EMBED), jnp.float32) * s_kv, 'bkv': jnp.zeros((2 * D_EMBED,), jnp.float32), 'Wo': jax.random.normal(ks[4], (D_EMBED, D_EMBED), jnp.float32) * s_q, 'bo': jnp.zeros((D_EMBED,), jnp.float32)}
    _L0_xattn_all = _L0_xattn_setup()
    _L0_xattn_in = {k: v for k, v in _L0_xattn_all.items() if k in ('Wq', 'bq', 'Wkv', 'bkv', 'Wo', 'bo')}
    del _L0_xattn_all

    def _L0_ffn_setup():
        import jax, jax.numpy as jnp
        import numpy as np
        B, S, D = (2, 128, 128)
        H, HD = (16, 64)
        E_R = 31
        K_ACT = 3
        INTER = 128
        EPS = 1e-05
        BASE = 10000.0

        def _rmsnorm(x, gamma):
            rms = jnp.sqrt(jnp.mean(x * x, axis=-1, keepdims=True) + EPS)
            return x / rms * gamma

        def _rope(x, theta):
            seq = x.shape[2]
            angles = jnp.arange(seq, dtype=theta.dtype)[:, None] * theta
            cos = jnp.cos(angles)[None, None]
            sin = jnp.sin(angles)[None, None]
            x1, x2 = (x[..., 0::2], x[..., 1::2])
            return jnp.concatenate([x1 * cos - x2 * sin, x1 * sin + x2 * cos], axis=-1)

        def _forward(x, theta, gamma1, gamma2, q_w, q_b, k_w, k_b, v_w, v_b, o_w, o_b, router_w, router_b, sh_w1, sh_b1, sh_w2, sh_b2, re_w1, re_b1, re_w2, re_b2):
            b, s, d = x.shape
            xn = _rmsnorm(x, gamma1)
            q = (xn @ q_w + q_b).reshape(b, s, H, HD).transpose(0, 2, 1, 3)
            k = (xn @ k_w + k_b).reshape(b, s, H, HD).transpose(0, 2, 1, 3)
            v = (xn @ v_w + v_b).reshape(b, s, H, HD).transpose(0, 2, 1, 3)
            q = _rope(q, theta)
            k = _rope(k, theta)
            scale = 1.0 / np.sqrt(HD)
            scores = jnp.einsum('bhqd,bhkd->bhqk', q, k) * scale
            causal = jnp.tril(jnp.ones((s, s), dtype=bool))
            scores = jnp.where(causal, scores, -jnp.inf)
            attn = jax.nn.softmax(scores, axis=-1)
            ctx = jnp.einsum('bhqk,bhkd->bhqd', attn, v)
            ctx = ctx.transpose(0, 2, 1, 3).reshape(b, s, H * HD)
            attn_out = ctx @ o_w + o_b + xn
            an = _rmsnorm(attn_out, gamma2)
            shared = jax.nn.gelu(an @ sh_w1 + sh_b1, approximate=False) @ sh_w2 + sh_b2
            logits = an @ router_w + router_b
            aff = jax.nn.softmax(logits, axis=-1)
            topv, topi = jax.lax.top_k(aff, K_ACT)
            gates = jnp.sum(jax.nn.one_hot(topi, E_R, dtype=aff.dtype) * topv[..., None], axis=-2)
            h = jax.nn.gelu(jnp.einsum('bsd,edh->besh', an, re_w1) + re_b1[None, :, None, :], approximate=False)
            routed = jnp.einsum('bse,besh,ehd->bsd', gates, h, re_w2) + jnp.einsum('bse,ed->bsd', gates, re_b2)
            return shared + routed + an + attn_out
        key = jax.random.key(seed)
        ks = jax.random.split(key, 24)
        s = 0.02
        theta = BASE ** (-jnp.arange(HD // 2, dtype=jnp.float32) * 2.0 / HD)
        inp = {'x': jax.random.normal(ks[0], (B, S, D), jnp.float32), 'positions': jnp.arange(S, dtype=jnp.int32), 'theta': theta, 'gamma1': jnp.ones((D,), jnp.float32), 'gamma2': jnp.ones((D,), jnp.float32), 'q_w': jax.random.normal(ks[1], (D, H * HD), jnp.float32) * s, 'q_b': jnp.zeros((H * HD,), jnp.float32), 'k_w': jax.random.normal(ks[2], (D, H * HD), jnp.float32) * s, 'k_b': jnp.zeros((H * HD,), jnp.float32), 'v_w': jax.random.normal(ks[3], (D, H * HD), jnp.float32) * s, 'v_b': jnp.zeros((H * HD,), jnp.float32), 'o_w': jax.random.normal(ks[4], (H * HD, D), jnp.float32) * s, 'o_b': jnp.zeros((D,), jnp.float32), 'router_w': jax.random.normal(ks[5], (D, E_R), jnp.float32) * s, 'router_b': jnp.zeros((E_R,), jnp.float32), 'sh_w1': jax.random.normal(ks[6], (D, INTER), jnp.float32) * s, 'sh_b1': jnp.zeros((INTER,), jnp.float32), 'sh_w2': jax.random.normal(ks[7], (INTER, D), jnp.float32) * s, 'sh_b2': jnp.zeros((D,), jnp.float32), 're_w1': jax.random.normal(ks[8], (E_R, D, INTER), jnp.float32) * s, 're_b1': jnp.zeros((E_R, INTER), jnp.float32), 're_w2': jax.random.normal(ks[9], (E_R, INTER, D), jnp.float32) * s, 're_b2': jnp.zeros((E_R, D), jnp.float32)}
        return inp
    _L0_ffn_all = _L0_ffn_setup()
    _L0_ffn_in = {k: v for k, v in _L0_ffn_all.items() if k in ('positions', 'theta', 'gamma1', 'gamma2', 'q_w', 'q_b', 'k_w', 'k_b', 'v_w', 'v_b', 'o_w', 'o_b', 'router_w', 'router_b', 'sh_w1', 'sh_b1', 'sh_w2', 'sh_b2', 're_w1', 're_b1', 're_w2', 're_b2')}
    del _L0_ffn_all
    return {'x': x, 'ctx_768': ctx_768, 'L0_attn_norm_w': _L0_attn_in['norm_w'], 'L0_attn_Wq': _L0_attn_in['Wq'], 'L0_attn_bq': _L0_attn_in['bq'], 'L0_attn_Wk': _L0_attn_in['Wk'], 'L0_attn_bk': _L0_attn_in['bk'], 'L0_attn_Wv': _L0_attn_in['Wv'], 'L0_attn_bv': _L0_attn_in['bv'], 'L0_attn_Wo': _L0_attn_in['Wo'], 'L0_attn_bo': _L0_attn_in['bo'], 'L0_xattn_Wq': _L0_xattn_in['Wq'], 'L0_xattn_bq': _L0_xattn_in['bq'], 'L0_xattn_Wkv': _L0_xattn_in['Wkv'], 'L0_xattn_bkv': _L0_xattn_in['bkv'], 'L0_xattn_Wo': _L0_xattn_in['Wo'], 'L0_xattn_bo': _L0_xattn_in['bo'], 'L0_ffn_positions': _L0_ffn_in['positions'], 'L0_ffn_theta': _L0_ffn_in['theta'], 'L0_ffn_gamma1': _L0_ffn_in['gamma1'], 'L0_ffn_gamma2': _L0_ffn_in['gamma2'], 'L0_ffn_q_w': _L0_ffn_in['q_w'], 'L0_ffn_q_b': _L0_ffn_in['q_b'], 'L0_ffn_k_w': _L0_ffn_in['k_w'], 'L0_ffn_k_b': _L0_ffn_in['k_b'], 'L0_ffn_v_w': _L0_ffn_in['v_w'], 'L0_ffn_v_b': _L0_ffn_in['v_b'], 'L0_ffn_o_w': _L0_ffn_in['o_w'], 'L0_ffn_o_b': _L0_ffn_in['o_b'], 'L0_ffn_router_w': _L0_ffn_in['router_w'], 'L0_ffn_router_b': _L0_ffn_in['router_b'], 'L0_ffn_sh_w1': _L0_ffn_in['sh_w1'], 'L0_ffn_sh_b1': _L0_ffn_in['sh_b1'], 'L0_ffn_sh_w2': _L0_ffn_in['sh_w2'], 'L0_ffn_sh_b2': _L0_ffn_in['sh_b2'], 'L0_ffn_re_w1': _L0_ffn_in['re_w1'], 'L0_ffn_re_b1': _L0_ffn_in['re_b1'], 'L0_ffn_re_w2': _L0_ffn_in['re_w2'], 'L0_ffn_re_b2': _L0_ffn_in['re_b2']}

def reference(x, ctx_768, L0_attn_norm_w, L0_attn_Wq, L0_attn_bq, L0_attn_Wk, L0_attn_bk, L0_attn_Wv, L0_attn_bv, L0_attn_Wo, L0_attn_bo, L0_xattn_Wq, L0_xattn_bq, L0_xattn_Wkv, L0_xattn_bkv, L0_xattn_Wo, L0_xattn_bo, L0_ffn_positions, L0_ffn_theta, L0_ffn_gamma1, L0_ffn_gamma2, L0_ffn_q_w, L0_ffn_q_b, L0_ffn_k_w, L0_ffn_k_b, L0_ffn_v_w, L0_ffn_v_b, L0_ffn_o_w, L0_ffn_o_b, L0_ffn_router_w, L0_ffn_router_b, L0_ffn_sh_w1, L0_ffn_sh_b1, L0_ffn_sh_w2, L0_ffn_sh_b2, L0_ffn_re_w1, L0_ffn_re_b1, L0_ffn_re_w2, L0_ffn_re_b2):
    import jax
    import jax.numpy as jnp

    def _L0_attn_ref(x, norm_w, Wq, bq, Wk, bk, Wv, bv, Wo, bo):
        import jax, jax.numpy as jnp
        import numpy as np
        N_HEADS = 16
        EPS = 1e-06
        B, T, D = x.shape
        H = N_HEADS
        hd = D // H
        xn = x * jax.lax.rsqrt(jnp.mean(x * x, axis=-1, keepdims=True) + EPS) * norm_w
        q = (xn @ Wq.T + bq).reshape(B, T, H, hd).transpose(0, 2, 1, 3)
        k = (xn @ Wk.T + bk).reshape(B, T, H, hd).transpose(0, 2, 1, 3)
        v = (xn @ Wv.T + bv).reshape(B, T, H, hd).transpose(0, 2, 1, 3)
        scale = 1.0 / jnp.sqrt(jnp.asarray(hd, dtype=x.dtype))
        scores = jnp.einsum('bhqd,bhkd->bhqk', q, k) * scale
        causal = jnp.triu(jnp.ones((T, T), dtype=bool), k=1)
        scores = jnp.where(causal, jnp.asarray(-jnp.inf, dtype=scores.dtype), scores)
        attn = jax.nn.softmax(scores, axis=-1)
        out = jnp.einsum('bhqk,bhkd->bhqd', attn, v)
        out = out.transpose(0, 2, 1, 3).reshape(B, T, D)
        out = out @ Wo.T + bo
        return xn + out

    def _L0_xattn_ref(x, y, Wq, bq, Wkv, bkv, Wo, bo):
        import jax, jax.numpy as jnp
        import numpy as np
        N_HEAD = 16
        D_EMBED = 128
        D_CROSS = 96
        D_HEAD = D_EMBED // N_HEAD
        B, SQ, _ = x.shape
        q = x @ Wq + bq
        kv = y @ Wkv + bkv
        k, v = jnp.split(kv, 2, axis=-1)
        q = q.reshape(B, SQ, N_HEAD, D_HEAD).transpose(0, 2, 1, 3)
        k = k.reshape(B, -1, N_HEAD, D_HEAD).transpose(0, 2, 1, 3)
        v = v.reshape(B, -1, N_HEAD, D_HEAD).transpose(0, 2, 1, 3)
        scale = 1.0 / np.sqrt(D_HEAD)
        attn = jnp.einsum('bhqd,bhkd->bhqk', q, k) * scale
        attn = jax.nn.softmax(attn, axis=-1)
        out = jnp.einsum('bhqk,bhkd->bhqd', attn, v)
        out = out.transpose(0, 2, 1, 3).reshape(B, SQ, D_EMBED)
        return out @ Wo + bo

    def _L0_ffn_ref(x, positions, theta, gamma1, gamma2, q_w, q_b, k_w, k_b, v_w, v_b, o_w, o_b, router_w, router_b, sh_w1, sh_b1, sh_w2, sh_b2, re_w1, re_b1, re_w2, re_b2):
        import jax, jax.numpy as jnp
        import numpy as np
        B, S, D = (2, 128, 128)
        H, HD = (16, 64)
        E_R = 31
        K_ACT = 3
        INTER = 128
        EPS = 1e-05
        BASE = 10000.0

        def _rmsnorm(x, gamma):
            rms = jnp.sqrt(jnp.mean(x * x, axis=-1, keepdims=True) + EPS)
            return x / rms * gamma

        def _rope(x, theta):
            seq = x.shape[2]
            angles = jnp.arange(seq, dtype=theta.dtype)[:, None] * theta
            cos = jnp.cos(angles)[None, None]
            sin = jnp.sin(angles)[None, None]
            x1, x2 = (x[..., 0::2], x[..., 1::2])
            return jnp.concatenate([x1 * cos - x2 * sin, x1 * sin + x2 * cos], axis=-1)

        def _forward(x, theta, gamma1, gamma2, q_w, q_b, k_w, k_b, v_w, v_b, o_w, o_b, router_w, router_b, sh_w1, sh_b1, sh_w2, sh_b2, re_w1, re_b1, re_w2, re_b2):
            b, s, d = x.shape
            xn = _rmsnorm(x, gamma1)
            q = (xn @ q_w + q_b).reshape(b, s, H, HD).transpose(0, 2, 1, 3)
            k = (xn @ k_w + k_b).reshape(b, s, H, HD).transpose(0, 2, 1, 3)
            v = (xn @ v_w + v_b).reshape(b, s, H, HD).transpose(0, 2, 1, 3)
            q = _rope(q, theta)
            k = _rope(k, theta)
            scale = 1.0 / np.sqrt(HD)
            scores = jnp.einsum('bhqd,bhkd->bhqk', q, k) * scale
            causal = jnp.tril(jnp.ones((s, s), dtype=bool))
            scores = jnp.where(causal, scores, -jnp.inf)
            attn = jax.nn.softmax(scores, axis=-1)
            ctx = jnp.einsum('bhqk,bhkd->bhqd', attn, v)
            ctx = ctx.transpose(0, 2, 1, 3).reshape(b, s, H * HD)
            attn_out = ctx @ o_w + o_b + xn
            an = _rmsnorm(attn_out, gamma2)
            shared = jax.nn.gelu(an @ sh_w1 + sh_b1, approximate=False) @ sh_w2 + sh_b2
            logits = an @ router_w + router_b
            aff = jax.nn.softmax(logits, axis=-1)
            topv, topi = jax.lax.top_k(aff, K_ACT)
            gates = jnp.sum(jax.nn.one_hot(topi, E_R, dtype=aff.dtype) * topv[..., None], axis=-2)
            h = jax.nn.gelu(jnp.einsum('bsd,edh->besh', an, re_w1) + re_b1[None, :, None, :], approximate=False)
            routed = jnp.einsum('bse,besh,ehd->bsd', gates, h, re_w2) + jnp.einsum('bse,ed->bsd', gates, re_b2)
            return shared + routed + an + attn_out
        del positions
        return _forward(x, theta, gamma1, gamma2, q_w, q_b, k_w, k_b, v_w, v_b, o_w, o_b, router_w, router_b, sh_w1, sh_b1, sh_w2, sh_b2, re_w1, re_b1, re_w2, re_b2)
    x = x + _L0_attn_ref(_layernorm(x, axis=-1), L0_attn_norm_w, L0_attn_Wq, L0_attn_bq, L0_attn_Wk, L0_attn_bk, L0_attn_Wv, L0_attn_bv, L0_attn_Wo, L0_attn_bo)
    x = x + _L0_xattn_ref(_layernorm(x, axis=-1), ctx_768, L0_xattn_Wq, L0_xattn_bq, L0_xattn_Wkv, L0_xattn_bkv, L0_xattn_Wo, L0_xattn_bo)
    x = x + _L0_ffn_ref(_layernorm(x, axis=-1), L0_ffn_positions, L0_ffn_theta, L0_ffn_gamma1, L0_ffn_gamma2, L0_ffn_q_w, L0_ffn_q_b, L0_ffn_k_w, L0_ffn_k_b, L0_ffn_v_w, L0_ffn_v_b, L0_ffn_o_w, L0_ffn_o_b, L0_ffn_router_w, L0_ffn_router_b, L0_ffn_sh_w1, L0_ffn_sh_b1, L0_ffn_sh_w2, L0_ffn_sh_b2, L0_ffn_re_w1, L0_ffn_re_b1, L0_ffn_re_w2, L0_ffn_re_b2)
    return x

_drawn_inputs = setup_inputs


def setup_inputs(seed=0):
    import zlib

    import numpy as np

    out = dict(_drawn_inputs(seed))
    spreads = {'L0_attn_norm_w': (1.0, 0.2),
     'L0_attn_bq': (0.0, 0.8),
     'L0_attn_bk': (0.0, 0.8),
     'L0_attn_bv': (0.0, 0.1),
     'L0_attn_bo': (0.0, 0.1),
     'L0_xattn_bq': (0.0, 0.716),
     'L0_xattn_bkv': (0.0, 0.1),
     'L0_xattn_bo': (0.0, 0.1),
     'L0_ffn_gamma1': (1.0, 0.2),
     'L0_ffn_gamma2': (1.0, 0.2),
     'L0_ffn_q_b': (0.0, 0.8),
     'L0_ffn_k_b': (0.0, 0.8),
     'L0_ffn_v_b': (0.0, 0.276),
     'L0_ffn_o_b': (0.0, 0.1),
     'L0_ffn_router_b': (0.0, 0.8),
     'L0_ffn_sh_b1': (0.0, 0.8),
     'L0_ffn_sh_b2': (0.0, 0.319),
     'L0_ffn_re_b1': (0.0, 0.8),
     'L0_ffn_re_b2': (0.0, 0.8)}
    factors = {'L0_ffn_theta': 8.0,
     'L0_ffn_q_w': 8.0,
     'L0_ffn_k_w': 8.0,
     'L0_ffn_router_w': 8.0,
     'L0_ffn_sh_w1': 8.0,
     'L0_ffn_sh_w2': 7.856,
     'L0_ffn_re_w1': 8.0,
     'L0_ffn_re_w2': 8.0}
    for name, (base, spread) in spreads.items():
        noise = np.random.default_rng([zlib.crc32(name.encode()), seed]).standard_normal(out[name].shape)
        drawn = base * np.exp(spread * noise) if base else spread * noise
        out[name] = jnp.asarray(drawn.astype(out[name].dtype))
    for name, factor in factors.items():
        out[name] = (out[name] * factor).astype(out[name].dtype)
    return out
```

```python
import concourse.bass as bass
from concourse import mybir
from contextlib import ExitStack

F32 = mybir.dt.float32
BF16 = mybir.dt.bfloat16
ACT = mybir.ActivationFunctionType
ALU = mybir.AluOpType
AX = mybir.AxisListType

P = 128
B, T, D = 8, 256, 128
QT = T // P
H, HD = 16, D // 16
G, GH = 4, 4
SKV, DC = 1601, 96
MASKED = -1.0e30

SLOTS = [(0, 0, 0), (8, 0, 1), (16, 1, 0), (24, 1, 1), (40, 0, 2), (48, 2, 0)]
SHIFT_ROW = 32


def build(nc, a, out):
    ctx = ExitStack()
    with ctx:
        def sb(name, shape, dt=F32):
            return ctx.enter_context(nc.sbuf_tensor(name, shape, dt))

        def sem(name):
            return ctx.enter_context(nc.semaphore(name))

        t = dict(
            x=sb("x_sb", [P, B * QT, D]),
            ident=sb("ident", [P, P]), identb=sb("identb", [P, P], BF16),
            mask_qk0=sb("mask_qk0", [P, 4, P], BF16), mask_qk1=sb("mask_qk1", [P, 2, 2 * P], BF16),
            mask_kq0=sb("mask_kq0", [P, 2, 2 * P], BF16), mask_kq1=sb("mask_kq1", [P, 2, P], BF16),
            neg_half=sb("neg_half", [P, QT]),
            qst=sb("q_stack", [P, H, T], BF16),
            kst=sb("k_stack", [P, H // 2, SKV + 1], BF16),
        )
        s = dict(stats=sb("stats", [P, QT, 6]), mv=sb("mv", [P, QT, 2]), ve=sb("ve", [P, QT]),
                 msq=sb("msq", [P, QT]), rstd=sb("rstd", [P, QT]), xn=sb("xn", [P, QT, D]),
                 xr=sb("xr", [P, QT, D]), spare=sb("spare", [P, 1]))
        psum = ctx.enter_context(nc.psum_tensor("psum", [P, 8, 512], F32))
        setup(nc, a, t, sem)
        self_attention(nc, a, t, psum, s)
        cross_attention(nc, a, t, psum, s)
        t["an_cur"] = sb("an_cur", [P, QT, D])
        an_all = sb("an_all", [P, B * QT, D])
        rotary_attention(nc, a, t, psum, s, an_all)
        d = dict(an=an_all, anT=sb("anT", [P, B * T]), gatesT=sb("gatesT", [32, B * T]), gparts=sb("gparts", [P, B * T], BF16),
                 sel=sb("sel", [P, 32, P], BF16), b1T=sb("b1T", [P, 32]), b2=sb("b2", [32, D]))
        gates_of_experts(nc, a, t, psum, d)
        experts(nc, a, t, psum, d, out)


def setup(nc, a, t, sem):
    with nc.Block() as block:
        x_loaded, cleared, idents = sem("x_loaded"), sem("cleared"), sem("idents")

        @block.sync
        def _(sp):
            sp.dma_start(t["x"][:], a["x"].rearrange("b (q p) d -> p (b q) d", p=P)).then_inc(x_loaded, 16)
            sp.wait_ge(x_loaded, 16)

        @block.vector
        def _(dve):
            for name in ("ident", "identb", "mask_qk0", "mask_qk1", "mask_kq0", "mask_kq1", "qst"):
                nc.vector.memset(t[name][:], 0.0).then_inc(cleared, 1)
            nc.vector.memset(t["neg_half"][:], -0.5)
            nc.vector.memset(t["kst"][:], 0.0).then_inc(cleared, 1)
            dve.wait_ge(cleared, 8)
            for i in range(2):
                r = 64 * i + SHIFT_ROW
                nc.vector.memset(t["kst"][r:r + 2, :, :], 1.0)

        @block.gpsimd
        def _(pool):
            pool.wait_ge(cleared, 6)
            for name in ("ident", "identb"):
                nc.gpsimd.affine_select(out=t[name][:], in_=t[name][:], compare_op=ALU.not_equal, fill=1.0,
                                        base=0, pattern=[[-1, P]], channel_multiplier=1).then_inc(idents, 1)
            for name, part in (("mask_qk0", t["mask_qk0"][:]), ("mask_qk1", t["mask_qk1"][:, :, P:2 * P])):
                nc.gpsimd.affine_select(out=part, in_=part, compare_op=ALU.is_ge, fill=MASKED, base=0,
                                        pattern=[[0, part.shape[1]], [-1, P]], channel_multiplier=1).then_inc(idents, 1)
            for name, part in (("mask_kq0", t["mask_kq0"][:, :, 0:P]), ("mask_kq1", t["mask_kq1"][:])):
                nc.gpsimd.affine_select(out=part, in_=part, compare_op=ALU.is_ge, fill=MASKED, base=0,
                                        pattern=[[0, part.shape[1]], [1, P]], channel_multiplier=-1).then_inc(idents, 1)


class Chain:

    def __init__(self, eng, sem, per, i):
        self.eng, self.sem, self.per, self.i, self.n = eng, sem, per, i, 0

    def __call__(self, ins):
        self.n += 1
        ins.then_inc(self.sem, 1)
        self.eng.wait_ge(self.sem, self.i * self.per + self.n)

    def end(self):
        assert self.n == self.per, (self.n, self.per)


def at(i, per, n):
    assert 1 <= n <= per
    return i * per + n


NORM_LINKS = 4
RMS_LINKS = 6


def layer_norm(nc, dve, link, x, s, var_ready, rstd_ready, ready_at, eps=1e-5):
    for q in range(QT):
        link(nc.vector.bn_stats(s["stats"][:, q, :], x(q)))
    nc.vector.memset(s["spare"][:], 0.0)
    for q in range(QT):
        ins = nc.vector.bn_aggr(s["mv"][:, q, :], s["stats"][:, q, :])
    link(ins)
    nc.vector.tensor_scalar_add(s["ve"][:], s["mv"][:, :, 1], eps).then_inc(var_ready, 1)
    dve.wait_ge(rstd_ready, ready_at)
    for q in range(QT):
        ins = nc.vector.tensor_scalar(s["xn"][:, q, :], x(q), s["mv"][:, q, 0:1], s["rstd"][:, q:q + 1],
                                      ALU.subtract, ALU.mult)
    link(ins)


def rms_norm(nc, dve, link, s, weight, eps, var_ready, rstd_ready, ready_at, done):
    for q in range(QT):
        link(nc.vector.bn_stats(s["stats"][:, q, :], s["xn"][:, q, :]))
    nc.vector.memset(s["spare"][:], 0.0)
    for q in range(QT):
        ins = nc.vector.bn_aggr(s["mv"][:, q, :], s["stats"][:, q, :])
    link(ins)
    link(nc.vector.tensor_tensor(s["msq"][:], s["mv"][:, :, 0], s["mv"][:, :, 0], ALU.mult))
    link(nc.vector.tensor_tensor(s["msq"][:], s["msq"][:], s["mv"][:, :, 1], ALU.add))
    nc.vector.tensor_scalar_add(s["ve"][:], s["msq"][:], eps).then_inc(var_ready, 1)
    dve.wait_ge(rstd_ready, ready_at)
    for q in range(QT):
        ins = nc.vector.scalar_tensor_tensor(out=s["xr"][:, q, :], in0=s["xn"][:, q, :],
                                             scalar=s["rstd"][:, q:q + 1], in1=weight, op0=ALU.mult, op1=ALU.mult)
    link(ins)
    done()


def split3(nc, dve, link, parts, rest, src):
    link(nc.vector.tensor_copy(parts[0], src))
    link(nc.vector.tensor_tensor(rest, src, parts[0], ALU.subtract))
    link(nc.vector.tensor_copy(parts[1], rest))
    return nc.vector.tensor_tensor(parts[2], rest, parts[1], ALU.subtract)


def unit_heads(u):
    per, v = (4, u) if u < 4 else (2, u - 4)
    return [2 * k + v % 2 for k in range(per * (v // 2), per * (v // 2) + per)]


def column(h):
    return (h % 2) * (H // 2) + h // 2


def queries_of(qst, h, cols):
    return qst[:, h, cols]


def keys_of(kst, h, cols):
    return kst[:, h // 2, cols]


def stack_rows(stack, which, i, row, count, tiles):
    rows = slice(64 * i + row, 64 * i + row + count)
    if which == 0:
        return stack[rows, slice(2 * tiles.start + i, 2 * tiles.stop, 2)]
    return stack[rows, tiles]


def load_stack(sp, stack, scratch, which, n, sem):
    v = scratch.rearrange("s (t i d) n -> s i d t n", i=2, d=HD)
    for slot in SLOTS:
        row, part = slot[0], slot[1 + which]
        for i in range(2):
            sp.dma_start(stack_rows(stack, which, i, row, HD, slice(0, H // 2))[:, :, 0:n], v[part, i]).then_inc(sem, 16)


def self_attention(nc, a, t, psum, s):
    ctx = ExitStack()
    with ctx:
        def sb(name, shape, dt=F32):
            return ctx.enter_context(nc.sbuf_tensor(name, shape, dt))

        def sem(name):
            return ctx.enter_context(nc.semaphore(name))

        w_nat = sb("a_w_nat", [P, 4, D])
        w_t = sb("a_w_t", [P, 4, D])
        bqk = sb("a_bqk", [P, 2])
        rows = sb("a_rows", [P, 3, D])
        resid = sb("a_resid", [P, QT, D])
        xT = sb("a_xT", [P, T])
        qk = sb("a_qk", [P, 2 * T])
        rest = sb("a_rest", [P, 2 * T])
        parts = sb("a_parts", [P, 3, 2 * T], BF16)
        v_aug = sb("a_v_aug", [P, QT, H, 32])
        mneg = sb("a_mneg", [P, QT, H])
        mparts = sb("a_mparts", [H, 2, T], BF16)
        prob = sb("a_prob", [P, 2, 4 * T])
        pvs = sb("a_pvs", [P, T])
        rec = sb("a_rec", [P, QT, GH])
        attn = sb("a_attn", [P, QT, D])
        attnT = sb("a_attnT", [P, T])
        scratch = nc.dram_tensor("a_scratch", [3, P, 2 * T], BF16, kind="Internal").ap()
        qst, kst, ident, identb = t["qst"], t["kst"], t["ident"], t["identb"]
        prep = psum[:, 0, :]
        pv = psum[:, 1, 0:T]

        ITEMS = 3 + 1 + G + 2
        UNITS = 4 + 8
        STEPS = 2 * G

        w_loaded, wT_full, wT_free = sem("a_w_loaded"), sem("a_wT_full"), sem("a_wT_free")
        var_ready, rstd_ready = sem("a_var_ready"), sem("a_rstd_ready")
        xr_ready, resid_ready = sem("a_xr_ready"), sem("a_resid_ready")
        dve_own, pool_own = sem("a_dve_own"), sem("a_pool_own")
        prep_full, prep_free = sem("a_prep_full"), sem("a_prep_free")
        parts_ready, bounced, stacked = sem("a_parts_ready"), sem("a_bounced"), sem("a_stacked")
        max_full, max_done = sem("a_max_full"), sem("a_max_done")
        m0_ready, m1_ready, m_stacked = sem("a_m0_ready"), sem("a_m1_ready"), sem("a_m_stacked")
        st_full, exp_done, pv_done, pv_copied = sem("a_st_full"), sem("a_exp_done"), sem("a_pv_done"), sem("a_pv_copied")
        attn_ready, x_done = sem("a_attn_ready"), sem("a_x_done")
        ones_set = sem("a_ones_set")

        block = ctx.enter_context(nc.Block())

        @block.sync
        def _(sp):
            for n, name in enumerate(("Wq", "Wk", "Wv", "Wo")):
                sp.dma_start(w_nat[:, n, :], a["L0_attn_" + name]).then_inc(w_loaded, 16)
            for n, name in enumerate(("bq", "bk")):
                sp.dma_start(bqk[:, n:n + 1], a["L0_attn_" + name].rearrange("(p a) -> p a", a=1)).then_inc(w_loaded, 16)
            for n, name in enumerate(("norm_w", "bv", "bo")):
                sp.dma_start(rows[:, n, :], a["L0_attn_" + name].rearrange("(a d) -> a d", a=1).to_broadcast([P, D]))\
                    .then_inc(w_loaded, 16)
            with sp.Fori(0, B) as i:
                sp.wait_ge(parts_ready, at(i, 1, 1))
                sp.dma_start(scratch.rearrange("s p n -> p s n"), parts[:]).then_inc(bounced, 16)
                sp.wait_ge(bounced, at(i, 16, 16))
                load_stack(sp, qst, scratch[:, :, 0:T], 0, T, stacked)
                load_stack(sp, kst, scratch[:, :, T:2 * T], 1, T, stacked)
                sp.wait_ge(stacked, at(i, 24 * 16, 24 * 16))
                sp.wait_ge(m1_ready, at(i, 1, 1))
                for par in range(2):
                    for m in range(2):
                        sp.dma_start(stack_rows(qst, 0, par, SHIFT_ROW + m, 1, slice(0, H // 2)), mparts[par * 8:par * 8 + 8, m, :]).then_inc(m_stacked, 16)

        @block.gpsimd
        def _(pool):
            pool.wait_ge(w_loaded, 9 * 16)
            with pool.Fori(0, B) as i:
                for n in range(2):
                    pool.wait_ge(var_ready, at(i, 2, n + 1))
                    nc.gpsimd.tensor_tensor(s["rstd"][:], s["ve"][:], t["neg_half"][:], ALU.pow).then_inc(rstd_ready, 1)
                link = Chain(pool, pool_own, QT, i)
                pool.wait_ge(xr_ready, at(i, 1, 1))
                for q in range(QT):
                    link(nc.gpsimd.tensor_tensor(resid[:, q, :], s["xr"][:, q, :], rows[:, 2, :], ALU.add))
                nc.gpsimd.tensor_tensor(resid[:], resid[:], t["x"][:, bass.ds(i * QT, QT), :], ALU.add)\
                    .then_inc(resid_ready, 1)
                link.end()

        @block.vector
        def _(dve):
            nc.vector.memset(v_aug[:], 1.0).then_inc(ones_set, 1)
            dve.wait_ge(w_loaded, 9 * 16)
            with dve.Fori(0, B) as i:
                item = 0
                link = Chain(dve, dve_own, NORM_LINKS + RMS_LINKS + 3 + G + 2, i)
                layer_norm(nc, dve, link, lambda q: t["x"][:, bass.ds(i * QT + q, 1), :].rearrange("p a d -> p (a d)"),
                           s, var_ready, rstd_ready, at(i, 2, 1))
                rms_norm(nc, dve, link, s, rows[:, 0, :], 1e-6, var_ready, rstd_ready, at(i, 2, 2),
                         lambda: dve.sem_inc(xr_ready, 1))
                dve.wait_ge(prep_free, at(i, ITEMS, 2))
                split3(nc, dve, link, [parts[:, n, :] for n in range(3)], rest[:], qk[:]).then_inc(parts_ready, 1)
                for u in range(UNITS):
                    dve.wait_ge(max_full, at(i, UNITS, u + 1))
                    bank = psum[:, 4 + u % 4, :]
                    heads = unit_heads(u)
                    c = column(heads[0])
                    dst = mneg[:, 0 if u < 4 else 1, c:c + len(heads)]
                    src = bank.rearrange("p (h k) -> p h k", h=len(heads))
                    nc.vector.tensor_reduce(out=dst, in_=src, axis=AX.X, op=ALU.max, negate=True).then_inc(max_done, 1)
                dve.wait_ge(m0_ready, at(i, 1, 1))
                nc.vector.tensor_tensor(mparts[:, 1, :], prep[0:H, 0:T], mparts[:, 0, :], ALU.subtract)\
                    .then_inc(m1_ready, 1)
                dve.wait_ge(m1_ready, at(i, 1, 1))
                dve.sem_inc(prep_free, 1)
                for g in range(G):
                    dve.wait_ge(prep_full, at(i, ITEMS, 5 + g))
                    o = prep[:, 0:2 * P].rearrange("p (q h c) -> p q h c", q=QT, h=GH)
                    link(nc.vector.reciprocal(rec[:], o[:, :, :, HD]))
                    nc.vector.tensor_tensor(
                        attn[:, :, 32 * g:32 * g + 32].rearrange("p q (h d) -> p q h d", h=GH), o[:, :, :, 0:HD],
                        rec[:].rearrange("p q (h a) -> p q h a", a=1).to_broadcast([P, QT, GH, HD]), ALU.mult)\
                        .then_inc(prep_free, 1)
                dve.wait_ge(prep_free, at(i, ITEMS, 4 + G))
                link(nc.vector.tensor_tensor(attn[:, 0, :], attn[:, 0, :], rows[:, 1, :], ALU.add))
                link(nc.vector.tensor_tensor(attn[:, 1, :], attn[:, 1, :], rows[:, 1, :], ALU.add))
                dve.sem_inc(attn_ready, 1)
                dve.wait_ge(resid_ready, at(i, 1, 1))
                dve.wait_ge(prep_full, at(i, ITEMS, ITEMS))
                nc.vector.tensor_tensor(t["x"][:, bass.ds(i * QT, QT), :],
                                        prep[:, 0:2 * P].rearrange("p (q d) -> p q d", q=QT), resid[:], ALU.add)\
                    .then_inc(x_done, 1)
                dve.wait_ge(x_done, at(i, 1, 1))
                dve.sem_inc(prep_free, 1)
                link.end()

        @block.scalar
        def _(act):
            act.wait_ge(wT_full, 1)
            nc.scalar.activation(w_t[:].rearrange("p n d -> p (n d)"), prep, ACT.Copy).then_inc(wT_free, 1)
            act.wait_ge(ones_set, 1)
            with act.Fori(0, B) as i:
                act.wait_ge(prep_full, at(i, ITEMS, 1))
                nc.scalar.activation(xT[:], prep[:, 0:T], ACT.Copy).then_inc(prep_free, 1)
                act.wait_ge(prep_full, at(i, ITEMS, 2))
                nc.scalar.activation(qk[:, 0:T], prep[:, 0:T], ACT.Identity, bias=bqk[:, 0:1])
                nc.scalar.activation(qk[:, T:2 * T], prep[:, T:2 * T], ACT.Identity, bias=bqk[:, 1:2]).then_inc(prep_free, 1)
                act.wait_ge(prep_full, at(i, ITEMS, 3))
                nc.scalar.activation(v_aug[:, :, :, 0:HD],
                                     prep[:, 0:2 * D].rearrange("p (q h d) -> p q h d", q=QT, h=H), ACT.Copy)\
                    .then_inc(prep_free, 1)
                act.wait_ge(prep_full, at(i, ITEMS, 4))
                nc.scalar.activation(mparts[:, 0, :], prep[0:H, 0:T], ACT.Copy).then_inc(m0_ready, 1)
                for n in range(STEPS):
                    act.wait_ge(st_full, at(i, STEPS, n + 1))
                    w = 2 * T if n % 2 == 0 else T
                    nc.scalar.activation(prob[:, n % 2, 0:2 * w].rearrange("p (a c) -> p a c", a=2),
                                         psum[:, 4 + 2 * (n % 2):6 + 2 * (n % 2), 0:w], ACT.Exp, scale=HD ** -0.5)\
                        .then_inc(exp_done, 1)
                    if n >= 2 and n % 2 == 0:
                        act.wait_ge(pv_done, at(i, STEPS, n))
                        nc.scalar.activation(pvs[:], pv, ACT.Copy).then_inc(pv_copied, 1)
                act.wait_ge(pv_done, at(i, STEPS, STEPS))
                act.wait_ge(prep_full, at(i, ITEMS, 4 + G - 1))
                nc.scalar.activation(pvs[:], pv, ACT.Copy).then_inc(pv_copied, 1)
                act.wait_ge(prep_full, at(i, ITEMS, ITEMS - 1))
                nc.scalar.activation(attnT[:], prep[:, 0:T], ACT.Copy).then_inc(prep_free, 1)

        @block.tensor
        def _(pe):
            pe.wait_ge(w_loaded, 9 * 16)
            for n in range(4):
                last = nc.tensor.transpose(prep[:, n * D:(n + 1) * D], w_nat[:, n, :], ident[:])
            last.then_inc(wT_full, 1)
            pe.wait_ge(wT_free, 1)
            with pe.Fori(0, B) as i:
                pe.wait_ge(xr_ready, at(i, 1, 1))
                for q in range(QT):
                    last = nc.tensor.transpose(prep[:, q * P:(q + 1) * P], s["xr"][:, q, :], ident[:])
                last.then_inc(prep_full, 1)
                pe.wait_ge(prep_free, at(i, ITEMS, 1))
                for n in range(2):
                    last = nc.tensor.matmul(prep[:, n * T:(n + 1) * T], w_t[:, n, :], xT[:], start=True, stop=True)
                last.then_inc(prep_full, 1)
                pe.wait_ge(prep_free, at(i, ITEMS, 2))
                for q in range(QT):
                    last = nc.tensor.matmul(prep[:, q * D:(q + 1) * D], xT[:, q * P:(q + 1) * P], w_t[:, 2, :],
                                            start=True, stop=True)
                last.then_inc(prep_full, 1)
                pe.wait_ge(prep_free, at(i, ITEMS, 3))

                pe.wait_ge(stacked, at(i, 24 * 16, 24 * 16))
                for u in range(UNITS):
                    if u >= 4:
                        pe.wait_ge(max_done, at(i, UNITS, u - 3))
                    bank = psum[:, 4 + u % 4, :]
                    q, keys, heads, mask = (0, P, unit_heads(u), "mask_qk0") if u < 4 else (1, 2 * P, unit_heads(u), "mask_qk1")
                    nc.tensor.matmul(bank, identb[:], t[mask][:].rearrange("p h k -> p (h k)"), start=True, stop=False)
                    for n, h in enumerate(heads):
                        last = nc.tensor.matmul(bank[:, n * keys:(n + 1) * keys], queries_of(qst, h, slice(q * P, q * P + P)),
                                                keys_of(kst, h, slice(0, keys)), start=False, stop=(n == len(heads) - 1))
                    last.then_inc(max_full, 1)
                pe.wait_ge(max_done, at(i, UNITS, UNITS))
                for q in range(QT):
                    last = nc.tensor.transpose(prep[0:H, q * P:(q + 1) * P], mneg[:, q, :], ident[:])
                last.then_inc(prep_full, 1)

                pe.wait_ge(m_stacked, at(i, 4 * 16, 4 * 16))

                def scores_t(n):
                    g, kt = n // 2, n % 2
                    if n >= 2:
                        pe.wait_ge(exp_done, at(i, STEPS, n - 1))
                    w = T - kt * P
                    for par in range(2):
                        nc.tensor.matmul(psum[:, 4 + 2 * (n % 2) + par, 0:2 * w], identb[:],
                                         t["mask_kq%d" % kt][:].rearrange("p h q -> p (h q)"), start=True, stop=False)
                    for hh in range(GH):
                        h = g * GH + hh
                        dst = psum[:, 4 + 2 * (n % 2) + hh % 2, (hh // 2) * w:(hh // 2) * w + w]
                        last = nc.tensor.matmul(dst, keys_of(kst, h, slice(kt * P, kt * P + P)),
                                                queries_of(qst, h, slice(kt * P, T)), start=False, stop=(hh >= 2))
                    last.then_inc(st_full, 1)

                def values(n):
                    g, kt = n // 2, n % 2
                    pe.wait_ge(exp_done, at(i, STEPS, n + 1))
                    if n % 2 == 0 and n >= 2:
                        pe.wait_ge(pv_copied, at(i, G, g))
                    w = T - kt * P
                    for hh in range(GH):
                        c = (hh % 2) * 2 * w + (hh // 2) * w
                        last = nc.tensor.matmul(pv[32 * hh:32 * hh + 32, kt * P:T], v_aug[:, kt, g * GH + hh, :],
                                                prob[:, n % 2, c:c + w], start=(kt == 0), stop=(kt == 1),
                                                tile_position=(0, 32 * hh))
                    last.then_inc(pv_done, 1)

                def group_out(g):
                    pe.wait_ge(pv_copied, at(i, G, g + 1))
                    pe.wait_ge(prep_free, at(i, ITEMS, 4 + g))
                    for q in range(QT):
                        last = nc.tensor.transpose(prep[:, q * P:(q + 1) * P], pvs[:, q * P:(q + 1) * P], ident[:])
                    last.then_inc(prep_full, 1)

                for n in range(STEPS):
                    scores_t(n)
                    if n >= 1:
                        values(n - 1)
                    if n >= 3 and n % 2 == 1:
                        group_out((n - 3) // 2)
                values(STEPS - 1)
                group_out(G - 1)
                pe.wait_ge(attn_ready, at(i, 1, 1))
                for q in range(QT):
                    last = nc.tensor.transpose(prep[:, q * P:(q + 1) * P], attn[:, q, :], ident[:])
                last.then_inc(prep_full, 1)
                pe.wait_ge(prep_free, at(i, ITEMS, ITEMS - 1))
                for q in range(QT):
                    last = nc.tensor.matmul(prep[:, q * D:(q + 1) * D], attnT[:, q * P:(q + 1) * P], w_t[:, 3, :],
                                            start=True, stop=True)
                last.then_inc(prep_full, 1)
                pe.wait_ge(prep_free, at(i, ITEMS, ITEMS))


class Tally:

    def __init__(self, per):
        self.n, self.per, self.i = dict.fromkeys(per, 0), per, None

    def up(self, name, by=1):
        self.n[name] += by
        return self.now(name)

    def now(self, name, back=0):
        n = self.n[name] - back
        return n if self.i is None else self.i * self.per[name] + n

    def enter(self, i):
        self.i, self.start = i, dict(self.n)

    def leave(self, rounds):
        for name, n in self.n.items():
            assert n - self.start[name] in (0, self.per[name]), (name, n - self.start[name], self.per[name])
            if n != self.start[name]:
                self.n[name] = self.start[name] + rounds * self.per[name]
        self.i = None


def wait(eng, sem, value):
    if not isinstance(value, int) or value > 0:
        eng.wait_ge(sem, value)


KT = -(-SKV // P)
CHUNKS = [(c * SKV // 4, (c + 1) * SKV // 4) for c in range(4)]
CW = max(e - s for s, e in CHUNKS)
UNITS_B = QT * GH * 4
M_STEP = 9


def tile_rows(kt):
    return min(P, SKV - kt * P)


def units_of_step(n):
    head = 22
    if n < M_STEP:
        lo, k = UNITS_B - head, M_STEP
        return [lo + u for u in range(n * head // k, (n + 1) * head // k)]
    k, n, total = KT - M_STEP, n - M_STEP, UNITS_B - head
    return list(range(n * total // k, (n + 1) * total // k))


PREP_AT = {(0, 0): ("ctx", 0), (0, 1): ("k", 0), (0, 2): ("pv", 0), (0, 3): ("ctx", 1), (0, 4): ("k", 1),
           (0, 5): ("ctx", 2), (0, 6): ("k", 2), (0, 7): ("ctx", 3), (0, 8): ("k", 3), (0, 9): ("m", 2),
           (0, 10): ("x", 0), (0, 11): ("q", 0), (0, 12): ("v", 0), (1, 0): ("v", 1), (1, 1): ("v", 2),
           (1, 2): ("pv", 1), (1, 3): ("v", 3), (1, 9): ("m", 3), (2, 2): ("pv", 2), (2, 9): ("m", 0),
           (3, 2): ("pv", 3), (3, 4): ("attnT", 0), (3, 6): ("out", 0), (3, 9): ("m", 1)}
NEXT_BATCH = ("ctx", "k", "x", "q", "v")


def prep_item(r, n, first=False, last=False):
    item = PREP_AT.get((r, n))
    if item is None or (last and (item[0] in NEXT_BATCH or item == ("m", 0))):
        return None
    if first and item[0] in ("pv", "attnT", "out"):
        return None
    return item


def column4(hh):
    return hh % 2 * 2 + hh // 2


PROLOGUE_ITEMS = [("ctx", 0), ("k", 0), ("ctx", 1), ("k", 1), ("ctx", 2), ("k", 2), ("ctx", 3), ("k", 3),
                  ("x", 0), ("q", 0), ("v", 0), ("v", 1), ("v", 2), ("v", 3), ("m", 0)]


def units_left(r, n, last):
    return not (last and (r == 2 or (r == 1 and n >= M_STEP)))


def cross_attention(nc, a, t, psum, s):
    ctx = ExitStack()
    with ctx:
        def sb(name, shape, dt=F32):
            return ctx.enter_context(nc.sbuf_tensor(name, shape, dt))

        def sem(name):
            return ctx.enter_context(nc.semaphore(name))

        wq, wo = sb("b_wq", [D, D]), sb("b_wo", [D, D])
        wkv = sb("b_wkv", [DC, 2 * D])
        bq, bk = sb("b_bq", [P, 1]), sb("b_bk", [P, 1])
        rows = sb("b_rows", [P, 2, D])
        resid = sb("b_resid", [P, QT, D])
        xT = sb("b_xT", [P, T])
        qf, qrest = sb("b_qf", [P, T]), sb("b_qrest", [P, T])
        qparts = sb("b_qparts", [P, 3, T], BF16)
        ctx_sb = sb("b_ctx", [P, KT, DC])
        ctxT = sb("b_ctxT", [DC, SKV])
        kf, krest = sb("b_kf", [P, 2, CW]), sb("b_krest", [P, 2, CW])
        zeros = sb("b_zeros", [P, CW])
        kparts = sb("b_kparts", [P, 3, SKV], BF16)
        v_new = sb("b_v_new", [P, KT, D])
        v_aug = sb("b_v_aug", [P, KT, H, 32])
        chunk_max = sb("b_chunk_max", [P, 2, QT, GH, 4])
        mneg = sb("b_mneg", [P, QT, GH])
        mparts = sb("b_mparts", [GH, 2, T], BF16)
        prob = sb("b_prob", [P, 2, GH * T])
        pvs = sb("b_pvs", [P, T])
        rec = sb("b_rec", [P, QT, GH])
        attn = sb("b_attn", [P, QT, D])
        attnT = sb("b_attnT", [P, T])
        q_scr = nc.dram_tensor("b_q_scratch", [3, P, T], BF16, kind="Internal").ap()
        k_scr = nc.dram_tensor("b_k_scratch", [3, P, SKV], BF16, kind="Internal").ap()
        qst, kst, ident = t["qst"], t["kst"], t["ident"]
        prep, pv = psum[:, 0, :], psum[:, 1, 0:T]

        w_loaded, ones_set = sem("b_w_loaded"), sem("b_ones_set")
        var_ready, rstd_ready, xn_ready = sem("b_var_ready"), sem("b_rstd_ready"), sem("b_xn_ready")
        dve_own, pool_own = sem("b_dve_own"), sem("b_pool_own")
        prep_full, prep_free = sem("b_prep_full"), sem("b_prep_free")
        ctx_loaded, ctx_used = sem("b_ctx_loaded"), sem("b_ctx_used")
        kf_ready, k_split = sem("b_kf_ready"), sem("b_k_split")
        qf_ready, q_split = sem("b_qf_ready"), sem("b_q_split")
        q_bounced, k_bounced, stacked = sem("b_q_bounced"), sem("b_k_bounced"), sem("b_stacked")
        v_evacuated, v_placed = sem("b_v_evacuated"), sem("b_v_placed")
        max_full, max_done, mneg_ready = sem("b_max_full"), sem("b_max_done"), sem("b_mneg_ready")
        m0_ready, m1_ready, m_stacked = sem("b_m0_ready"), sem("b_m1_ready"), sem("b_m_stacked")
        st_full, exp_done, pv_done, pv_copied = sem("b_st_full"), sem("b_exp_done"), sem("b_pv_done"), sem("b_pv_copied")
        attn_ready, resid_ready, x_done = sem("b_attn_ready"), sem("b_resid_ready"), sem("b_x_done")

        passed = sem("b_passed")
        PER = dict(item=len(PREP_AT), step=4 * KT, unit=4 * UNITS_B, group=4, batch=1, kchunk=4, half=2,
                   stacked=48 * 16, m_stacked=4 * 64, dma=16, ctx=32, own_dve=NORM_LINKS + G + 2,
                   own_pool=4 * 2 + 2, mneg=4, vchunk=4, placed=2, out=1)
        N_W = 7
        block = ctx.enter_context(nc.Block())

        def parts_of_program(eng, tally, prologue, part):
            prologue()
            part(None, 3, first=True, last=False)
            with eng.Fori(0, B - 1) as i:
                tally.enter(i)
                for r in range(4):
                    part(i, r, first=False, last=False)
                tally.leave(B - 1)
            for r in range(3):
                part(None, r, first=False, last=True)

        @block.sync
        def _(sp):
            T_ = Tally(PER)
            for dst, src in ((wq[:], a["L0_xattn_Wq"]), (wo[:], a["L0_xattn_Wo"]), (wkv[:], a["L0_xattn_Wkv"]),
                             (bq[:], a["L0_xattn_bq"].rearrange("(p a) -> p a", a=1)),
                             (bk[:], a["L0_xattn_bkv"][0:D].rearrange("(p a) -> p a", a=1)),
                             (rows[:, 0, :], a["L0_xattn_bkv"][D:2 * D].rearrange("(a d) -> a d", a=1).to_broadcast([P, D])),
                             (rows[:, 1, :], a["L0_xattn_bo"].rearrange("(a d) -> a d", a=1).to_broadcast([P, D]))):
                sp.dma_start(dst, src).then_inc(w_loaded, 16)

            def load_ctx(b):
                wait(sp, ctx_used, T_.now("batch"))
                sp.sem_inc(passed, 1)
                src = a["ctx_768"][b] if isinstance(b, int) else a["ctx_768"][bass.ds(b, 1)].rearrange("a s d -> (a s) d")
                sp.dma_start(ctx_sb[:, 0:KT - 1, :], src[0:(KT - 1) * P].rearrange("(k p) d -> p k d", p=P)).then_inc(ctx_loaded, 16)
                sp.dma_start(ctx_sb[0:tile_rows(KT - 1), KT - 1, :], src[(KT - 1) * P:SKV]).then_inc(ctx_loaded, 16)

            def bounce():
                wait(sp, stacked, T_.now("stacked"))
                sp.sem_inc(passed, 1)
                sp.wait_ge(k_split, T_.up("kchunk", 4))
                sp.dma_start(k_scr.rearrange("s p n -> p s n"), kparts[:]).then_inc(k_bounced, 16)
                sp.wait_ge(q_split, T_.up("batch"))
                sp.dma_start(q_scr.rearrange("s p n -> p s n"), qparts[:]).then_inc(q_bounced, 16)
                sp.wait_ge(q_bounced, T_.up("dma", 16))
                sp.wait_ge(k_bounced, T_.now("dma"))

            def load_half(half):
                T_.up("stacked", 24 * 16)
                for stack, scr, which, n in ((qst, q_scr, 0, T), (kst, k_scr, 1, SKV)):
                    v = scr.rearrange("s (t i d) n -> s i d t n", i=2, d=HD)
                    for slot in SLOTS:
                        row, part = slot[0], slot[1 + which]
                        for i in range(2):
                            sp.dma_start(stack_rows(stack, which, i, row, HD, slice(4 * half, 4 * half + 4))[:, :, 0:n],
                                         v[part, i, :, 4 * half:4 * half + 4]).then_inc(stacked, 16)

            def store_m(g):
                sp.wait_ge(m1_ready, T_.up("group"))
                for par in range(2):
                    for m in range(2):
                        sp.dma_start(stack_rows(qst, 0, par, SHIFT_ROW + m, 1, slice(2 * g, 2 * g + 2)), mparts[2 * par:2 * par + 2, m, :])\
                            .then_inc(m_stacked, 16)

            def prologue():
                load_ctx(0)
                bounce()
                load_half(0)
                load_half(1)
                store_m(0)

            def part(i, r, first, last):
                if r == 0 and not last:
                    load_ctx(i + 1)
                if r == 3:
                    if not first:
                        sp.wait_ge(st_full, T_.now("step"))
                        load_half(1)
                if prep_item(r, M_STEP, first, last):
                    store_m(PREP_AT[(r, M_STEP)][1])
                T_.up("step", KT)
                if r == 0 and not last:
                    bounce()
                    sp.wait_ge(st_full, T_.now("step"))
                    load_half(0)

            parts_of_program(sp, T_, prologue, part)

        @block.gpsimd
        def _(pool):
            T_ = Tally(PER)

            def own(ins):
                ins.then_inc(pool_own, 1)
                pool.wait_ge(pool_own, T_.up("own_pool"))

            def power():
                pool.wait_ge(var_ready, T_.up("batch"))
                nc.gpsimd.tensor_tensor(s["rstd"][:], s["ve"][:], t["neg_half"][:], ALU.pow).then_inc(rstd_ready, 1)

            def split_k():
                wait(pool, k_bounced, T_.now("dma"))
                for c, (lo, hi) in enumerate(CHUNKS):
                    n = T_.up("kchunk")
                    pool.wait_ge(kf_ready, n)
                    own(nc.gpsimd.tensor_tensor(krest[:, c % 2, 0:hi - lo], kf[:, c % 2, 0:hi - lo], kparts[:, 0, lo:hi], ALU.subtract))
                    own(nc.gpsimd.tensor_tensor(kparts[:, 1, lo:hi], krest[:, c % 2, 0:hi - lo], zeros[:, 0:hi - lo], ALU.add))
                    nc.gpsimd.tensor_tensor(kparts[:, 2, lo:hi], krest[:, c % 2, 0:hi - lo], kparts[:, 1, lo:hi], ALU.subtract)\
                        .then_inc(k_split, 1)

            def split_q():
                wait(pool, q_bounced, T_.now("dma"))
                T_.up("dma", 16)
                pool.wait_ge(qf_ready, T_.now("batch"))
                own(nc.gpsimd.tensor_tensor(qrest[:], qf[:], qparts[:, 0, :], ALU.subtract))
                own(nc.gpsimd.tensor_tensor(qparts[:, 1, :], qrest[:], zeros[:, 0:T], ALU.add))
                nc.gpsimd.tensor_tensor(qparts[:, 2, :], qrest[:], qparts[:, 1, :], ALU.subtract).then_inc(q_split, 1)

            def place_v(half):
                pool.wait_ge(v_evacuated, T_.now("kchunk"))
                wait(pool, pv_done, T_.now("step"))
                pool.sem_inc(passed, 1)
                c = half * H // 2
                for lo, hi, n in ((0, KT - 1, P), (KT - 1, KT, tile_rows(KT - 1))):
                    ins = nc.gpsimd.tensor_copy(v_aug[0:n, lo:hi, c:c + H // 2, 0:HD],
                                                v_new[0:n, lo:hi, c * HD:(c + H // 2) * HD].rearrange("p k (h d) -> p k h d", h=H // 2))
                ins.then_inc(v_placed, 1)

            def residual(b):
                wait(pool, x_done, T_.now("out"))
                T_.up("out")
                for q in range(QT):
                    ins = nc.gpsimd.tensor_tensor(
                        resid[:, q, :], t["x"][:, bass.ds(b * QT + q, 1), :].rearrange("p a d -> p (a d)"), rows[:, 1, :], ALU.add)
                ins.then_inc(resid_ready, 1)

            def prologue():
                pool.wait_ge(w_loaded, N_W * 16)
                pool.wait_ge(ones_set, 1)
                power()
                split_k()
                split_q()
                place_v(0)
                place_v(1)

            def part(i, r, first, last):
                if r == 0 and not last:
                    power()
                    split_k()
                    split_q()
                T_.up("step", KT)
                if r == 1 and not last:
                    T_.up("step", -KT)
                    place_v(0)
                    T_.up("step", KT)
                if r == 2:
                    residual(B - 1 if last else i)
                    if not last:
                        place_v(1)

            parts_of_program(pool, T_, prologue, part)

        @block.vector
        def _(dve):
            T_ = Tally(PER)

            def own(ins):
                ins.then_inc(dve_own, 1)
                dve.wait_ge(dve_own, T_.up("own_dve"))

            def norm(b):
                T_.up("batch")
                layer_norm(nc, dve, own, lambda q: t["x"][:, bass.ds(b * QT + q, 1), :].rearrange("p a d -> p (a d)"),
                           s, var_ready, rstd_ready, T_.now("batch"))
                dve.sem_inc(xn_ready, 1)

            def unit(u):
                v = T_.up("unit")
                q, c, hh = u // (4 * GH), u // GH % 4, u % GH
                half = (T_.n["unit"] - 1) // UNITS_B % 2
                w = CHUNKS[c][1] - CHUNKS[c][0]
                dve.wait_ge(max_full, v)
                nc.vector.tensor_reduce(out=chunk_max[:, half, q, column4(hh), c:c + 1], in_=psum[:, 2 + u % 2, 0:w],
                                        axis=AX.X, op=ALU.max).then_inc(max_done, 1)
                if u == UNITS_B - 1:
                    dve.wait_ge(max_done, T_.now("unit"))
                    nc.vector.tensor_reduce(out=mneg[:], in_=chunk_max[:, half], axis=AX.X, op=ALU.max, negate=True)\
                        .then_inc(mneg_ready, 1)

            def item(kind, g, b):
                n = T_.up("item")
                if kind == "m":
                    dve.wait_ge(m0_ready, T_.up("group"))
                    nc.vector.tensor_tensor(mparts[:, 1, :], prep[0:GH, 0:T], mparts[:, 0, :], ALU.subtract)\
                        .then_inc(m1_ready, 1)
                    dve.wait_ge(m1_ready, T_.now("group"))
                    dve.sem_inc(prep_free, 1)
                elif kind == "pv":
                    dve.wait_ge(prep_full, n)
                    o = prep[:, 0:2 * P].rearrange("p (q h c) -> p q h c", q=QT, h=GH)
                    own(nc.vector.reciprocal(rec[:], o[:, :, :, HD]))
                    nc.vector.tensor_tensor(
                        attn[:, :, 32 * g:32 * g + 32].rearrange("p q (h d) -> p q h d", h=GH), o[:, :, :, 0:HD],
                        rec[:].rearrange("p q (h a) -> p q h a", a=1).to_broadcast([P, QT, GH, HD]), ALU.mult)\
                        .then_inc(prep_free, 1)
                    if g == G - 1:
                        dve.wait_ge(prep_free, n)
                        own(nc.vector.tensor_tensor(attn[:, 0, :], attn[:, 0, :], rows[:, 0, :], ALU.add))
                        own(nc.vector.tensor_tensor(attn[:, 1, :], attn[:, 1, :], rows[:, 0, :], ALU.add))
                        dve.sem_inc(attn_ready, 1)
                elif kind == "out":
                    dve.wait_ge(resid_ready, T_.up("out"))
                    dve.wait_ge(prep_full, n)
                    nc.vector.tensor_tensor(t["x"][:, bass.ds(b * QT, QT), :],
                                            prep[:, 0:2 * P].rearrange("p (q d) -> p q d", q=QT), resid[:], ALU.add)\
                        .then_inc(x_done, 1)
                    dve.wait_ge(x_done, T_.now("out"))
                    dve.sem_inc(prep_free, 1)

            def prologue():
                nc.vector.memset(zeros[:], 0.0)
                nc.vector.memset(v_aug[:], 1.0).then_inc(ones_set, 1)
                norm(0)
                T_.up("item", 14)
                for u in range(UNITS_B):
                    unit(u)
                item("m", 0, 0)
                for u in range(UNITS_B - 22):
                    unit(u)

            def part(i, r, first, last):
                b = B - 1 if last else i
                for n in range(KT):
                    if r == 0 and n == 0 and not last:
                        norm(i + 1)
                    if units_left(r, n, last):
                        for u in units_of_step(n):
                            unit(u)
                    it = prep_item(r, n, first, last)
                    if it:
                        item(*it, b)

            parts_of_program(dve, T_, prologue, part)
            for it in (("pv", 3), ("attnT", 0), ("out", 0)):
                item(*it, B - 1)

        @block.scalar
        def _(act):
            T_ = Tally(PER)

            def item(kind, g):
                n = T_.up("item")
                if kind in ("pv", "out"):
                    return
                act.wait_ge(prep_full, n)
                if kind == "ctx":
                    cols = min(4 * P, SKV - 4 * P * g)
                    nc.scalar.activation(ctxT[:, 4 * P * g:4 * P * g + cols], prep[0:DC, 0:cols], ACT.Copy).then_inc(prep_free, 1)
                elif kind == "k":
                    lo, hi = CHUNKS[g]
                    v = T_.up("kchunk")
                    wait(act, k_split, T_.now("kchunk", 2))
                    wait(act, k_bounced, T_.now("dma"))
                    nc.scalar.activation(kf[:, g % 2, 0:hi - lo], prep[:, 0:hi - lo], ACT.Identity, bias=bk[:])
                    nc.scalar.activation(kparts[:, 0, lo:hi], prep[:, 0:hi - lo], ACT.Identity, bias=bk[:]).then_inc(kf_ready, 1)
                    act.wait_ge(kf_ready, v)
                    act.sem_inc(prep_free, 1)
                elif kind == "x":
                    nc.scalar.activation(xT[:], prep[:, 0:T], ACT.Copy).then_inc(prep_free, 1)
                elif kind == "q":
                    v = T_.up("batch")
                    wait(act, q_bounced, T_.now("dma"))
                    T_.up("dma", 16)
                    nc.scalar.activation(qf[:], prep[:, 0:T], ACT.Identity, bias=bq[:])
                    nc.scalar.activation(qparts[:, 0, :], prep[:, 0:T], ACT.Identity, bias=bq[:]).then_inc(qf_ready, 1)
                    act.wait_ge(qf_ready, v)
                    act.sem_inc(prep_free, 1)
                elif kind == "v":
                    wait(act, v_placed, T_.now("half"))
                    if g == 3:
                        T_.up("half", 2)
                        nc.scalar.activation(v_new[0:tile_rows(KT - 1), KT - 1, :], prep[0:tile_rows(KT - 1), 0:D], ACT.Copy)\
                            .then_inc(v_evacuated, 1)
                    else:
                        nc.scalar.activation(v_new[:, 4 * g:4 * g + 4, :], prep[:, 0:4 * D].rearrange("p (k d) -> p k d", k=4),
                                             ACT.Copy).then_inc(v_evacuated, 1)
                    act.wait_ge(v_evacuated, T_.up("vchunk"))
                    act.sem_inc(prep_free, 1)
                elif kind == "m":
                    nc.scalar.activation(mparts[:, 0, :], prep[0:GH, 0:T], ACT.Copy).then_inc(m0_ready, 1)
                elif kind == "attnT":
                    nc.scalar.activation(attnT[:], prep[:, 0:T], ACT.Copy).then_inc(prep_free, 1)

            def copy_pv():
                act.wait_ge(pv_done, T_.now("step"))
                nc.scalar.activation(pvs[:], pv, ACT.Copy).then_inc(pv_copied, 1)

            def prologue():
                act.wait_ge(w_loaded, N_W * 16)
                for it in PROLOGUE_ITEMS:
                    item(*it)

            def part(i, r, first, last):
                for n in range(KT):
                    v = T_.up("step")
                    act.wait_ge(st_full, v)
                    wait(act, pv_done, T_.now("step", 2))
                    k, buf = tile_rows(n), (T_.n["step"] - 1) % 2
                    nc.scalar.activation(prob[0:k, buf, :].rearrange("p (a c) -> p a c", a=2),
                                         psum[0:k, 4 + 2 * buf:6 + 2 * buf, :], ACT.Exp, scale=HD ** -0.5)\
                        .then_inc(exp_done, 1)
                    if n == 0 and not first:
                        T_.up("step", -1)
                        copy_pv()
                        T_.up("step")
                    it = prep_item(r, n, first, last)
                    if it:
                        item(*it)

            parts_of_program(act, T_, prologue, part)
            copy_pv()
            for it in (("pv", 3), ("attnT", 0), ("out", 0)):
                item(*it)

        @block.tensor
        def _(pe):
            T_ = Tally(PER)
            pending = []

            def item(kind, g):
                n = T_.up("item")
                wait(pe, prep_free, T_.now("item", 1))
                if kind == "ctx":
                    if g == 0:
                        pe.wait_ge(ctx_loaded, T_.up("ctx", 32))
                    for j, kt in enumerate(range(4 * g, min(4 * g + 4, KT))):
                        k = tile_rows(kt)
                        last = nc.tensor.transpose(prep[0:DC, j * P:j * P + k], ctx_sb[0:k, kt, :], ident[0:k, 0:k])
                    last.then_inc(prep_full, 1)
                    if g == 3:
                        pe.wait_ge(prep_full, n)
                        pe.sem_inc(ctx_used, 1)
                elif kind == "k":
                    lo, hi = CHUNKS[g]
                    nc.tensor.matmul(prep[:, 0:hi - lo], wkv[:, 0:D], ctxT[:, lo:hi], start=True, stop=True).then_inc(prep_full, 1)
                elif kind == "x":
                    pe.wait_ge(xn_ready, T_.up("batch"))
                    for q in range(QT):
                        last = nc.tensor.transpose(prep[:, q * P:(q + 1) * P], s["xn"][:, q, :], ident[:])
                    last.then_inc(prep_full, 1)
                elif kind == "q":
                    nc.tensor.matmul(prep[:, 0:T], wq[:], xT[:], start=True, stop=True).then_inc(prep_full, 1)
                elif kind == "v":
                    for j, kt in enumerate(range(4 * g, min(4 * g + 4, KT))):
                        k = tile_rows(kt)
                        last = nc.tensor.matmul(prep[0:k, j * D:(j + 1) * D], ctxT[:, kt * P:kt * P + k], wkv[:, D:2 * D],
                                                start=True, stop=True)
                    last.then_inc(prep_full, 1)
                elif kind == "m":
                    pe.wait_ge(mneg_ready, T_.up("mneg"))
                    for q in range(QT):
                        last = nc.tensor.transpose(prep[0:GH, q * P:(q + 1) * P], mneg[:, q, :], ident[:])
                    last.then_inc(prep_full, 1)
                elif kind == "pv":
                    pe.wait_ge(pv_copied, T_.up("group"))
                    for q in range(QT):
                        last = nc.tensor.transpose(prep[:, q * P:(q + 1) * P], pvs[:, q * P:(q + 1) * P], ident[:])
                    last.then_inc(prep_full, 1)
                elif kind == "attnT":
                    pe.wait_ge(attn_ready, T_.up("out"))
                    for q in range(QT):
                        last = nc.tensor.transpose(prep[:, q * P:(q + 1) * P], attn[:, q, :], ident[:])
                    last.then_inc(prep_full, 1)
                elif kind == "out":
                    for q in range(QT):
                        last = nc.tensor.matmul(prep[:, q * D:(q + 1) * D], attnT[:, q * P:(q + 1) * P], wo[:],
                                                start=True, stop=True)
                    last.then_inc(prep_full, 1)

            def unit(g, u):
                T_.up("unit")
                wait(pe, max_done, T_.now("unit", 2))
                q, c, hh = u // (4 * GH), u // GH % 4, u % GH
                lo, hi = CHUNKS[c]
                h = g * GH + hh
                nc.tensor.matmul(psum[:, 2 + u % 2, 0:hi - lo], queries_of(qst, h, slice(q * P, q * P + P)),
                                 keys_of(kst, h, slice(lo, hi)), start=True, stop=True).then_inc(max_full, 1)

            def values():
                g, kt, buf, back = pending.pop()
                pe.wait_ge(exp_done, T_.now("step", back))
                k = tile_rows(kt)
                for hh in range(GH):
                    c = (hh % 2) * 2 * T + (hh // 2) * T
                    last = nc.tensor.matmul(pv[32 * hh:32 * hh + 32, :], v_aug[0:k, kt, g * GH + hh, :],
                                            prob[0:k, buf, c:c + T], start=(kt == 0), stop=(kt == KT - 1),
                                            tile_position=(0, 32 * hh))
                last.then_inc(pv_done, 1)

            def prologue():
                pe.wait_ge(w_loaded, N_W * 16)
                for it in PROLOGUE_ITEMS[:-1]:
                    item(*it)
                pe.wait_ge(stacked, 48 * 16)
                T_.up("stacked", 48 * 16)
                for u in range(UNITS_B):
                    unit(0, u)
                item(*PROLOGUE_ITEMS[-1])
                for u in range(UNITS_B - 22):
                    unit(1, u)

            def part(i, r, first, last):
                g = (r + 1) % 4
                for n in range(KT):
                    T_.up("step")
                    if n == 0:
                        pe.wait_ge(m_stacked, T_.up("m_stacked", 64))
                    wait(pe, exp_done, T_.now("step", 2))
                    k, buf = tile_rows(n), (T_.n["step"] - 1) % 2
                    for hh in range(GH):
                        h = g * GH + hh
                        lastmm = nc.tensor.matmul(psum[0:k, 4 + 2 * buf + hh % 2, (hh // 2) * T:(hh // 2) * T + T],
                                                  keys_of(kst, h, slice(n * P, n * P + k)),
                                                  queries_of(qst, h, slice(0, T)), start=True, stop=True)
                    lastmm.then_inc(st_full, 1)
                    if units_left(r, n, last):
                        for u in units_of_step(n):
                            unit_group = (g + 1) % 4 if n < M_STEP else (g + 2) % 4
                            if u == 0 and unit_group % 2 == 0 and not first:
                                pe.wait_ge(stacked, T_.up("stacked", 24 * 16))
                            unit(unit_group, u)
                    it = prep_item(r, n, first, last)
                    if it:
                        item(*it)
                    if n == 1 and not first:
                        pe.wait_ge(pv_copied, T_.now("group", -1))
                    if n == 1 and r == 3:
                        pe.wait_ge(v_placed, T_.up("placed", 2 if first else 1))
                    if n == 1 and r == 1:
                        pe.wait_ge(v_placed, T_.now("placed"))
                    if pending:
                        values()
                    pending.append((g, n, buf, 1))
                if r == 3 and not first:
                    T_.up("placed")

            parts_of_program(pe, T_, prologue, part)
            pending[0] = pending[0][:3] + (0,)
            values()
            for it in (("pv", 3), ("attnT", 0), ("out", 0)):
                item(*it)


CH, CD = 16, 64
UN = CH // 2
C_ITEMS = {0: [("x", 0), ("c", 1)], 1: [("v", 0)], 2: [("c", 2), ("v", 1)], 4: [("c", 3), ("v", 2)],
           5: [("o", 0), ("v", 3)], 6: [("c", 0)]}
C_PREV = (("c", 1), ("c", 2), ("c", 3), ("o", 0))
SCORES_LAG, TURN_LAG, VALUES_LAG = 2, 3, 4


def c_items(slot, first, drain):
    return [it for it in C_ITEMS.get(slot, []) if not (first and it in C_PREV) and not (drain and it not in C_PREV)]


def c_unit(slot, lag, first, drain):
    n = slot - lag
    if (n < 0 and first) or (n >= 0 and drain):
        return None
    return n % UN


def rotary_tables(nc, a, t, sem, tab, w1, w2, raw, bias, theta):
    import numpy as np
    two_pi = 2 * np.pi
    c1 = 6.28125
    c2 = float(np.float32(np.uint32(np.float32(two_pi - c1).view(np.uint32) & 0xFFFFF000).view(np.float32)))
    c3 = float(np.float32(two_pi - c1 - c2))
    magic = 1.5 * 2 ** 23
    with nc.Block() as block, ExitStack() as ctx:
        loaded, pos_set, own, reduced, made = sem("t_loaded"), sem("t_pos"), sem("t_own"), sem("t_reduced"), sem("t_made")
        pos = ctx.enter_context(nc.sbuf_tensor("t_pos", [P, T], F32))
        posi = ctx.enter_context(nc.sbuf_tensor("t_posi", [P, T], mybir.dt.int32))
        ang, k, r = (ctx.enter_context(nc.sbuf_tensor("t_" + n, [P, 2, T], F32)) for n in ("ang", "k", "r"))
        copied = sem("t_copied")

        @block.sync
        def _(sp):
            n = 0
            for m, name in enumerate(("q_w", "k_w")):
                sp.dma_start(raw[:, m, :], a["L0_ffn_" + name]).then_inc(loaded, 16)
                n += 1
            with nc.allow_non_contiguous_dma(reason="biases are spread over partitions once"):
                for quarter in range(4):
                    sp.dma_start(theta[32 * quarter:32 * quarter + 32, :], a["L0_ffn_theta"].rearrange("(p a) -> p a", a=1))\
                        .then_inc(loaded, 16)
                    n += 1
                    hh, par = quarter // 2, quarter % 2
                    for m, name in enumerate(("q_b", "k_b")):
                        v = a["L0_ffn_" + name].rearrange("(j h f a) -> h a f j", j=UN, h=2, a=2)
                        for w in range(2):
                            sp.dma_start(bias[32 * quarter:32 * quarter + 32, m, w, :], v[hh, (par + w) % 2]).then_inc(loaded, 16)
                            n += 1
            sp.wait_ge(loaded, 16 * n)

        @block.gpsimd
        def _(pool):
            nc.gpsimd.iota(posi[:], pattern=[[1, T]], base=0, channel_multiplier=0).then_inc(pos_set, 1)
            pool.wait_ge(loaded, 16 * 22)
            for m in range(2):
                v = raw[:, m, :].rearrange("p (g f a) -> p g a f", g=CH, a=2)
                for par in range(2):
                    nc.gpsimd.tensor_copy(w1[:, m, :].rearrange("p (g a f) -> p g a f", g=CH, a=2)[:, :, par], v[:, :, par])
                    nc.gpsimd.tensor_copy(w2[:, m, :].rearrange("p (g a f) -> p g a f", g=CH, a=2)[:, :, par], v[:, :, 1 - par])

        @block.vector
        def _(dve):
            n = 0

            def link(ins):
                nonlocal n
                n += 1
                ins.then_inc(own, 1)
                dve.wait_ge(own, n)

            dve.wait_ge(pos_set, 1)
            link(nc.vector.tensor_copy(pos[:], posi[:]))
            dve.wait_ge(loaded, 16 * 22)
            for m in range(2):
                link(nc.vector.tensor_scalar(ang[:, m, :], pos[:], theta[:], None, ALU.mult))
            for m in range(2):
                link(nc.vector.tensor_scalar(k[:, m, :], ang[:, m, :], 1.0 / two_pi, 0.25 * (1 - m), ALU.mult, ALU.add))
            link(nc.vector.tensor_scalar_add(k[:], k[:], magic))
            link(nc.vector.tensor_scalar_add(k[:], k[:], -magic))
            for c in (c1, c2, c3):
                link(nc.vector.tensor_scalar(r[:], k[:], -c, None, ALU.mult))
                link(nc.vector.tensor_tensor(ang[:], ang[:], r[:], ALU.add))
            link(nc.vector.tensor_scalar_add(ang[:, 0, :], ang[:, 0, :], np.pi / 2))
            nc.vector.tensor_scalar(r[:], ang[:], 3.1415925, -3.1415925, ALU.min, ALU.max).then_inc(reduced, 1)
            dve.wait_ge(made, 1)
            for q in range(0, P, 64):
                link(nc.vector.tensor_scalar(tab[q:q + 32, 1, 1, :], tab[q:q + 32, 1, 1, :], -1.0, None, ALU.mult))
            nc.vector.tensor_scalar(tab[:, 0, :, :], tab[:, 1, :, :], CD ** -0.5, None, ALU.mult)

        @block.scalar
        def _(act):
            act.wait_ge(reduced, 1)
            nc.scalar.activation(tab[:, 1, :, :], r[:], ACT.Sin).then_inc(made, 1)


def rotary_attention(nc, a, t, psum, s, an_all):
    ctx = ExitStack()
    with ctx:
        def sb(name, shape, dt=F32):
            return ctx.enter_context(nc.sbuf_tensor(name, shape, dt))

        def sem(name):
            return ctx.enter_context(nc.semaphore(name))

        w1, w2 = sb("c_w1", [P, 2, CH * CD]), sb("c_w2", [P, 2, CH * CD])
        tab = sb("c_tab", [P, 2, 2, T])
        bias, theta = sb("c_bias", [P, 2, 2, UN]), sb("c_theta", [P, 1])
        vw, ow = sb("c_vw", [D, CH * CD]), sb("c_ow", [P, UN, D])
        rows = sb("c_rows", [P, 3, D])
        vb = sb("c_vb", [P, CH * CD])
        xT = sb("c_xT", [P, T])
        resid, o = sb("c_resid", [P, QT, D]), sb("c_o", [P, QT, D])
        turned = sb("c_turned", [P, 2, 2, 2, T])
        qz = sb("c_qz", [P, CH, T])
        kT = sb("c_kT", [P, UN, T])
        v_aug = sb("c_v_aug", [P, QT, CH, CD + 1])
        mneg = sb("c_mneg", [P, 2, QT, 2])
        prob = sb("c_prob", [P, 2, 2, 3 * P])
        probT = sb("c_probT", [P, 2, 2, 3 * P])
        rec = sb("c_rec", [P, 2, QT])
        att = sb("c_att", [P, QT, CH * CD])
        attT = sb("c_attT", [P, UN, T])
        with nc.sbuf_tensor("c_raw", [P, 2, CH * CD], F32) as raw:
            rotary_tables(nc, a, t, sem, tab, w1, w2, raw, bias, theta)

        item_full, item_free = sem("c_item_full"), sem("c_item_free")
        w_loaded, cleared = sem("c_w_loaded"), sem("c_cleared")
        var_ready, rstd_ready, xr_ready = sem("c_var_ready"), sem("c_rstd_ready"), sem("c_xr_ready")
        own_dve, own_pool = sem("c_own_dve"), sem("c_own_pool")
        proj_full, terms_ready, turned_ready = sem("c_proj_full"), sem("c_terms_ready"), sem("c_turned_ready")
        s_full, m_ready, exp_done = sem("c_s_full"), sem("c_m_ready"), sem("c_exp_done")
        tp_full, probT_ready, pv_full, att_ready = sem("c_tp_full"), sem("c_probT_ready"), sem("c_pv_full"), sem("c_att_ready")
        o_ready, resid_ready, x_done = sem("c_o_ready"), sem("c_resid_ready"), sem("c_x_done")
        v_done = sem("c_v_done")
        q_bank, k_bank, s0_bank, s1_bank = psum[:, 0, :], psum[:, 1, :], psum[:, 2, :], psum[:, 3, :]
        misc, pv_bank = psum[:, 6, :], psum[:, 7, :]
        PER = dict(unit=UN, scores=UN, turn=UN, values=UN, item=10, batch=1, norm=3, out=1, v=4, own_pool=2 * UN,
                   own_dve=(NORM_LINKS + RMS_LINKS) + RMS_LINKS + UN + 3)
        N_W = 6
        block = ctx.enter_context(nc.Block())

        def program(eng, tally, slot):
            for n in range(UN):
                slot(0, n, True, False)
            with eng.Fori(0, B - 1) as i:
                tally.enter(i)
                for n in range(UN):
                    slot(i, n, False, False)
                tally.leave(B - 1)
            for n in range(max(VALUES_LAG, 6)):
                slot(B - 1, n, False, True)

        @block.sync
        def _(sp):
            sp.dma_start(vw[:], a["L0_ffn_v_w"]).then_inc(w_loaded, 16)
            sp.dma_start(ow[:], a["L0_ffn_o_w"].rearrange("(j p) d -> p j d", p=P)).then_inc(w_loaded, 16)
            for n, name in enumerate(("gamma1", "gamma2", "o_b")):
                sp.dma_start(rows[:, n, :], a["L0_ffn_" + name].rearrange("(a d) -> a d", a=1).to_broadcast([P, D]))\
                    .then_inc(w_loaded, 16)
            sp.dma_start(vb[:], a["L0_ffn_v_b"].rearrange("(a d) -> a d", a=1).to_broadcast([P, CH * CD])).then_inc(w_loaded, 16)
            sp.wait_ge(w_loaded, N_W * 16)

        @block.gpsimd
        def _(pool):
            T_ = Tally(PER)
            nc.gpsimd.memset(qz[:], 0.0).then_inc(cleared, 1)
            nc.gpsimd.memset(v_aug[:], 1.0).then_inc(cleared, 1)
            pool.wait_ge(cleared, 2)
            pool.wait_ge(w_loaded, N_W * 16)

            def power():
                pool.wait_ge(var_ready, T_.up("norm"))
                nc.gpsimd.tensor_tensor(s["rstd"][:], s["ve"][:], t["neg_half"][:], ALU.pow).then_inc(rstd_ready, 1)

            def slot(i, n, first, drain):
                if n == 0 and not drain:
                    power()
                    power()
                u = c_unit(n, 0, first, drain)
                if ("o", 0) in c_items(n, first, drain):
                    power()
                if u is not None:
                    pool.wait_ge(terms_ready, T_.up("unit"))
                    par = u % 2
                    for hh in range(2):
                        r = slice(64 * hh, 64 * hh + 64)
                        nc.gpsimd.tensor_tensor(qz[r, 2 * u + hh, :], turned[r, par, 0, 0, :], turned[r, par, 0, 1, :], ALU.add)\
                            .then_inc(own_pool, 1)
                        pool.wait_ge(own_pool, T_.up("own_pool"))
                    nc.gpsimd.tensor_tensor(kT[:, u, :], turned[:, par, 1, 0, :], turned[:, par, 1, 1, :], ALU.add)\
                        .then_inc(turned_ready, 1)
                    pool.wait_ge(turned_ready, T_.now("unit"))
                if n == 6 and not drain:
                    wait(pool, x_done, T_.now("out"))
                    T_.up("out")
                    for q in range(QT):
                        ins = nc.gpsimd.tensor_tensor(resid[:, q, :], s["xr"][:, q, :], rows[:, 2, :], ALU.add)
                    ins.then_inc(resid_ready, 1)

            program(pool, T_, slot)

        @block.vector
        def _(dve):
            T_ = Tally(PER)
            dve.wait_ge(w_loaded, N_W * 16)

            def own(ins):
                ins.then_inc(own_dve, 1)
                dve.wait_ge(own_dve, T_.up("own_dve"))

            def item(kind, g, b):
                n = T_.up("item")
                if kind == "v":
                    dve.wait_ge(item_full, n)
                    q, half = g % 2, g // 2
                    w = CH * CD // 2
                    nc.vector.tensor_tensor(v_aug[:, q, 8 * half:8 * half + 8, 0:CD], misc.rearrange("p (h d) -> p h d", h=8),
                                            vb[:, half * w:half * w + w].rearrange("p (h d) -> p h d", h=8), ALU.add)\
                        .then_inc(v_done, 1)
                    dve.wait_ge(v_done, T_.up("v"))
                    dve.sem_inc(item_free, 1)
                elif kind == "o":
                    dve.wait_ge(resid_ready, T_.up("out"))
                    dve.wait_ge(item_full, n)
                    own(nc.vector.tensor_tensor(o[:], misc[:, 0:2 * D].rearrange("p (q d) -> p q d", q=QT), resid[:], ALU.add))
                    dve.sem_inc(item_free, 1)
                    s2 = dict(s, xn=o, xr=t["an_cur"])
                    T_.up("norm")
                    rms_norm(nc, dve, own, s2, rows[:, 1, :], 1e-5, var_ready, rstd_ready, T_.now("norm"), lambda: None)
                    own(nc.vector.tensor_copy(an_all[:, bass.ds(b * QT, QT), :], t["an_cur"][:]))
                    own(nc.vector.tensor_tensor(o[:], o[:], t["an_cur"][:], ALU.add))
                    x = t["x"][:, bass.ds(b * QT, QT), :]
                    nc.vector.tensor_tensor(x, x, o[:], ALU.add).then_inc(x_done, 1)

            def slot(i, n, first, drain):
                b = B - 1 if drain else i + (not first)
                if n == 0 and not drain:
                    T_.up("norm")
                    layer_norm(nc, dve, own, lambda q: t["x"][:, bass.ds(b * QT + q, 1), :].rearrange("p a d -> p (a d)"),
                               s, var_ready, rstd_ready, T_.now("norm"))
                    T_.up("norm")
                    rms_norm(nc, dve, own, s, rows[:, 0, :], 1e-5, var_ready, rstd_ready, T_.now("norm"),
                             lambda: dve.sem_inc(xr_ready, 1))
                u = c_unit(n, SCORES_LAG, first, drain)
                if u is not None:
                    dve.wait_ge(s_full, T_.up("scores"))
                    par = u % 2
                    nc.vector.tensor_reduce(out=mneg[:, par, 0, :], in_=s0_bank[:, 0:2 * P].rearrange("p (h k) -> p h k", h=2),
                                            axis=AX.X, op=ALU.max, negate=True)
                    nc.vector.tensor_reduce(out=mneg[:, par, 1, :], in_=s1_bank.rearrange("p (h k) -> p h k", h=2),
                                            axis=AX.X, op=ALU.max, negate=True).then_inc(m_ready, 1)
                u = c_unit(n, VALUES_LAG, first, drain)
                if u is not None:
                    dve.wait_ge(pv_full, T_.up("values"))
                    v = pv_bank[:, 0:4 * (CD + 1)].rearrange("p (h q c) -> p h q c", h=2, q=QT)
                    own(nc.vector.reciprocal(rec[:], v[:, :, :, CD]))
                    nc.vector.tensor_tensor(att[:, :, P * u:P * u + P].rearrange("p q (h d) -> p h q d", h=2), v[:, :, :, 0:CD],
                                            rec[:].rearrange("p h (q a) -> p h q a", a=1).to_broadcast([P, 2, QT, CD]), ALU.mult)\
                        .then_inc(att_ready, 1)
                for it in c_items(n, first, drain):
                    item(*it, (B - 1 if drain else i))
                u = c_unit(n, 0, first, drain)
                if u is not None:
                    v = T_.up("unit")
                    dve.wait_ge(proj_full, v)
                    wait(dve, turned_ready, T_.now("unit", 2))
                    for m, bank in enumerate((q_bank, k_bank)):
                        for w in range(2):
                            ins = nc.vector.scalar_tensor_tensor(out=turned[:, u % 2, m, w, :], in0=bank[:, w * T:(w + 1) * T],
                                                                 scalar=bias[:, m, w, u:u + 1], in1=tab[:, m, w, :],
                                                                 op0=ALU.add, op1=ALU.mult)
                    ins.then_inc(terms_ready, 1)

            program(dve, T_, slot)

        @block.scalar
        def _(act):
            T_ = Tally(PER)

            def slot(i, n, first, drain):
                u = c_unit(n, SCORES_LAG, first, drain)
                if u is not None:
                    act.wait_ge(m_ready, T_.up("scores"))
                    wait(act, tp_full, T_.now("scores", 2))
                    par = u % 2
                    for hh in range(2):
                        nc.scalar.activation(prob[:, par, hh, 0:P], s0_bank[:, hh * P:(hh + 1) * P], ACT.Exp,
                                             bias=mneg[:, par, 0, hh:hh + 1])
                        ins = nc.scalar.activation(prob[:, par, hh, P:3 * P], s1_bank[:, hh * 2 * P:(hh + 1) * 2 * P], ACT.Exp,
                                                   bias=mneg[:, par, 1, hh:hh + 1])
                    ins.then_inc(exp_done, 1)
                u = c_unit(n, TURN_LAG, first, drain)
                if u is not None:
                    act.wait_ge(tp_full, T_.up("turn"))
                    wait(act, pv_full, T_.now("turn", 2))
                    nc.scalar.activation(probT[:, u % 2, :, :], psum[:, 4:6, 0:3 * P], ACT.Copy).then_inc(probT_ready, 1)
                for kind, g in c_items(n, first, drain):
                    v = T_.up("item")
                    if kind == "x":
                        act.wait_ge(item_full, v)
                        nc.scalar.activation(xT[:], misc[:, 0:T], ACT.Copy).then_inc(item_free, 1)
                    elif kind == "c":
                        act.wait_ge(item_full, v)
                        nc.scalar.activation(attT[:, 2 * g:2 * g + 2, :].rearrange("p j t -> p (j t)"), misc, ACT.Copy)\
                            .then_inc(item_free, 1)

            program(act, T_, slot)

        @block.tensor
        def _(pe):
            T_ = Tally(PER)
            pe.wait_ge(w_loaded, N_W * 16)
            pe.wait_ge(cleared, 2)

            def item(kind, g):
                T_.up("item")
                wait(pe, item_free, T_.now("item", 1))
                if kind == "x":
                    pe.wait_ge(xr_ready, T_.up("batch"))
                    for q in range(QT):
                        last = nc.tensor.transpose(misc[:, q * P:(q + 1) * P], s["xr"][:, q, :], t["ident"][:])
                elif kind == "v":
                    q, half = g % 2, g // 2
                    if g == 0:
                        pe.wait_ge(item_free, T_.now("item", 1))
                    w = CH * CD // 2
                    last = nc.tensor.matmul(misc, xT[:, q * P:(q + 1) * P], vw[:, half * w:half * w + w], start=True, stop=True)
                elif kind == "c":
                    for j in range(2):
                        for q in range(QT):
                            last = nc.tensor.transpose(misc[:, (j * QT + q) * P:(j * QT + q + 1) * P],
                                                       att[:, q, (2 * g + j) * P:(2 * g + j + 1) * P], t["ident"][:])
                elif kind == "o":
                    for q in range(QT):
                        for j in range(UN):
                            last = nc.tensor.matmul(misc[:, q * D:(q + 1) * D], attT[:, j, q * P:(q + 1) * P], ow[:, j, :],
                                                    start=(j == 0), stop=(j == UN - 1))
                last.then_inc(item_full, 1)

            def slot(i, n, first, drain):
                u = c_unit(n, SCORES_LAG, first, drain)
                if u is not None:
                    pe.wait_ge(turned_ready, T_.up("scores"))
                    wait(pe, exp_done, T_.now("scores", 1))
                    nc.tensor.matmul(s0_bank[:, 0:2 * P], t["identb"][:], t["mask_qk0"][:, 0:2].rearrange("p h k -> p (h k)"),
                                     start=True, stop=False)
                    nc.tensor.matmul(s1_bank, t["identb"][:], t["mask_qk1"][:].rearrange("p h k -> p (h k)"), start=True, stop=False)
                    for hh in range(2):
                        nc.tensor.matmul(s0_bank[:, hh * P:(hh + 1) * P], qz[:, 2 * u + hh, 0:P], kT[:, u, 0:P],
                                         start=False, stop=(hh == 1))
                        last = nc.tensor.matmul(s1_bank[:, hh * 2 * P:(hh + 1) * 2 * P], qz[:, 2 * u + hh, P:2 * P], kT[:, u, :],
                                                start=False, stop=(hh == 1))
                    last.then_inc(s_full, 1)
                u = c_unit(n, TURN_LAG, first, drain)
                if u is not None:
                    pe.wait_ge(exp_done, T_.up("turn"))
                    wait(pe, probT_ready, T_.now("turn", 1))
                    for hh in range(2):
                        for k in range(3):
                            last = nc.tensor.transpose(psum[:, 4 + hh, k * P:(k + 1) * P], prob[:, u % 2, hh, k * P:(k + 1) * P],
                                                       t["ident"][:])
                    last.then_inc(tp_full, 1)
                u = c_unit(n, VALUES_LAG, first, drain)
                if u is not None:
                    pe.wait_ge(probT_ready, T_.up("values"))
                    wait(pe, att_ready, T_.now("values", 1))
                    if u % 4 == 0:
                        pe.wait_ge(v_done, T_.up("v", 2))
                    for hh in range(2):
                        for q in range(QT):
                            c = (hh * QT + q) * (CD + 1)
                            for kt in range(q + 1):
                                last = nc.tensor.matmul(pv_bank[:, c:c + CD + 1], probT[:, u % 2, hh, (q + kt) * P:(q + kt + 1) * P],
                                                        v_aug[:, kt, 2 * u + hh, :], start=(kt == 0), stop=(kt == q))
                    last.then_inc(pv_full, 1)
                for kind, g in c_items(n, first, drain):
                    if kind == "c":
                        pe.wait_ge(att_ready, T_.now("values"))
                    item(kind, g)
                u = c_unit(n, 0, first, drain)
                if u is not None:
                    T_.up("unit")
                    if n == 0:
                        pe.wait_ge(item_free, T_.now("item") if not any(it == ("c", 1) for it in c_items(n, first, drain)) else T_.now("item", 1))
                    wait(pe, terms_ready, T_.now("unit", 1))
                    for m, bank in enumerate((q_bank, k_bank)):
                        for w, weights in enumerate((w1, w2)):
                            last = nc.tensor.matmul(bank[:, w * T:(w + 1) * T], weights[:, m, u * P:(u + 1) * P], xT[:],
                                                    start=True, stop=True)
                    last.then_inc(proj_full, 1)

            program(pe, T_, slot)


NE = 31
TOP = 3
GW = 4 * 32
WCH = 4
TW = B * T // WCH


def gates_of_experts(nc, a, t, psum, d):
    ctx = ExitStack()
    with ctx:
        def sb(name, shape, dt=F32):
            return ctx.enter_context(nc.sbuf_tensor(name, shape, dt))

        def sem(name):
            return ctx.enter_context(nc.semaphore(name))

        NT = B * QT
        PAD = 40
        rw, rb = sb("g_rw", [P, NE]), sb("g_rb", [P, NE])
        b1 = sb("g_b1", [32, P])
        lg = sb("g_lg", [P, NT, NE])
        mx, sm = sb("g_mx", [P, NT]), sb("g_sm", [P, NT])
        aff, cut = sb("g_aff", [P, NT, PAD]), sb("g_cut", [P, NT, PAD])
        top = sb("g_top", [P, NT, 8])
        gates, rest = sb("g_gates", [P, NT, 32]), sb("g_rest", [P, NT, 32])
        parts = sb("g_parts", [P, NT, 4, 32], BF16)
        sel1 = sb("g_sel1", [P, 32], BF16)
        loaded, own, pool_own = sem("g_loaded"), sem("g_own"), sem("g_pool_own")
        turned, copied, logits, sums = sem("g_turned"), sem("g_copied"), sem("g_logits"), sem("g_sums")
        exp_done, gates_ready, sel_ready = sem("g_exp_done"), sem("g_gates_ready"), sem("g_sel_ready")
        gates_turned, gates_copied = sem("g_gates_turned"), sem("g_gates_copied")
        N_W = 6
        block = ctx.enter_context(nc.Block())

        @block.sync
        def _(sp):
            sp.dma_start(rw[:], a["L0_ffn_router_w"]).then_inc(loaded, 16)
            sp.dma_start(rb[:], a["L0_ffn_router_b"].rearrange("(a e) -> a e", a=1).to_broadcast([P, NE])).then_inc(loaded, 16)
            for dst, name, shared in ((b1, "re_b1", "sh_b1"), (d["b2"], "re_b2", "sh_b2")):
                sp.dma_start(dst[0:NE, :], a["L0_ffn_" + name]).then_inc(loaded, 16)
                sp.dma_start(dst[NE:32, :], a["L0_ffn_" + shared].rearrange("(a d) -> a d", a=1)).then_inc(loaded, 16)
            sp.wait_ge(loaded, N_W * 16)

        @block.gpsimd
        def _(pool):
            nc.gpsimd.memset(sel1[:], 0.0).then_inc(pool_own, 1)
            for k in range(3):
                pool.wait_ge(pool_own, k + 1)
                nc.gpsimd.affine_select(out=sel1[:], in_=sel1[:], compare_op=ALU.not_equal, fill=1.0, base=-32 * k,
                                        pattern=[[-1, 32]], channel_multiplier=1).then_inc(pool_own, 1)

        @block.vector
        def _(dve):
            n = 0

            def link(ins):
                nonlocal n
                n += 1
                ins.then_inc(own, 1)
                dve.wait_ge(own, n)

            def wide(v, w):
                return v.rearrange("p (t a) -> p t a", a=1).to_broadcast([P, NT, w])

            nc.vector.memset(aff[:], -1.0)
            nc.vector.memset(parts[:], 0.0)
            dve.wait_ge(pool_own, 4)
            nc.vector.tensor_copy(d["sel"][:], sel1[:].rearrange("p (e a) -> p e a", a=1).to_broadcast([P, 32, P]))
            dve.wait_ge(loaded, N_W * 16)
            dve.wait_ge(logits, 1)
            link(nc.vector.tensor_tensor(lg[:], psum[:, 4, :].rearrange("p (t e) -> p t e", e=32)[:, :, 0:NE],
                                         rb[:].rearrange("p (a e) -> p a e", a=1).to_broadcast([P, NT, NE]), ALU.add))
            link(nc.vector.tensor_reduce(out=mx[:], in_=lg[:], axis=AX.X, op=ALU.max))
            link(nc.vector.tensor_tensor(lg[:], lg[:], wide(mx[:], NE), ALU.subtract))
            dve.sem_inc(sums, 1)
            dve.wait_ge(exp_done, 1)
            link(nc.vector.tensor_reduce(out=sm[:], in_=lg[:], axis=AX.X, op=ALU.add))
            link(nc.vector.reciprocal(sm[:], sm[:]))
            link(nc.vector.tensor_tensor(aff[:, :, 0:NE], lg[:], wide(sm[:], NE), ALU.mult))
            for k in range(NT):
                ins = nc.vector.max(top[:, k, :], aff[:, k, :])
            link(ins)
            link(nc.vector.memset(top[:, :, TOP:8], -1.0))
            for k in range(NT):
                ins = nc.vector.match_replace(out=cut[:, k, :], in_to_replace=top[:, k, :], in_values=aff[:, k, :], imm_value=-2.0)
            link(ins)
            link(nc.vector.tensor_tensor(cut[:, :, 0:NE], cut[:, :, 0:NE], aff[:, :, 0:NE], ALU.not_equal))
            link(nc.vector.tensor_tensor(gates[:, :, 0:NE], cut[:, :, 0:NE], aff[:, :, 0:NE], ALU.mult))
            link(nc.vector.memset(gates[:, :, NE:32], 1.0))
            split3(nc, dve, link, [parts[:, :, k, :] for k in range(3)], rest[:], gates[:]).then_inc(gates_ready, 1)

        @block.scalar
        def _(act):
            for c in range(WCH):
                act.wait_ge(turned, c + 1)
                nc.scalar.activation(d["anT"][:, c * TW:(c + 1) * TW], psum[:, c, :], ACT.Copy).then_inc(copied, 1)
            act.wait_ge(turned, WCH + 1)
            nc.scalar.activation(d["b1T"][:], psum[:, 5, 0:32], ACT.Copy).then_inc(copied, 1)
            act.wait_ge(sums, 1)
            nc.scalar.activation(lg[:], lg[:], ACT.Exp).then_inc(exp_done, 1)
            for c in range(WCH):
                act.wait_ge(gates_turned, c + 1)
                nc.scalar.activation(d["gatesT"][:, c * TW:(c + 1) * TW], psum[0:32, c, :], ACT.Copy)
                nc.scalar.activation(d["gparts"][:, c * TW:(c + 1) * TW], psum[:, 4 + c, :], ACT.Copy).then_inc(gates_copied, 1)

        @block.tensor
        def _(pe):
            per = NT // WCH
            for c in range(WCH):
                for k in range(per):
                    ins = nc.tensor.transpose(psum[:, c, k * P:(k + 1) * P], d["an"][:, c * per + k, :], t["ident"][:])
                ins.then_inc(turned, 1)
            pe.wait_ge(loaded, N_W * 16)
            nc.tensor.transpose(psum[:, 5, 0:32], b1[:], t["ident"][0:32, 0:32]).then_inc(turned, 1)
            for k in range(NT):
                if k % per == 0:
                    pe.wait_ge(copied, k // per + 1)
                ins = nc.tensor.matmul(psum[:, 4, k * 32:k * 32 + NE], d["anT"][:, k * P:(k + 1) * P], rw[:], start=True, stop=True)
            ins.then_inc(logits, 1)
            pe.wait_ge(copied, WCH + 1)
            pe.wait_ge(gates_ready, 1)
            for c in range(WCH):
                for k in range(c * per, (c + 1) * per):
                    cols = slice((k % per) * P, (k % per + 1) * P)
                    nc.tensor.transpose(psum[0:32, c, cols], gates[:, k, :], t["ident"][:])
                    ins = nc.tensor.matmul(psum[:, 4 + c, cols], parts[:, k, :, :].rearrange("p s e -> p (s e)"), t["identb"][:],
                                           start=True, stop=True)
                ins.then_inc(gates_turned, 1)


def experts(nc, a, t, psum, d, out):
    ctx = ExitStack()
    with ctx:
        def sb(name, shape, dt=F32):
            return ctx.enter_context(nc.sbuf_tensor(name, shape, dt))

        def sem(name):
            return ctx.enter_context(nc.semaphore(name))

        w = sb("e_w", [P, 2, 2, P])
        gl = sb("e_gl", [P, 2, TW])
        hg = sb("e_hg", [P, 2, TW])
        yT = sb("e_yT", [P, WCH, TW])
        h_full, gelu_done, passed = sem("e_h_full"), sem("e_gelu_done"), sem("e_passed")
        w_loaded = [sem("e_w_loaded0"), sem("e_w_loaded1")]
        g_full, hg_ready, y_done = sem("e_g_full"), sem("e_hg_ready"), sem("e_y_done")
        b2_done, y_copied, y_turned, x_done, stored = (sem("e_b2_done"), sem("e_y_copied"), sem("e_y_turned"),
                                                       sem("e_x_done"), sem("e_stored"))
        ROUNDS = NE // 2
        STEPS = 2 * WCH
        PER = dict(step=STEPS, y=STEPS, load=1)
        block = ctx.enter_context(nc.Block())

        def program(tally, eng, part):
            for k in range(STEPS):
                part(None, k)
            with eng.Fori(0, ROUNDS) as i:
                tally.enter(i)
                for k in range(STEPS):
                    part(i, k)
                tally.leave(ROUNDS)

        @block.sync
        def _(sp):
            T_ = Tally(PER)

            def load(e, j):
                for m in range(2):
                    if e is None:
                        src = a["L0_ffn_sh_w%d" % (m + 1)]
                    else:
                        v = a["L0_ffn_re_w%d" % (m + 1)]
                        src = v[e, :, :] if isinstance(e, int) else v[bass.ds(e, 1), :, :].rearrange("a p d -> p (a d)")
                    sp.dma_start(w[:, j, m, :], src).then_inc(w_loaded[j], 16)

            load(None, 0)
            load(0, 1)
            T_.n["y"] = 0
            with sp.Fori(0, ROUNDS) as i:
                T_.enter(i)
                for j in range(2):
                    sp.wait_ge(y_done, T_.up("y", WCH))
                    load(i * 2 + 1 + j, j)
                T_.leave(ROUNDS)
            for c in range(WCH):
                sp.wait_ge(x_done, c + 1)
                sp.dma_start(out.rearrange("b (q p) d -> p (b q) d", p=P)[:, c * 4:(c + 1) * 4, :], t["x"][:, c * 4:(c + 1) * 4, :])\
                    .then_inc(stored, 16)
            sp.wait_ge(stored, WCH * 16)

        @block.scalar
        def _(act):
            T_ = Tally(PER)

            def part(i, k):
                act.wait_ge(h_full, T_.up("step"))
                wait(act, hg_ready, T_.now("step", 2))
                act.sem_inc(passed, 1)
                j = k // WCH
                b1 = d["b1T"][:, (NE, 0)[j]:(NE, 0)[j] + 1] if i is None else d["b1T"][:, bass.ds(i * 2 + 1 + j, 1)]
                nc.scalar.activation(gl[:, k % 2, :], psum[:, 4 + k % 2, :], ACT.Gelu, bias=b1).then_inc(gelu_done, 1)

            program(T_, act, part)
            for c in range(WCH):
                act.wait_ge(b2_done, c + 1)
                nc.scalar.activation(yT[:, c, :], psum[:, c, :], ACT.Copy).then_inc(y_copied, 1)

        @block.vector
        def _(dve):
            T_ = Tally(PER)

            def part(i, k):
                v = T_.up("step")
                dve.wait_ge(gelu_done, v)
                dve.wait_ge(g_full, v)
                wait(dve, y_done, T_.now("step", 2))
                nc.vector.tensor_tensor(hg[:, k % 2, :], gl[:, k % 2, :], psum[:, 6 + k % 2, :], ALU.mult).then_inc(hg_ready, 1)

            program(T_, dve, part)
            for c in range(WCH):
                dve.wait_ge(y_turned, c + 1)
                x = t["x"][:, c * 4:(c + 1) * 4, :]
                nc.vector.tensor_tensor(x, x, psum[:, 4 + c, :].rearrange("p (q d) -> p q d", q=4), ALU.add).then_inc(x_done, 1)

        @block.tensor
        def _(pe):
            T_ = Tally(PER)

            def second(c, j, buf):
                pe.wait_ge(hg_ready, T_.up("y"))
                nc.tensor.matmul(psum[:, c, :], w[:, j, 1, :], hg[:, buf, :], start=second.start, stop=False).then_inc(y_done, 1)

            second.start = True

            def part(i, k):
                T_.up("step")
                j, c = divmod(k, WCH)
                if c == 0:
                    if j == 0:
                        T_.up("load")
                    pe.wait_ge(w_loaded[j], 32 * T_.now("load"))
                wait(pe, gelu_done, T_.now("step", 2))
                nc.tensor.matmul(psum[:, 4 + k % 2, :], w[:, j, 0, :], d["anT"][:, c * TW:(c + 1) * TW], start=True, stop=True)\
                    .then_inc(h_full, 1)
                wait(pe, hg_ready, T_.now("step", 2))
                e = (NE, 0)[j] if i is None else None
                sel = d["sel"][:, e, :] if i is None else d["sel"][:, bass.ds(i * 2 + 1 + j, 1), :].rearrange("p a m -> p (a m)")
                nc.tensor.matmul(psum[:, 6 + k % 2, :], sel, d["gparts"][:, c * TW:(c + 1) * TW], start=True, stop=True)\
                    .then_inc(g_full, 1)
                if not (i is None and k == 0):
                    second((c - 1) % WCH, ((k - 1) % STEPS) // WCH, (k - 1) % 2)
                if i is None and k == WCH:
                    second.start = False

            program(T_, pe, part)
            second(WCH - 1, 1, 1)
            for c in range(WCH):
                nc.tensor.matmul(psum[:, c, :], d["b2"][:], d["gatesT"][:, c * TW:(c + 1) * TW], start=False, stop=True)\
                    .then_inc(b2_done, 1)
            pe.wait_ge(hg_ready, T_.now("step"))
            for c in range(WCH):
                pe.wait_ge(y_copied, c + 1)
                for q in range(4):
                    ins = nc.tensor.transpose(psum[:, 4 + c, q * P:(q + 1) * P], yT[:, c, q * P:(q + 1) * P], t["ident"][:])
                ins.then_inc(y_turned, 1)


_NAMES = ['x', 'ctx_768', 'L0_attn_norm_w', 'L0_attn_Wq', 'L0_attn_bq', 'L0_attn_Wk', 'L0_attn_bk', 'L0_attn_Wv',
          'L0_attn_bv', 'L0_attn_Wo', 'L0_attn_bo', 'L0_xattn_Wq', 'L0_xattn_bq', 'L0_xattn_Wkv', 'L0_xattn_bkv',
          'L0_xattn_Wo', 'L0_xattn_bo', 'L0_ffn_theta', 'L0_ffn_gamma1', 'L0_ffn_gamma2', 'L0_ffn_q_w', 'L0_ffn_q_b',
          'L0_ffn_k_w', 'L0_ffn_k_b', 'L0_ffn_v_w', 'L0_ffn_v_b', 'L0_ffn_o_w', 'L0_ffn_o_b', 'L0_ffn_router_w',
          'L0_ffn_router_b', 'L0_ffn_sh_w1', 'L0_ffn_sh_b1', 'L0_ffn_sh_w2', 'L0_ffn_sh_b2', 'L0_ffn_re_w1',
          'L0_ffn_re_b1', 'L0_ffn_re_w2', 'L0_ffn_re_b2']


def kernel(**inputs):
    import numpy as _np
    import concourse.bacc as _bacc
    from concourse import mybir as _mybir
    from concourse.bass_utils import run_bass_kernel_spmd as _run

    nc = _bacc.Bacc("TRN2", target_bir_lowering=False, num_devices=1)
    arrays, args = {}, {}
    for name in _NAMES:
        v = _np.ascontiguousarray(inputs[name])
        arrays["in_" + name] = v
        args[name] = nc.dram_tensor("in_" + name, v.shape, _mybir.dt.from_np(v.dtype), kind="ExternalInput").ap()
    out = nc.dram_tensor("out_x", (B, T, D), F32, kind="ExternalOutput").ap()
    build(nc, args, out)
    r = _run(nc, [arrays], core_ids=[0])
    return r.results[0]["out_x"]
```

```python
import concourse.bass as bass
from concourse import mybir
from contextlib import ExitStack

F32 = mybir.dt.float32
BF16 = mybir.dt.bfloat16
ACT = mybir.ActivationFunctionType
ALU = mybir.AluOpType
AX = mybir.AxisListType

P = 128
B, T, D = 8, 256, 128
QT = T // P
H, HD = 16, D // 16
G, GH = 4, 4
SKV, DC = 1601, 96
MASKED = -1.0e30

SLOTS = [(0, 0, 0), (8, 0, 1), (16, 1, 0), (24, 1, 1), (40, 0, 2), (48, 2, 0)]
TWO_ONES = 1.0019378662109375
SHIFT_ROW = 32


def build(nc, a, out):
    ctx = ExitStack()
    with ctx:
        def sb(name, shape, dt=F32):
            return ctx.enter_context(nc.sbuf_tensor(name, shape, dt))

        def sem(name):
            return ctx.enter_context(nc.semaphore(name))

        t = dict(
            x=sb("x_sb", [P, B * QT, D]),
            ident=sb("ident", [P, P]), identb=sb("identb", [P, P], BF16),
            mask_qk0=sb("mask_qk0", [P, 4, P], BF16), mask_qk1=sb("mask_qk1", [P, 2, 2 * P], BF16),
            mask_kq0=sb("mask_kq0", [P, 2, 2 * P], BF16), mask_kq1=sb("mask_kq1", [P, 2, P], BF16),
            neg_half=sb("neg_half", [P, QT]),
            qst=sb("q_stack", [P, H, T], BF16),
            kst=sb("k_stack", [P, H // 2, SKV + 1], BF16),
        )
        s = dict(stats=sb("stats", [P, QT, 6]), mv=sb("mv", [P, QT, 2]), ve=sb("ve", [P, QT]),
                 msq=sb("msq", [P, QT]), rstd=sb("rstd", [P, QT]), xn=sb("xn", [P, QT, D]),
                 xr=sb("xr", [P, QT, D]), spare=sb("spare", [P, 1]))
        psum = ctx.enter_context(nc.psum_tensor("psum", [P, 8, 512], F32))
        setup(nc, a, t, sem)
        self_attention(nc, a, t, psum, s)
        cross_attention(nc, a, t, psum, s)
        t["an_cur"] = sb("an_cur", [P, QT, D])
        an_all = sb("an_all", [P, B * QT, D])
        rotary_attention(nc, a, t, psum, s, an_all)
        d = dict(an=an_all, anT=sb("anT", [P, B * T]), gatesT=sb("gatesT", [32, B * T]), gparts=sb("gparts", [P, B * T], BF16),
                 sel=sb("sel", [P, 32, P], BF16), b1T=sb("b1T", [P, 32]), b2=sb("b2", [32, D]))
        gates_of_experts(nc, a, t, psum, d)
        experts(nc, a, t, psum, d, out)


def setup(nc, a, t, sem):
    with nc.Block() as block:
        x_loaded, cleared, idents = sem("x_loaded"), sem("cleared"), sem("idents")

        @block.sync
        def _(sp):
            sp.dma_start(t["x"][:], a["x"].rearrange("b (q p) d -> p (b q) d", p=P)).then_inc(x_loaded, 16)
            sp.wait_ge(x_loaded, 16)

        @block.vector
        def _(dve):
            for name in ("ident", "identb", "mask_qk0", "mask_qk1", "mask_kq0", "mask_kq1"):
                nc.vector.memset(t[name][:], 0.0).then_inc(cleared, 1)
            nc.vector.memset(t["neg_half"][:], -0.5)
            nc.vector.memset(t["qst"].bitcast(F32)[:], 0.0)
            nc.vector.memset(t["kst"].bitcast(F32)[:, :, 0:T], TWO_ONES)

        @block.gpsimd
        def _(pool):
            pool.wait_ge(cleared, 6)
            for name in ("ident", "identb"):
                nc.gpsimd.affine_select(out=t[name][:], in_=t[name][:], compare_op=ALU.not_equal, fill=1.0,
                                        base=0, pattern=[[-1, P]], channel_multiplier=1).then_inc(idents, 1)
            for name, part in (("mask_qk0", t["mask_qk0"][:]), ("mask_qk1", t["mask_qk1"][:, :, P:2 * P])):
                nc.gpsimd.affine_select(out=part, in_=part, compare_op=ALU.is_ge, fill=MASKED, base=0,
                                        pattern=[[0, part.shape[1]], [-1, P]], channel_multiplier=1).then_inc(idents, 1)
            for name, part in (("mask_kq0", t["mask_kq0"][:, :, 0:P]), ("mask_kq1", t["mask_kq1"][:])):
                nc.gpsimd.affine_select(out=part, in_=part, compare_op=ALU.is_ge, fill=MASKED, base=0,
                                        pattern=[[0, part.shape[1]], [1, P]], channel_multiplier=-1).then_inc(idents, 1)
            nc.gpsimd.memset(t["kst"].bitcast(F32)[:, :, T:(SKV + 1) // 2], TWO_ONES)


class Chain:

    def __init__(self, eng, sem, per, i):
        self.eng, self.sem, self.per, self.i, self.n = eng, sem, per, i, 0

    def __call__(self, ins):
        self.n += 1
        ins.then_inc(self.sem, 1)
        self.eng.wait_ge(self.sem, self.i * self.per + self.n)

    def end(self):
        assert self.n == self.per, (self.n, self.per)


def at(i, per, n):
    assert 1 <= n <= per
    return i * per + n


NORM_LINKS = 4
RMS_LINKS = 6


def layer_norm(nc, dve, link, x, s, var_ready, rstd_ready, ready_at, eps=1e-5):
    layer_stats(nc, link, x, s, var_ready, eps)
    layer_scale(nc, dve, link, x, s, rstd_ready, ready_at)


def layer_stats(nc, link, x, s, var_ready, eps=1e-5):
    for q in range(QT):
        link(nc.vector.bn_stats(s["stats"][:, q, :], x(q)))
    nc.vector.memset(s["spare"][:], 0.0)
    for q in range(QT):
        ins = nc.vector.bn_aggr(s["mv"][:, q, :], s["stats"][:, q, :])
    link(ins)
    nc.vector.tensor_scalar_add(s["ve"][:], s["mv"][:, :, 1], eps).then_inc(var_ready, 1)


def layer_scale(nc, dve, link, x, s, rstd_ready, ready_at):
    dve.wait_ge(rstd_ready, ready_at)
    for q in range(QT):
        ins = nc.vector.tensor_scalar(s["xn"][:, q, :], x(q), s["mv"][:, q, 0:1], s["rstd"][:, q:q + 1],
                                      ALU.subtract, ALU.mult)
    link(ins)


def rms_norm(nc, dve, link, s, weight, eps, var_ready, rstd_ready, ready_at, done):
    rms_stats(nc, link, s, eps, var_ready)
    rms_scale(nc, dve, link, s, weight, rstd_ready, ready_at)
    done()


def rms_stats(nc, link, s, eps, var_ready):
    for q in range(QT):
        link(nc.vector.bn_stats(s["stats"][:, q, :], s["xn"][:, q, :]))
    nc.vector.memset(s["spare"][:], 0.0)
    for q in range(QT):
        ins = nc.vector.bn_aggr(s["mv"][:, q, :], s["stats"][:, q, :])
    link(ins)
    link(nc.vector.tensor_tensor(s["msq"][:], s["mv"][:, :, 0], s["mv"][:, :, 0], ALU.mult))
    link(nc.vector.tensor_tensor(s["msq"][:], s["msq"][:], s["mv"][:, :, 1], ALU.add))
    nc.vector.tensor_scalar_add(s["ve"][:], s["msq"][:], eps).then_inc(var_ready, 1)


def rms_scale(nc, dve, link, s, weight, rstd_ready, ready_at):
    dve.wait_ge(rstd_ready, ready_at)
    for q in range(QT):
        ins = nc.vector.scalar_tensor_tensor(out=s["xr"][:, q, :], in0=s["xn"][:, q, :],
                                             scalar=s["rstd"][:, q:q + 1], in1=weight, op0=ALU.mult, op1=ALU.mult)
    link(ins)


def split3(nc, dve, link, parts, rest, src):
    link(nc.vector.tensor_copy(parts[0], src))
    link(nc.vector.tensor_tensor(rest, src, parts[0], ALU.subtract))
    link(nc.vector.tensor_copy(parts[1], rest))
    return nc.vector.tensor_tensor(parts[2], rest, parts[1], ALU.subtract)


def unit_heads(u):
    per, v = (4, u) if u < 4 else (2, u - 4)
    return [2 * k + v % 2 for k in range(per * (v // 2), per * (v // 2) + per)]


def column(h):
    return (h % 2) * (H // 2) + h // 2


def queries_of(qst, h, cols):
    return qst[:, h, cols]


def keys_of(kst, h, cols):
    return kst[:, h // 2, cols]


def stack_rows(stack, which, i, row, count, tiles):
    rows = slice(64 * i + row, 64 * i + row + count)
    if which == 0:
        return stack[rows, slice(2 * tiles.start + i, 2 * tiles.stop, 2)]
    return stack[rows, tiles]


def load_stack(sp, stack, scratch, which, n, sem):
    v = scratch.rearrange("s (t i d) n -> s i d t n", i=2, d=HD)
    for slot in SLOTS:
        row, part = slot[0], slot[1 + which]
        for i in range(2):
            sp.dma_start(stack_rows(stack, which, i, row, HD, slice(0, H // 2))[:, :, 0:n], v[part, i]).then_inc(sem, 16)


def self_attention(nc, a, t, psum, s):
    ctx = ExitStack()
    with ctx:
        def sb(name, shape, dt=F32):
            return ctx.enter_context(nc.sbuf_tensor(name, shape, dt))

        def sem(name):
            return ctx.enter_context(nc.semaphore(name))

        w_nat = sb("a_w_nat", [P, 4, D])
        w_t = sb("a_w_t", [P, 4, D])
        bqk = sb("a_bqk", [P, 2])
        rows = sb("a_rows", [P, 3, D])
        resid = sb("a_resid", [P, 2, QT, D])
        xT = sb("a_xT", [P, T])
        qk = sb("a_qk", [P, 2 * T])
        rest = sb("a_rest", [P, 2 * T])
        parts = sb("a_parts", [P, 3, 2 * T], BF16)
        v_augs = [sb("a_v_aug%d" % j, [P, QT, H, 32]) for j in range(2)]
        mneg = sb("a_mneg", [P, QT, H])
        mparts = sb("a_mparts", [H, 2, T], BF16)
        prob = sb("a_prob", [P, 2, 4 * T])
        pvs = sb("a_pvs", [P, T])
        rec = sb("a_rec", [P, QT, GH])
        attn = sb("a_attn", [P, QT, D])
        attnT = sb("a_attnT", [P, T])
        scratch = nc.dram_tensor("a_scratch", [3, P, 2 * T], BF16, kind="Internal").ap()
        ident, identb = t["ident"], t["identb"]
        qsts = [t["qst"], sb("a_q_stack1", [P, H, T], BF16)]
        ksts = [t["kst"][:, :, j * T:(j + 1) * T] for j in range(2)]
        prep = psum[:, 0, :]
        pv = psum[:, 1, 0:T]

        UNITS = 4 + 8
        STEPS = 2 * G
        NEXT_AT = {0: "qk", 1: "v"}

        w_loaded, wT_full, wT_free = sem("a_w_loaded"), sem("a_wT_full"), sem("a_wT_free")
        var_ready, rstd_ready = sem("a_var_ready"), sem("a_rstd_ready")
        xr_ready, resid_ready = sem("a_xr_ready"), sem("a_resid_ready")
        dve_own, pool_own = sem("a_dve_own"), sem("a_pool_own")
        prep_full, prep_free = sem("a_prep_full"), sem("a_prep_free")
        parts_ready, bounced, stacked = sem("a_parts_ready"), sem("a_bounced"), sem("a_stacked")
        max_full, max_done = sem("a_max_full"), sem("a_max_done")
        m0_ready, m1_ready, m_stacked = sem("a_m0_ready"), sem("a_m1_ready"), sem("a_m_stacked")
        st_full, exp_done, pv_done, pv_copied = sem("a_st_full"), sem("a_exp_done"), sem("a_pv_done"), sem("a_pv_copied")
        attn_ready, x_done = sem("a_attn_ready"), sem("a_x_done")
        ones_set, stack_cleared = sem("a_ones_set"), sem("a_stack_cleared")

        PER = {name: 2 * n for name, n in dict(
            item=3 + 1 + G + 2, norm=2, next=1, batch=1, unit=UNITS, scores=STEPS, values=STEPS, group=G,
            dve_own=NORM_LINKS + RMS_LINKS + 3 + G + 2, pool_own=QT).items()}
        block = ctx.enter_context(nc.Block())

        def program(eng, tally, begin, attend):
            begin()
            with eng.Fori(0, B // 2 - 1) as i:
                tally.enter(i)
                for j in range(2):
                    attend(i * 2 + j, j, True)
                tally.leave(B // 2 - 1)
            for j in range(2):
                attend(B - 2 + j, j, j == 0)

        @block.sync
        def _(sp):
            T_ = Tally(PER)
            for n, name in enumerate(("Wq", "Wk", "Wv", "Wo")):
                sp.dma_start(w_nat[:, n, :], a["L0_attn_" + name]).then_inc(w_loaded, 16)
            for n, name in enumerate(("bq", "bk")):
                sp.dma_start(bqk[:, n:n + 1], a["L0_attn_" + name].rearrange("(p a) -> p a", a=1)).then_inc(w_loaded, 16)
            for n, name in enumerate(("norm_w", "bv", "bo")):
                sp.dma_start(rows[:, n, :], a["L0_attn_" + name].rearrange("(a d) -> a d", a=1).to_broadcast([P, D]))\
                    .then_inc(w_loaded, 16)

            def project(j):
                sp.wait_ge(parts_ready, T_.up("next"))
                sp.dma_start(scratch.rearrange("s p n -> p s n"), parts[:]).then_inc(bounced, 16)
                sp.wait_ge(bounced, 16 * T_.now("next"))
                load_stack(sp, qsts[j], scratch[:, :, 0:T], 0, T, stacked)
                load_stack(sp, ksts[j], scratch[:, :, T:2 * T], 1, T, stacked)

            def attend(b, j, more):
                sp.wait_ge(m1_ready, T_.up("batch"))
                for par in range(2):
                    for m in range(2):
                        sp.dma_start(stack_rows(qsts[j], 0, par, SHIFT_ROW + m, 1, slice(0, H // 2)), mparts[par * 8:par * 8 + 8, m, :]).then_inc(m_stacked, 16)
                if more:
                    project(1 - j)

            sp.wait_ge(stack_cleared, 1)
            program(sp, T_, lambda: project(0), attend)

        @block.gpsimd
        def _(pool):
            T_ = Tally(PER)
            nc.gpsimd.memset(qsts[1][:], 0.0).then_inc(stack_cleared, 1)
            pool.wait_ge(w_loaded, 9 * 16)

            def project(b, j):
                for n in range(2):
                    pool.wait_ge(var_ready, T_.up("norm"))
                    nc.gpsimd.tensor_tensor(s["rstd"][:], s["ve"][:], t["neg_half"][:], ALU.pow).then_inc(rstd_ready, 1)
                pool.wait_ge(xr_ready, T_.up("next"))
                for q in range(QT):
                    nc.gpsimd.tensor_tensor(resid[:, j, q, :], s["xr"][:, q, :], rows[:, 2, :], ALU.add).then_inc(pool_own, 1)
                    pool.wait_ge(pool_own, T_.up("pool_own"))
                nc.gpsimd.tensor_tensor(resid[:, j], resid[:, j], t["x"][:, bass.ds(b * QT, QT), :], ALU.add)\
                    .then_inc(resid_ready, 1)

            def attend(b, j, more):
                if more:
                    project(b + 1, 1 - j)

            program(pool, T_, lambda: project(0, 0), attend)

        @block.vector
        def _(dve):
            T_ = Tally(PER)
            for j in range(2):
                nc.vector.memset(v_augs[j][:], 1.0).then_inc(ones_set, 1)
            dve.wait_ge(w_loaded, 9 * 16)

            def own(ins):
                ins.then_inc(dve_own, 1)
                dve.wait_ge(dve_own, T_.up("dve_own"))

            def norm(b):
                T_.up("norm")
                layer_norm(nc, dve, own, lambda q: t["x"][:, bass.ds(b * QT + q, 1), :].rearrange("p a d -> p (a d)"),
                           s, var_ready, rstd_ready, T_.now("norm"))
                T_.up("norm")
                rms_norm(nc, dve, own, s, rows[:, 0, :], 1e-6, var_ready, rstd_ready, T_.now("norm"),
                         lambda: dve.sem_inc(xr_ready, 1))

            def item(kind, g=0):
                n = T_.up("item")
                if kind == "qk":
                    dve.wait_ge(prep_free, n)
                    split3(nc, dve, own, [parts[:, n, :] for n in range(3)], rest[:], qk[:]).then_inc(parts_ready, 1)
                elif kind == "m":
                    dve.wait_ge(m0_ready, T_.up("batch"))
                    nc.vector.tensor_tensor(mparts[:, 1, :], prep[0:H, 0:T], mparts[:, 0, :], ALU.subtract)\
                        .then_inc(m1_ready, 1)
                    dve.wait_ge(m1_ready, T_.now("batch"))
                    dve.sem_inc(prep_free, 1)
                elif kind == "pv":
                    dve.wait_ge(prep_full, n)
                    o = prep[:, 0:2 * P].rearrange("p (q h c) -> p q h c", q=QT, h=GH)
                    own(nc.vector.reciprocal(rec[:], o[:, :, :, HD]))
                    nc.vector.tensor_tensor(
                        attn[:, :, 32 * g:32 * g + 32].rearrange("p q (h d) -> p q h d", h=GH), o[:, :, :, 0:HD],
                        rec[:].rearrange("p q (h a) -> p q h a", a=1).to_broadcast([P, QT, GH, HD]), ALU.mult)\
                        .then_inc(prep_free, 1)
                    if g == G - 1:
                        dve.wait_ge(prep_free, n)
                        for q in range(QT):
                            own(nc.vector.tensor_tensor(attn[:, q, :], attn[:, q, :], rows[:, 1, :], ALU.add))
                        dve.sem_inc(attn_ready, 1)

            def begin():
                norm(0)
                for kind in ("x", "qk", "v"):
                    item(kind)

            def attend(b, j, more):
                for u in range(UNITS):
                    dve.wait_ge(max_full, T_.up("unit"))
                    bank = psum[:, 4 + u % 4, :]
                    heads = unit_heads(u)
                    c = column(heads[0])
                    dst = mneg[:, 0 if u < 4 else 1, c:c + len(heads)]
                    src = bank.rearrange("p (h k) -> p h k", h=len(heads))
                    nc.vector.tensor_reduce(out=dst, in_=src, axis=AX.X, op=ALU.max, negate=True).then_inc(max_done, 1)
                item("m")
                if more:
                    norm(b + 1)
                    item("x")
                for n in range(STEPS):
                    if more and n in NEXT_AT:
                        item(NEXT_AT[n])
                    if n >= 3 and n % 2 == 1:
                        item("pv", (n - 3) // 2)
                item("pv", G - 1)
                item("attnT")
                n = T_.up("item")
                dve.wait_ge(resid_ready, T_.now("batch"))
                dve.wait_ge(prep_full, n)
                nc.vector.tensor_tensor(t["x"][:, bass.ds(b * QT, QT), :],
                                        prep[:, 0:2 * P].rearrange("p (q d) -> p q d", q=QT), resid[:, j], ALU.add)\
                    .then_inc(x_done, 1)
                dve.wait_ge(x_done, T_.now("batch"))
                dve.sem_inc(prep_free, 1)

            program(dve, T_, begin, attend)

        @block.scalar
        def _(act):
            T_ = Tally(PER)
            act.wait_ge(wT_full, 1)
            nc.scalar.activation(w_t[:].rearrange("p n d -> p (n d)"), prep, ACT.Copy).then_inc(wT_free, 1)
            act.wait_ge(ones_set, 2)

            def item(kind, j=0):
                n = T_.up("item")
                if kind == "x":
                    act.wait_ge(prep_full, n)
                    nc.scalar.activation(xT[:], prep[:, 0:T], ACT.Copy).then_inc(prep_free, 1)
                elif kind == "qk":
                    act.wait_ge(prep_full, n)
                    nc.scalar.activation(qk[:, 0:T], prep[:, 0:T], ACT.Identity, bias=bqk[:, 0:1])
                    nc.scalar.activation(qk[:, T:2 * T], prep[:, T:2 * T], ACT.Identity, bias=bqk[:, 1:2]).then_inc(prep_free, 1)
                elif kind == "v":
                    act.wait_ge(prep_full, n)
                    nc.scalar.activation(v_augs[j][:, :, :, 0:HD],
                                         prep[:, 0:2 * D].rearrange("p (q h d) -> p q h d", q=QT, h=H), ACT.Copy)\
                        .then_inc(prep_free, 1)
                elif kind == "m":
                    act.wait_ge(prep_full, n)
                    nc.scalar.activation(mparts[:, 0, :], prep[0:H, 0:T], ACT.Copy).then_inc(m0_ready, 1)
                elif kind == "attnT":
                    act.wait_ge(prep_full, n)
                    nc.scalar.activation(attnT[:], prep[:, 0:T], ACT.Copy).then_inc(prep_free, 1)

            def begin():
                for kind in ("x", "qk", "v"):
                    item(kind, 0)

            def copy_pv():
                act.wait_ge(pv_done, T_.up("values", 2))
                wait(act, prep_full, T_.now("item"))
                nc.scalar.activation(pvs[:], pv, ACT.Copy).then_inc(pv_copied, 1)

            def attend(b, j, more):
                item("m")
                if more:
                    item("x")
                for n in range(STEPS):
                    act.wait_ge(st_full, T_.up("scores"))
                    w = 2 * T if n % 2 == 0 else T
                    nc.scalar.activation(prob[:, n % 2, 0:2 * w].rearrange("p (a c) -> p a c", a=2),
                                         psum[:, 4 + 2 * (n % 2):6 + 2 * (n % 2), 0:w], ACT.Exp, scale=HD ** -0.5)\
                        .then_inc(exp_done, 1)
                    if n >= 2 and n % 2 == 0:
                        copy_pv()
                    if more and n in NEXT_AT:
                        item(NEXT_AT[n], 1 - j)
                    if n >= 3 and n % 2 == 1:
                        item("pv")
                copy_pv()
                item("pv")
                item("attnT")
                item("out")

            program(act, T_, begin, attend)

        @block.tensor
        def _(pe):
            T_ = Tally(PER)
            pe.wait_ge(w_loaded, 9 * 16)
            for n in range(4):
                last = nc.tensor.transpose(prep[:, n * D:(n + 1) * D], w_nat[:, n, :], ident[:])
            last.then_inc(wT_full, 1)
            pe.wait_ge(wT_free, 1)

            def item(kind):
                T_.up("item")
                wait(pe, prep_free, T_.now("item", 1))
                if kind == "x":
                    pe.wait_ge(xr_ready, T_.up("next"))
                    for q in range(QT):
                        last = nc.tensor.transpose(prep[:, q * P:(q + 1) * P], s["xr"][:, q, :], ident[:])
                elif kind == "qk":
                    for n in range(2):
                        last = nc.tensor.matmul(prep[:, n * T:(n + 1) * T], w_t[:, n, :], xT[:], start=True, stop=True)
                elif kind == "v":
                    for q in range(QT):
                        last = nc.tensor.matmul(prep[:, q * D:(q + 1) * D], xT[:, q * P:(q + 1) * P], w_t[:, 2, :],
                                                start=True, stop=True)
                elif kind == "m":
                    pe.wait_ge(max_done, T_.now("unit"))
                    for q in range(QT):
                        last = nc.tensor.transpose(prep[0:H, q * P:(q + 1) * P], mneg[:, q, :], ident[:])
                elif kind == "pv":
                    pe.wait_ge(pv_copied, T_.up("group"))
                    for q in range(QT):
                        last = nc.tensor.transpose(prep[:, q * P:(q + 1) * P], pvs[:, q * P:(q + 1) * P], ident[:])
                elif kind == "attnT":
                    pe.wait_ge(attn_ready, T_.now("batch"))
                    for q in range(QT):
                        last = nc.tensor.transpose(prep[:, q * P:(q + 1) * P], attn[:, q, :], ident[:])
                elif kind == "out":
                    for q in range(QT):
                        last = nc.tensor.matmul(prep[:, q * D:(q + 1) * D], attnT[:, q * P:(q + 1) * P], w_t[:, 3, :],
                                                start=True, stop=True)
                last.then_inc(prep_full, 1)

            def scores_t(n, j):
                g, kt = n // 2, n % 2
                T_.up("scores")
                if n >= 2:
                    pe.wait_ge(exp_done, T_.now("scores", 2))
                w = T - kt * P
                for par in range(2):
                    nc.tensor.matmul(psum[:, 4 + 2 * (n % 2) + par, 0:2 * w], identb[:],
                                     t["mask_kq%d" % kt][:].rearrange("p h q -> p (h q)"), start=True, stop=False)
                for hh in range(GH):
                    h = g * GH + hh
                    dst = psum[:, 4 + 2 * (n % 2) + hh % 2, (hh // 2) * w:(hh // 2) * w + w]
                    last = nc.tensor.matmul(dst, keys_of(ksts[j], h, slice(kt * P, kt * P + P)),
                                            queries_of(qsts[j], h, slice(kt * P, T)), start=False, stop=(hh >= 2))
                last.then_inc(st_full, 1)

            def values(n, j):
                g, kt = n // 2, n % 2
                pe.wait_ge(exp_done, T_.up("values"))
                if kt == 0 and n > 0:
                    pe.wait_ge(pv_copied, T_.now("group", -1))
                w = T - kt * P
                for hh in range(GH):
                    c = (hh % 2) * 2 * w + (hh // 2) * w
                    last = nc.tensor.matmul(pv[32 * hh:32 * hh + 32, kt * P:T], v_augs[j][:, kt, g * GH + hh, :],
                                            prob[:, n % 2, c:c + w], start=(kt == 0), stop=(kt == 1),
                                            tile_position=(0, 32 * hh))
                last.then_inc(pv_done, 1)

            def begin():
                for kind in ("x", "qk", "v"):
                    item(kind)

            def attend(b, j, more):
                pe.wait_ge(stacked, T_.up("batch") * 24 * 16)
                for u in range(UNITS):
                    T_.up("unit")
                    if u >= 4:
                        pe.wait_ge(max_done, T_.now("unit", 4))
                    bank = psum[:, 4 + u % 4, :]
                    q, keys, heads, mask = (0, P, unit_heads(u), "mask_qk0") if u < 4 else (1, 2 * P, unit_heads(u), "mask_qk1")
                    nc.tensor.matmul(bank, identb[:], t[mask][:].rearrange("p h k -> p (h k)"), start=True, stop=False)
                    for n, h in enumerate(heads):
                        last = nc.tensor.matmul(bank[:, n * keys:(n + 1) * keys], queries_of(qsts[j], h, slice(q * P, q * P + P)),
                                                keys_of(ksts[j], h, slice(0, keys)), start=False, stop=(n == len(heads) - 1))
                    last.then_inc(max_full, 1)
                item("m")
                if more:
                    item("x")
                pe.wait_ge(m_stacked, T_.now("batch") * 4 * 16)
                for n in range(STEPS):
                    scores_t(n, j)
                    if n >= 1:
                        values(n - 1, j)
                    if more and n in NEXT_AT:
                        item(NEXT_AT[n])
                    if n >= 3 and n % 2 == 1:
                        item("pv")
                values(STEPS - 1, j)
                item("pv")
                item("attnT")
                item("out")

            program(pe, T_, begin, attend)


class Tally:

    def __init__(self, per):
        self.n, self.per, self.i = dict.fromkeys(per, 0), per, None

    def up(self, name, by=1):
        self.n[name] += by
        return self.now(name)

    def now(self, name, back=0):
        n = self.n[name] - back
        return n if self.i is None else self.i * self.per[name] + n

    def enter(self, i):
        self.i, self.start = i, dict(self.n)

    def leave(self, rounds):
        for name, n in self.n.items():
            assert n - self.start[name] in (0, self.per[name]), (name, n - self.start[name], self.per[name])
            if n != self.start[name]:
                self.n[name] = self.start[name] + rounds * self.per[name]
        self.i = None


def wait(eng, sem, value):
    if not isinstance(value, int) or value > 0:
        eng.wait_ge(sem, value)


KT = -(-SKV // P)
CHUNKS = [(c * SKV // 4, (c + 1) * SKV // 4) for c in range(4)]
CW = max(e - s for s, e in CHUNKS)
UNITS_B = QT * GH * 4
M_STEP = 9


def tile_rows(kt):
    return min(P, SKV - kt * P)


def units_of_step(n):
    head = 22
    if n < M_STEP:
        lo, k = UNITS_B - head, M_STEP
        return [lo + u for u in range(n * head // k, (n + 1) * head // k)]
    k, n, total = KT - M_STEP, n - M_STEP, UNITS_B - head
    return list(range(n * total // k, (n + 1) * total // k))


PREP_AT = {(0, 0): ("ctx", 0), (0, 1): ("k", 0), (0, 2): ("pv", 0), (0, 3): ("ctx", 1), (0, 4): ("k", 1),
           (0, 5): ("ctx", 2), (0, 6): ("k", 2), (0, 7): ("ctx", 3), (0, 8): ("k", 3), (0, 9): ("m", 2),
           (0, 10): ("x", 0), (0, 11): ("q", 0), (0, 12): ("v", 0), (1, 0): ("v", 1), (1, 1): ("v", 2),
           (1, 2): ("pv", 1), (1, 3): ("v", 3), (1, 9): ("m", 3), (2, 2): ("pv", 2), (2, 9): ("m", 0),
           (3, 2): ("pv", 3), (3, 4): ("attnT", 0), (3, 6): ("out", 0), (3, 9): ("m", 1)}
NEXT_BATCH = ("ctx", "k", "x", "q", "v")


def prep_item(r, n, first=False, last=False):
    item = PREP_AT.get((r, n))
    if item is None or (last and (item[0] in NEXT_BATCH or item == ("m", 0))):
        return None
    if first and item[0] in ("pv", "attnT", "out"):
        return None
    return item


def column4(hh):
    return hh % 2 * 2 + hh // 2


PROLOGUE_ITEMS = [("ctx", 0), ("k", 0), ("ctx", 1), ("k", 1), ("ctx", 2), ("k", 2), ("ctx", 3), ("k", 3),
                  ("x", 0), ("q", 0), ("v", 0), ("v", 1), ("v", 2), ("v", 3), ("m", 0)]


def units_left(r, n, last):
    return not (last and (r == 2 or (r == 1 and n >= M_STEP)))


def cross_attention(nc, a, t, psum, s):
    ctx = ExitStack()
    with ctx:
        def sb(name, shape, dt=F32):
            return ctx.enter_context(nc.sbuf_tensor(name, shape, dt))

        def sem(name):
            return ctx.enter_context(nc.semaphore(name))

        wq, wo = sb("b_wq", [D, D]), sb("b_wo", [D, D])
        wkv = sb("b_wkv", [DC, 2 * D])
        bq, bk = sb("b_bq", [P, 1]), sb("b_bk", [P, 1])
        rows = sb("b_rows", [P, 2, D])
        resid = sb("b_resid", [P, QT, D])
        xT = sb("b_xT", [P, T])
        qf, qrest = sb("b_qf", [P, T]), sb("b_qrest", [P, T])
        qparts = sb("b_qparts", [P, 3, T], BF16)
        ctx_sb = sb("b_ctx", [P, KT, DC])
        ctxT = sb("b_ctxT", [DC, SKV])
        kf, krest = sb("b_kf", [P, 2, CW]), sb("b_krest", [P, 2, CW])
        zeros = sb("b_zeros", [P, CW])
        kparts = sb("b_kparts", [P, 3, SKV], BF16)
        v_new = sb("b_v_new", [P, KT, D])
        v_aug = sb("b_v_aug", [P, KT, H, 32])
        chunk_max = sb("b_chunk_max", [P, 2, QT, GH, 4])
        mneg = sb("b_mneg", [P, QT, GH])
        mparts = sb("b_mparts", [GH, 2, T], BF16)
        prob = sb("b_prob", [P, 2, GH * T])
        pvs = sb("b_pvs", [P, T])
        rec = sb("b_rec", [P, QT, GH])
        attn = sb("b_attn", [P, QT, D])
        attnT = sb("b_attnT", [P, T])
        q_scr = nc.dram_tensor("b_q_scratch", [3, P, T], BF16, kind="Internal").ap()
        k_scr = nc.dram_tensor("b_k_scratch", [3, P, SKV], BF16, kind="Internal").ap()
        qst, kst, ident = t["qst"], t["kst"], t["ident"]
        prep, pv = psum[:, 0, :], psum[:, 1, 0:T]

        w_loaded, ones_set = sem("b_w_loaded"), sem("b_ones_set")
        var_ready, rstd_ready, xn_ready = sem("b_var_ready"), sem("b_rstd_ready"), sem("b_xn_ready")
        dve_own, pool_own = sem("b_dve_own"), sem("b_pool_own")
        prep_full, prep_free = sem("b_prep_full"), sem("b_prep_free")
        ctx_loaded, ctx_used = sem("b_ctx_loaded"), sem("b_ctx_used")
        kf_ready, k_split = sem("b_kf_ready"), sem("b_k_split")
        qf_ready, q_split = sem("b_qf_ready"), sem("b_q_split")
        q_bounced, k_bounced, stacked = sem("b_q_bounced"), sem("b_k_bounced"), sem("b_stacked")
        v_evacuated, v_placed = sem("b_v_evacuated"), sem("b_v_placed")
        max_full, max_done, mneg_ready = sem("b_max_full"), sem("b_max_done"), sem("b_mneg_ready")
        m0_ready, m1_ready, m_stacked = sem("b_m0_ready"), sem("b_m1_ready"), sem("b_m_stacked")
        st_full, exp_done, pv_done, pv_copied = sem("b_st_full"), sem("b_exp_done"), sem("b_pv_done"), sem("b_pv_copied")
        attn_ready, resid_ready, x_done = sem("b_attn_ready"), sem("b_resid_ready"), sem("b_x_done")

        passed = sem("b_passed")
        PER = dict(item=len(PREP_AT), step=4 * KT, unit=4 * UNITS_B, group=4, batch=1, kchunk=4, half=2,
                   stacked=48 * 16, m_stacked=4 * 64, dma=16, ctx=32, own_dve=NORM_LINKS + G + 2,
                   own_pool=4 * 2 + 2, mneg=4, vchunk=4, placed=2, out=1)
        N_W = 7
        block = ctx.enter_context(nc.Block())

        def parts_of_program(eng, tally, prologue, part):
            prologue()
            part(-1, 3, first=True, last=False)
            with eng.Fori(0, B - 2) as i:
                tally.enter(i)
                for r in range(4):
                    part(i, r, first=False, last=False)
                tally.leave(B - 2)
            for r in range(4):
                part(B - 2, r, first=False, last=False)
            for r in range(3):
                part(B - 1, r, first=False, last=True)

        @block.sync
        def _(sp):
            T_ = Tally(PER)
            for dst, src in ((wq[:], a["L0_xattn_Wq"]), (wo[:], a["L0_xattn_Wo"]), (wkv[:], a["L0_xattn_Wkv"]),
                             (bq[:], a["L0_xattn_bq"].rearrange("(p a) -> p a", a=1)),
                             (bk[:], a["L0_xattn_bkv"][0:D].rearrange("(p a) -> p a", a=1)),
                             (rows[:, 0, :], a["L0_xattn_bkv"][D:2 * D].rearrange("(a d) -> a d", a=1).to_broadcast([P, D])),
                             (rows[:, 1, :], a["L0_xattn_bo"].rearrange("(a d) -> a d", a=1).to_broadcast([P, D]))):
                sp.dma_start(dst, src).then_inc(w_loaded, 16)

            def load_ctx(b):
                wait(sp, ctx_used, T_.now("batch"))
                sp.sem_inc(passed, 1)
                src = a["ctx_768"][b] if isinstance(b, int) else a["ctx_768"][bass.ds(b, 1)].rearrange("a s d -> (a s) d")
                sp.dma_start(ctx_sb[:, 0:KT - 1, :], src[0:(KT - 1) * P].rearrange("(k p) d -> p k d", p=P)).then_inc(ctx_loaded, 16)
                sp.dma_start(ctx_sb[0:tile_rows(KT - 1), KT - 1, :], src[(KT - 1) * P:SKV]).then_inc(ctx_loaded, 16)

            def bounce():
                wait(sp, stacked, T_.now("stacked"))
                sp.sem_inc(passed, 1)
                sp.wait_ge(k_split, T_.up("kchunk", 4))
                sp.dma_start(k_scr.rearrange("s p n -> p s n"), kparts[:]).then_inc(k_bounced, 16)
                sp.wait_ge(q_split, T_.up("batch"))
                sp.dma_start(q_scr.rearrange("s p n -> p s n"), qparts[:]).then_inc(q_bounced, 16)
                sp.wait_ge(q_bounced, T_.up("dma", 16))
                sp.wait_ge(k_bounced, T_.now("dma"))

            def load_half(half):
                T_.up("stacked", 24 * 16)
                for stack, scr, which, n in ((qst, q_scr, 0, T), (kst, k_scr, 1, SKV)):
                    v = scr.rearrange("s (t i d) n -> s i d t n", i=2, d=HD)
                    for slot in SLOTS:
                        row, part = slot[0], slot[1 + which]
                        for i in range(2):
                            sp.dma_start(stack_rows(stack, which, i, row, HD, slice(4 * half, 4 * half + 4))[:, :, 0:n],
                                         v[part, i, :, 4 * half:4 * half + 4]).then_inc(stacked, 16)

            def store_m(g):
                sp.wait_ge(m1_ready, T_.up("group"))
                for par in range(2):
                    for m in range(2):
                        sp.dma_start(stack_rows(qst, 0, par, SHIFT_ROW + m, 1, slice(2 * g, 2 * g + 2)), mparts[2 * par:2 * par + 2, m, :])\
                            .then_inc(m_stacked, 16)

            def prologue():
                load_ctx(0)
                bounce()
                load_half(0)
                load_half(1)
                store_m(0)

            def part(i, r, first, last):
                if r == 3:
                    if not first:
                        sp.wait_ge(st_full, T_.now("step"))
                        load_half(1)
                    if not isinstance(i, int) or i + 2 < B:
                        load_ctx(i + 2)
                if prep_item(r, M_STEP, first, last):
                    store_m(PREP_AT[(r, M_STEP)][1])
                T_.up("step", KT)
                if r == 0 and not last:
                    bounce()
                    sp.wait_ge(st_full, T_.now("step"))
                    load_half(0)

            parts_of_program(sp, T_, prologue, part)

        @block.gpsimd
        def _(pool):
            T_ = Tally(PER)

            def own(ins):
                ins.then_inc(pool_own, 1)
                pool.wait_ge(pool_own, T_.up("own_pool"))

            def power():
                pool.wait_ge(var_ready, T_.up("batch"))
                nc.gpsimd.tensor_tensor(s["rstd"][:], s["ve"][:], t["neg_half"][:], ALU.pow).then_inc(rstd_ready, 1)

            def split_k():
                wait(pool, k_bounced, T_.now("dma"))
                for c, (lo, hi) in enumerate(CHUNKS):
                    n = T_.up("kchunk")
                    pool.wait_ge(kf_ready, n)
                    own(nc.gpsimd.tensor_tensor(krest[:, c % 2, 0:hi - lo], kf[:, c % 2, 0:hi - lo], kparts[:, 0, lo:hi], ALU.subtract))
                    own(nc.gpsimd.tensor_tensor(kparts[:, 1, lo:hi], krest[:, c % 2, 0:hi - lo], zeros[:, 0:hi - lo], ALU.add))
                    nc.gpsimd.tensor_tensor(kparts[:, 2, lo:hi], krest[:, c % 2, 0:hi - lo], kparts[:, 1, lo:hi], ALU.subtract)\
                        .then_inc(k_split, 1)

            def split_q():
                wait(pool, q_bounced, T_.now("dma"))
                T_.up("dma", 16)
                pool.wait_ge(qf_ready, T_.now("batch"))
                own(nc.gpsimd.tensor_tensor(qrest[:], qf[:], qparts[:, 0, :], ALU.subtract))
                own(nc.gpsimd.tensor_tensor(qparts[:, 1, :], qrest[:], zeros[:, 0:T], ALU.add))
                nc.gpsimd.tensor_tensor(qparts[:, 2, :], qrest[:], qparts[:, 1, :], ALU.subtract).then_inc(q_split, 1)

            def place_v(half):
                pool.wait_ge(v_evacuated, T_.now("kchunk"))
                wait(pool, pv_done, T_.now("step"))
                pool.sem_inc(passed, 1)
                c = half * H // 2
                for lo, hi, n in ((0, KT - 1, P), (KT - 1, KT, tile_rows(KT - 1))):
                    ins = nc.gpsimd.tensor_copy(v_aug[0:n, lo:hi, c:c + H // 2, 0:HD],
                                                v_new[0:n, lo:hi, c * HD:(c + H // 2) * HD].rearrange("p k (h d) -> p k h d", h=H // 2))
                ins.then_inc(v_placed, 1)

            def residual(b):
                wait(pool, x_done, T_.now("out"))
                T_.up("out")
                for q in range(QT):
                    ins = nc.gpsimd.tensor_tensor(
                        resid[:, q, :], t["x"][:, bass.ds(b * QT + q, 1), :].rearrange("p a d -> p (a d)"), rows[:, 1, :], ALU.add)
                ins.then_inc(resid_ready, 1)

            def prologue():
                pool.wait_ge(w_loaded, N_W * 16)
                pool.wait_ge(ones_set, 1)
                power()
                split_k()
                split_q()
                place_v(0)
                place_v(1)

            def part(i, r, first, last):
                if r == 0 and not last:
                    power()
                    split_k()
                    split_q()
                T_.up("step", KT)
                if r == 1 and not last:
                    T_.up("step", -KT)
                    place_v(0)
                    T_.up("step", KT)
                if r == 2:
                    residual(B - 1 if last else i)
                    if not last:
                        place_v(1)

            parts_of_program(pool, T_, prologue, part)

        @block.vector
        def _(dve):
            T_ = Tally(PER)

            def own(ins):
                ins.then_inc(dve_own, 1)
                dve.wait_ge(dve_own, T_.up("own_dve"))

            def tile_of(b):
                return lambda q: t["x"][:, bass.ds(b * QT + q, 1), :].rearrange("p a d -> p (a d)")

            def norm_stats(b):
                T_.up("batch")
                layer_stats(nc, own, tile_of(b), s, var_ready)

            def norm_scale(b):
                layer_scale(nc, dve, own, tile_of(b), s, rstd_ready, T_.now("batch"))
                dve.sem_inc(xn_ready, 1)

            def unit(u):
                v = T_.up("unit")
                q, c, hh = u // (4 * GH), u // GH % 4, u % GH
                half = (T_.n["unit"] - 1) // UNITS_B % 2
                w = CHUNKS[c][1] - CHUNKS[c][0]
                dve.wait_ge(max_full, v)
                nc.vector.tensor_reduce(out=chunk_max[:, half, q, column4(hh), c:c + 1], in_=psum[:, 2 + u % 2, 0:w],
                                        axis=AX.X, op=ALU.max).then_inc(max_done, 1)
                if u == UNITS_B - 1:
                    dve.wait_ge(max_done, T_.now("unit"))
                    nc.vector.tensor_reduce(out=mneg[:], in_=chunk_max[:, half], axis=AX.X, op=ALU.max, negate=True)\
                        .then_inc(mneg_ready, 1)

            def item(kind, g, b):
                n = T_.up("item")
                if kind == "m":
                    dve.wait_ge(m0_ready, T_.up("group"))
                    nc.vector.tensor_tensor(mparts[:, 1, :], prep[0:GH, 0:T], mparts[:, 0, :], ALU.subtract)\
                        .then_inc(m1_ready, 1)
                    dve.wait_ge(m1_ready, T_.now("group"))
                    dve.sem_inc(prep_free, 1)
                elif kind == "pv":
                    dve.wait_ge(prep_full, n)
                    o = prep[:, 0:2 * P].rearrange("p (q h c) -> p q h c", q=QT, h=GH)
                    own(nc.vector.reciprocal(rec[:], o[:, :, :, HD]))
                    nc.vector.tensor_tensor(
                        attn[:, :, 32 * g:32 * g + 32].rearrange("p q (h d) -> p q h d", h=GH), o[:, :, :, 0:HD],
                        rec[:].rearrange("p q (h a) -> p q h a", a=1).to_broadcast([P, QT, GH, HD]), ALU.mult)\
                        .then_inc(prep_free, 1)
                    if g == G - 1:
                        dve.wait_ge(prep_free, n)
                        own(nc.vector.tensor_tensor(attn[:, 0, :], attn[:, 0, :], rows[:, 0, :], ALU.add))
                        own(nc.vector.tensor_tensor(attn[:, 1, :], attn[:, 1, :], rows[:, 0, :], ALU.add))
                        dve.sem_inc(attn_ready, 1)
                elif kind == "out":
                    dve.wait_ge(resid_ready, T_.up("out"))
                    dve.wait_ge(prep_full, n)
                    nc.vector.tensor_tensor(t["x"][:, bass.ds(b * QT, QT), :],
                                            prep[:, 0:2 * P].rearrange("p (q d) -> p q d", q=QT), resid[:], ALU.add)\
                        .then_inc(x_done, 1)
                    dve.wait_ge(x_done, T_.now("out"))
                    dve.sem_inc(prep_free, 1)

            def prologue():
                nc.vector.memset(zeros[:], 0.0)
                nc.vector.memset(v_aug[:], 1.0).then_inc(ones_set, 1)
                norm_stats(0)
                norm_scale(0)
                T_.up("item", 14)
                for u in range(UNITS_B):
                    unit(u)
                item("m", 0, 0)
                for u in range(UNITS_B - 22):
                    unit(u)

            def part(i, r, first, last):
                b = B - 1 if last else i
                for n in range(KT):
                    if r == 0 and n == 0 and not last:
                        norm_stats(i + 1)
                    if r == 0 and n == 2 and not last:
                        norm_scale(i + 1)
                    if units_left(r, n, last):
                        for u in units_of_step(n):
                            unit(u)
                    it = prep_item(r, n, first, last)
                    if it:
                        item(*it, b)

            parts_of_program(dve, T_, prologue, part)
            for it in (("pv", 3), ("attnT", 0), ("out", 0)):
                item(*it, B - 1)

        @block.scalar
        def _(act):
            T_ = Tally(PER)

            def item(kind, g):
                n = T_.up("item")
                if kind in ("pv", "out"):
                    return
                act.wait_ge(prep_full, n)
                if kind == "ctx":
                    cols = min(4 * P, SKV - 4 * P * g)
                    nc.scalar.activation(ctxT[:, 4 * P * g:4 * P * g + cols], prep[0:DC, 0:cols], ACT.Copy).then_inc(prep_free, 1)
                elif kind == "k":
                    lo, hi = CHUNKS[g]
                    v = T_.up("kchunk")
                    wait(act, k_split, T_.now("kchunk", 2))
                    wait(act, k_bounced, T_.now("dma"))
                    nc.scalar.activation(kf[:, g % 2, 0:hi - lo], prep[:, 0:hi - lo], ACT.Identity, bias=bk[:])
                    nc.scalar.activation(kparts[:, 0, lo:hi], prep[:, 0:hi - lo], ACT.Identity, bias=bk[:]).then_inc(kf_ready, 1)
                    act.wait_ge(kf_ready, v)
                    act.sem_inc(prep_free, 1)
                elif kind == "x":
                    nc.scalar.activation(xT[:], prep[:, 0:T], ACT.Copy).then_inc(prep_free, 1)
                elif kind == "q":
                    v = T_.up("batch")
                    wait(act, q_bounced, T_.now("dma"))
                    T_.up("dma", 16)
                    nc.scalar.activation(qf[:], prep[:, 0:T], ACT.Identity, bias=bq[:])
                    nc.scalar.activation(qparts[:, 0, :], prep[:, 0:T], ACT.Identity, bias=bq[:]).then_inc(qf_ready, 1)
                    act.wait_ge(qf_ready, v)
                    act.sem_inc(prep_free, 1)
                elif kind == "v":
                    wait(act, v_placed, T_.now("half"))
                    if g == 3:
                        T_.up("half", 2)
                        nc.scalar.activation(v_new[0:tile_rows(KT - 1), KT - 1, :], prep[0:tile_rows(KT - 1), 0:D], ACT.Copy)\
                            .then_inc(v_evacuated, 1)
                    else:
                        nc.scalar.activation(v_new[:, 4 * g:4 * g + 4, :], prep[:, 0:4 * D].rearrange("p (k d) -> p k d", k=4),
                                             ACT.Copy).then_inc(v_evacuated, 1)
                    act.wait_ge(v_evacuated, T_.up("vchunk"))
                    act.sem_inc(prep_free, 1)
                elif kind == "m":
                    nc.scalar.activation(mparts[:, 0, :], prep[0:GH, 0:T], ACT.Copy).then_inc(m0_ready, 1)
                elif kind == "attnT":
                    nc.scalar.activation(attnT[:], prep[:, 0:T], ACT.Copy).then_inc(prep_free, 1)

            def copy_pv():
                act.wait_ge(pv_done, T_.now("step"))
                nc.scalar.activation(pvs[:], pv, ACT.Copy).then_inc(pv_copied, 1)

            def prologue():
                act.wait_ge(w_loaded, N_W * 16)
                for it in PROLOGUE_ITEMS:
                    item(*it)

            def part(i, r, first, last):
                for n in range(KT):
                    v = T_.up("step")
                    act.wait_ge(st_full, v)
                    wait(act, pv_done, T_.now("step", 2))
                    k, buf = tile_rows(n), (T_.n["step"] - 1) % 2
                    nc.scalar.activation(prob[0:k, buf, :].rearrange("p (a c) -> p a c", a=2),
                                         psum[0:k, 4 + 2 * buf:6 + 2 * buf, :], ACT.Exp, scale=HD ** -0.5)\
                        .then_inc(exp_done, 1)
                    if n == 0 and not first:
                        T_.up("step", -1)
                        copy_pv()
                        T_.up("step")
                    it = prep_item(r, n, first, last)
                    if it:
                        item(*it)

            parts_of_program(act, T_, prologue, part)
            copy_pv()
            for it in (("pv", 3), ("attnT", 0), ("out", 0)):
                item(*it)

        @block.tensor
        def _(pe):
            T_ = Tally(PER)
            pending = []

            def item(kind, g):
                n = T_.up("item")
                wait(pe, prep_free, T_.now("item", 1))
                if kind == "ctx":
                    if g == 0:
                        pe.wait_ge(ctx_loaded, T_.up("ctx", 32))
                    for j, kt in enumerate(range(4 * g, min(4 * g + 4, KT))):
                        k = tile_rows(kt)
                        last = nc.tensor.transpose(prep[0:DC, j * P:j * P + k], ctx_sb[0:k, kt, :], ident[0:k, 0:k])
                    last.then_inc(prep_full, 1)
                    if g == 3:
                        pe.wait_ge(prep_full, n)
                        pe.sem_inc(ctx_used, 1)
                elif kind == "k":
                    lo, hi = CHUNKS[g]
                    nc.tensor.matmul(prep[:, 0:hi - lo], wkv[:, 0:D], ctxT[:, lo:hi], start=True, stop=True).then_inc(prep_full, 1)
                elif kind == "x":
                    pe.wait_ge(xn_ready, T_.up("batch"))
                    for q in range(QT):
                        last = nc.tensor.transpose(prep[:, q * P:(q + 1) * P], s["xn"][:, q, :], ident[:])
                    last.then_inc(prep_full, 1)
                elif kind == "q":
                    nc.tensor.matmul(prep[:, 0:T], wq[:], xT[:], start=True, stop=True).then_inc(prep_full, 1)
                elif kind == "v":
                    for j, kt in enumerate(range(4 * g, min(4 * g + 4, KT))):
                        k = tile_rows(kt)
                        last = nc.tensor.matmul(prep[0:k, j * D:(j + 1) * D], ctxT[:, kt * P:kt * P + k], wkv[:, D:2 * D],
                                                start=True, stop=True)
                    last.then_inc(prep_full, 1)
                elif kind == "m":
                    pe.wait_ge(mneg_ready, T_.up("mneg"))
                    for q in range(QT):
                        last = nc.tensor.transpose(prep[0:GH, q * P:(q + 1) * P], mneg[:, q, :], ident[:])
                    last.then_inc(prep_full, 1)
                elif kind == "pv":
                    pe.wait_ge(pv_copied, T_.up("group"))
                    for q in range(QT):
                        last = nc.tensor.transpose(prep[:, q * P:(q + 1) * P], pvs[:, q * P:(q + 1) * P], ident[:])
                    last.then_inc(prep_full, 1)
                elif kind == "attnT":
                    pe.wait_ge(attn_ready, T_.up("out"))
                    for q in range(QT):
                        last = nc.tensor.transpose(prep[:, q * P:(q + 1) * P], attn[:, q, :], ident[:])
                    last.then_inc(prep_full, 1)
                elif kind == "out":
                    for q in range(QT):
                        last = nc.tensor.matmul(prep[:, q * D:(q + 1) * D], attnT[:, q * P:(q + 1) * P], wo[:],
                                                start=True, stop=True)
                    last.then_inc(prep_full, 1)

            def unit(g, u):
                T_.up("unit")
                wait(pe, max_done, T_.now("unit", 2))
                q, c, hh = u // (4 * GH), u // GH % 4, u % GH
                lo, hi = CHUNKS[c]
                h = g * GH + hh
                nc.tensor.matmul(psum[:, 2 + u % 2, 0:hi - lo], queries_of(qst, h, slice(q * P, q * P + P)),
                                 keys_of(kst, h, slice(lo, hi)), start=True, stop=True).then_inc(max_full, 1)

            def values():
                g, kt, buf, back = pending.pop()
                pe.wait_ge(exp_done, T_.now("step", back))
                k = tile_rows(kt)
                for hh in range(GH):
                    c = (hh % 2) * 2 * T + (hh // 2) * T
                    last = nc.tensor.matmul(pv[32 * hh:32 * hh + 32, :], v_aug[0:k, kt, g * GH + hh, :],
                                            prob[0:k, buf, c:c + T], start=(kt == 0), stop=(kt == KT - 1),
                                            tile_position=(0, 32 * hh))
                last.then_inc(pv_done, 1)

            def prologue():
                pe.wait_ge(w_loaded, N_W * 16)
                for it in PROLOGUE_ITEMS[:-1]:
                    item(*it)
                pe.wait_ge(stacked, 48 * 16)
                T_.up("stacked", 48 * 16)
                for u in range(UNITS_B):
                    unit(0, u)
                item(*PROLOGUE_ITEMS[-1])
                for u in range(UNITS_B - 22):
                    unit(1, u)

            def part(i, r, first, last):
                g = (r + 1) % 4
                for n in range(KT):
                    T_.up("step")
                    if n == 0:
                        pe.wait_ge(m_stacked, T_.up("m_stacked", 64))
                    wait(pe, exp_done, T_.now("step", 2))
                    k, buf = tile_rows(n), (T_.n["step"] - 1) % 2
                    for hh in range(GH):
                        h = g * GH + hh
                        lastmm = nc.tensor.matmul(psum[0:k, 4 + 2 * buf + hh % 2, (hh // 2) * T:(hh // 2) * T + T],
                                                  keys_of(kst, h, slice(n * P, n * P + k)),
                                                  queries_of(qst, h, slice(0, T)), start=True, stop=True)
                    lastmm.then_inc(st_full, 1)
                    units = units_of_step(n) if units_left(r, n, last) else []
                    for u in units[:1]:
                        unit_group = (g + 1) % 4 if n < M_STEP else (g + 2) % 4
                        if u == 0 and unit_group % 2 == 0 and not first:
                            pe.wait_ge(stacked, T_.up("stacked", 24 * 16))
                        unit(unit_group, u)
                    it = prep_item(r, n, first, last)
                    if it:
                        item(*it)
                    if n == 1 and not first:
                        pe.wait_ge(pv_copied, T_.now("group", -1))
                    if n == 1 and r == 3:
                        pe.wait_ge(v_placed, T_.up("placed", 2 if first else 1))
                    if n == 1 and r == 1:
                        pe.wait_ge(v_placed, T_.now("placed"))
                    for u in units[1:2]:
                        unit(unit_group, u)
                    if pending:
                        values()
                    pending.append((g, n, buf, 1))
                    for u in units[2:]:
                        unit(unit_group, u)
                if r == 3 and not first:
                    T_.up("placed")

            parts_of_program(pe, T_, prologue, part)
            pending[0] = pending[0][:3] + (0,)
            values()
            for it in (("pv", 3), ("attnT", 0), ("out", 0)):
                item(*it)


CH, CD = 16, 64
UN = CH // 2
C_ITEMS = {0: [("c", 1)], 1: [("v", 0)], 2: [("c", 2), ("v", 1)], 4: [("c", 3), ("v", 2)],
           5: [("o", 0), ("v", 3)], 6: [("c", 0)]}
C_PREV = (("c", 1), ("c", 2), ("c", 3), ("o", 0))
SCORES_LAG, TURN_LAG, VALUES_LAG = 2, 3, 4


def c_items(slot, first, drain):
    return [it for it in C_ITEMS.get(slot, []) if not (first and it in C_PREV) and not (drain and it not in C_PREV)]


def c_unit(slot, lag, first, drain):
    n = slot - lag
    if (n < 0 and first) or (n >= 0 and drain):
        return None
    return n % UN


def rotary_tables(nc, a, t, sem, tab, w1, w2, raw, bias, theta):
    import numpy as np
    two_pi = 2 * np.pi
    c1 = 6.28125
    c2 = float(np.float32(np.uint32(np.float32(two_pi - c1).view(np.uint32) & 0xFFFFF000).view(np.float32)))
    c3 = float(np.float32(two_pi - c1 - c2))
    magic = 1.5 * 2 ** 23
    with nc.Block() as block, ExitStack() as ctx:
        loaded, pos_set, own, reduced, made = sem("t_loaded"), sem("t_pos"), sem("t_own"), sem("t_reduced"), sem("t_made")
        pos = ctx.enter_context(nc.sbuf_tensor("t_pos", [P, T], F32))
        posi = ctx.enter_context(nc.sbuf_tensor("t_posi", [P, T], mybir.dt.int32))
        ang, k, r = (ctx.enter_context(nc.sbuf_tensor("t_" + n, [P, 2, T], F32)) for n in ("ang", "k", "r"))
        copied = sem("t_copied")

        @block.sync
        def _(sp):
            n = 0
            for m, name in enumerate(("q_w", "k_w")):
                sp.dma_start(raw[:, m, :], a["L0_ffn_" + name]).then_inc(loaded, 16)
                n += 1
            with nc.allow_non_contiguous_dma(reason="biases are spread over partitions once"):
                for quarter in range(4):
                    sp.dma_start(theta[32 * quarter:32 * quarter + 32, :], a["L0_ffn_theta"].rearrange("(p a) -> p a", a=1))\
                        .then_inc(loaded, 16)
                    n += 1
                    hh, par = quarter // 2, quarter % 2
                    for m, name in enumerate(("q_b", "k_b")):
                        v = a["L0_ffn_" + name].rearrange("(j h f a) -> h a f j", j=UN, h=2, a=2)
                        for w in range(2):
                            sp.dma_start(bias[32 * quarter:32 * quarter + 32, m, w, :], v[hh, (par + w) % 2]).then_inc(loaded, 16)
                            n += 1
            sp.wait_ge(loaded, 16 * n)

        @block.gpsimd
        def _(pool):
            nc.gpsimd.iota(posi[:], pattern=[[1, T]], base=0, channel_multiplier=0).then_inc(pos_set, 1)
            pool.wait_ge(loaded, 16 * 22)
            for m in range(2):
                v = raw[:, m, :].rearrange("p (g f a) -> p g a f", g=CH, a=2)
                for par in range(2):
                    nc.gpsimd.tensor_copy(w1[:, m, :].rearrange("p (g a f) -> p g a f", g=CH, a=2)[:, :, par], v[:, :, par])
                    nc.gpsimd.tensor_copy(w2[:, m, :].rearrange("p (g a f) -> p g a f", g=CH, a=2)[:, :, par], v[:, :, 1 - par])

        @block.vector
        def _(dve):
            n = 0

            def link(ins):
                nonlocal n
                n += 1
                ins.then_inc(own, 1)
                dve.wait_ge(own, n)

            dve.wait_ge(pos_set, 1)
            link(nc.vector.tensor_copy(pos[:], posi[:]))
            dve.wait_ge(loaded, 16 * 22)
            for m in range(2):
                link(nc.vector.tensor_scalar(ang[:, m, :], pos[:], theta[:], None, ALU.mult))
            for m in range(2):
                link(nc.vector.tensor_scalar(k[:, m, :], ang[:, m, :], 1.0 / two_pi, 0.25 * (1 - m), ALU.mult, ALU.add))
            link(nc.vector.tensor_scalar_add(k[:], k[:], magic))
            link(nc.vector.tensor_scalar_add(k[:], k[:], -magic))
            for c in (c1, c2, c3):
                link(nc.vector.tensor_scalar(r[:], k[:], -c, None, ALU.mult))
                link(nc.vector.tensor_tensor(ang[:], ang[:], r[:], ALU.add))
            link(nc.vector.tensor_scalar_add(ang[:, 0, :], ang[:, 0, :], np.pi / 2))
            nc.vector.tensor_scalar(r[:], ang[:], 3.1415925, -3.1415925, ALU.min, ALU.max).then_inc(reduced, 1)
            dve.wait_ge(made, 1)
            for q in range(0, P, 64):
                link(nc.vector.tensor_scalar(tab[q:q + 32, 1, 1, :], tab[q:q + 32, 1, 1, :], -1.0, None, ALU.mult))
            nc.vector.tensor_scalar(tab[:, 0, :, :], tab[:, 1, :, :], CD ** -0.5, None, ALU.mult)

        @block.scalar
        def _(act):
            act.wait_ge(reduced, 1)
            nc.scalar.activation(tab[:, 1, :, :], r[:], ACT.Sin).then_inc(made, 1)


def rotary_attention(nc, a, t, psum, s, an_all):
    ctx = ExitStack()
    with ctx:
        def sb(name, shape, dt=F32):
            return ctx.enter_context(nc.sbuf_tensor(name, shape, dt))

        def sem(name):
            return ctx.enter_context(nc.semaphore(name))

        w1, w2 = sb("c_w1", [P, 2, CH * CD]), sb("c_w2", [P, 2, CH * CD])
        tab = sb("c_tab", [P, 2, 2, T])
        bias, theta = sb("c_bias", [P, 2, 2, UN]), sb("c_theta", [P, 1])
        vw, ow = sb("c_vw", [D, CH * CD]), sb("c_ow", [P, UN, D])
        rows = sb("c_rows", [P, 3, D])
        vb = sb("c_vb", [P, CH * CD])
        xT = sb("c_xT", [P, T])
        o = sb("c_o", [P, QT, D])
        turned = sb("c_turned", [P, 2, 2, 2, T])
        qz = sb("c_qz", [P, CH, T])
        kT = sb("c_kT", [P, UN, T])
        v_aug = sb("c_v_aug", [P, QT, CH, CD + 1])
        mneg = sb("c_mneg", [P, 2, QT, 2])
        prob = sb("c_prob", [P, 2, 2, 3 * P])
        probT = sb("c_probT", [P, 2, 2, 3 * P])
        rec = sb("c_rec", [P, 2, QT])
        att = sb("c_att", [P, QT, CH * CD])
        attT = sb("c_attT", [P, UN, T])
        with nc.sbuf_tensor("c_raw", [P, 2, CH * CD], F32) as raw:
            rotary_tables(nc, a, t, sem, tab, w1, w2, raw, bias, theta)

        item_full, item_free = sem("c_item_full"), sem("c_item_free")
        w_loaded, cleared = sem("c_w_loaded"), sem("c_cleared")
        var_ready, rstd_ready, xr_ready = sem("c_var_ready"), sem("c_rstd_ready"), sem("c_xr_ready")
        own_dve, own_pool = sem("c_own_dve"), sem("c_own_pool")
        proj_full, terms_ready, turned_ready = sem("c_proj_full"), sem("c_terms_ready"), sem("c_turned_ready")
        s_full, m_ready, exp_done = sem("c_s_full"), sem("c_m_ready"), sem("c_exp_done")
        tp_full, probT_ready, pv_full, att_ready = sem("c_tp_full"), sem("c_probT_ready"), sem("c_pv_full"), sem("c_att_ready")
        o_ready, resid_ready, x_done = sem("c_o_ready"), sem("c_resid_ready"), sem("c_x_done")
        v_done, passed = sem("c_v_done"), sem("c_passed")
        q_bank, k_bank, s0_bank, s1_bank = psum[:, 0, :], psum[:, 1, :], psum[:, 2, :], psum[:, 3, :]
        misc, pv_bank = psum[:, 6, :], psum[:, 7, :]
        PER = dict(unit=UN, scores=UN, turn=UN, values=UN, item=10, batch=1, norm=3, out=1, v=4, own_pool=2 * UN,
                   own_dve=(NORM_LINKS + RMS_LINKS) + RMS_LINKS + UN + 3)
        N_W = 6
        block = ctx.enter_context(nc.Block())

        def program(eng, tally, norm, turn_x, slot):
            def batch(i, b, first):
                for n in range(UN):
                    slot(i, n, first, False)
                    if b is not None and 1 <= n <= 3:
                        norm(b, n)
                if b is not None:
                    turn_x()

            for n in range(1, 4):
                norm(0, n)
            turn_x()
            batch(0, 1, True)
            with eng.Fori(0, B - 2) as i:
                tally.enter(i)
                batch(i, i + 2, False)
                tally.leave(B - 2)
            batch(B - 2, None, False)
            for n in range(7):
                slot(B - 1, n, False, True)

        @block.sync
        def _(sp):
            sp.dma_start(vw[:], a["L0_ffn_v_w"]).then_inc(w_loaded, 16)
            sp.dma_start(ow[:], a["L0_ffn_o_w"].rearrange("(j p) d -> p j d", p=P)).then_inc(w_loaded, 16)
            for n, name in enumerate(("gamma1", "gamma2", "o_b")):
                sp.dma_start(rows[:, n, :], a["L0_ffn_" + name].rearrange("(a d) -> a d", a=1).to_broadcast([P, D]))\
                    .then_inc(w_loaded, 16)
            sp.dma_start(vb[:], a["L0_ffn_v_b"].rearrange("(a d) -> a d", a=1).to_broadcast([P, CH * CD])).then_inc(w_loaded, 16)
            sp.wait_ge(w_loaded, N_W * 16)

        @block.gpsimd
        def _(pool):
            T_ = Tally(PER)
            nc.gpsimd.memset(qz[:], 0.0).then_inc(cleared, 1)
            nc.gpsimd.memset(v_aug[:], 1.0).then_inc(cleared, 1)
            pool.wait_ge(cleared, 2)
            pool.wait_ge(w_loaded, N_W * 16)

            def power():
                pool.wait_ge(var_ready, T_.up("norm"))
                nc.gpsimd.tensor_tensor(s["rstd"][:], s["ve"][:], t["neg_half"][:], ALU.pow).then_inc(rstd_ready, 1)

            def norm(b, stage):
                if stage < 3:
                    power()
                    return
                pool.wait_ge(xr_ready, T_.up("batch"))
                pool.sem_inc(passed, 1)
                for q in range(QT):
                    ins = nc.gpsimd.tensor_tensor(an_all[:, bass.ds(b * QT + q, 1), :].rearrange("p a d -> p (a d)"),
                                                  s["xr"][:, q, :], rows[:, 2, :], ALU.add)
                ins.then_inc(resid_ready, 1)

            def slot(i, n, first, drain):
                u = c_unit(n, 0, first, drain)
                if ("o", 0) in c_items(n, first, drain):
                    power()
                if u is not None:
                    pool.wait_ge(terms_ready, T_.up("unit"))
                    par = u % 2
                    for hh in range(2):
                        r = slice(64 * hh, 64 * hh + 64)
                        nc.gpsimd.tensor_tensor(qz[r, 2 * u + hh, :], turned[r, par, 0, 0, :], turned[r, par, 0, 1, :], ALU.add)\
                            .then_inc(own_pool, 1)
                        pool.wait_ge(own_pool, T_.up("own_pool"))
                    nc.gpsimd.tensor_tensor(kT[:, u, :], turned[:, par, 1, 0, :], turned[:, par, 1, 1, :], ALU.add)\
                        .then_inc(turned_ready, 1)
                    pool.wait_ge(turned_ready, T_.now("unit"))
            program(pool, T_, norm, lambda: None, slot)

        @block.vector
        def _(dve):
            T_ = Tally(PER)
            dve.wait_ge(w_loaded, N_W * 16)
            s2 = dict(s, xn=o, xr=t["an_cur"])

            def own(ins):
                ins.then_inc(own_dve, 1)
                dve.wait_ge(own_dve, T_.up("own_dve"))

            def item(kind, g, b):
                n = T_.up("item")
                if kind == "v":
                    dve.wait_ge(item_full, n)
                    q, half = g % 2, g // 2
                    w = CH * CD // 2
                    nc.vector.tensor_tensor(v_aug[:, q, 8 * half:8 * half + 8, 0:CD], misc.rearrange("p (h d) -> p h d", h=8),
                                            vb[:, half * w:half * w + w].rearrange("p (h d) -> p h d", h=8), ALU.add)\
                        .then_inc(v_done, 1)
                    dve.wait_ge(v_done, T_.up("v"))
                    dve.sem_inc(item_free, 1)
                elif kind == "o":
                    dve.wait_ge(resid_ready, T_.up("out"))
                    dve.wait_ge(item_full, n)
                    own(nc.vector.tensor_tensor(o[:], misc[:, 0:2 * D].rearrange("p (q d) -> p q d", q=QT),
                                                an_all[:, bass.ds(b * QT, QT), :], ALU.add))
                    dve.sem_inc(item_free, 1)
                    rms_stats(nc, own, s2, 1e-5, var_ready)

            def finish(b):
                rms_scale(nc, dve, own, s2, rows[:, 1, :], rstd_ready, T_.up("norm"))
                own(nc.vector.tensor_scalar(an_all[:, bass.ds(b * QT, QT), :], t["an_cur"][:], 1.0, None, ALU.mult))
                own(nc.vector.tensor_tensor(o[:], o[:], t["an_cur"][:], ALU.add))
                x = t["x"][:, bass.ds(b * QT, QT), :]
                nc.vector.tensor_tensor(x, x, o[:], ALU.add).then_inc(x_done, 1)

            def norm(b, stage):
                def x(q):
                    return t["x"][:, bass.ds(b * QT + q, 1), :].rearrange("p a d -> p (a d)")

                if stage == 1:
                    layer_stats(nc, own, x, s, var_ready)
                elif stage == 2:
                    layer_scale(nc, dve, own, x, s, rstd_ready, T_.up("norm"))
                    rms_stats(nc, own, s, 1e-5, var_ready)
                else:
                    rms_scale(nc, dve, own, s, rows[:, 0, :], rstd_ready, T_.up("norm"))
                    dve.sem_inc(xr_ready, 1)

            def slot(i, n, first, drain):
                u = c_unit(n, SCORES_LAG, first, drain)
                if u is not None:
                    dve.wait_ge(s_full, T_.up("scores"))
                    par = u % 2
                    nc.vector.tensor_reduce(out=mneg[:, par, 0, :], in_=s0_bank[:, 0:2 * P].rearrange("p (h k) -> p h k", h=2),
                                            axis=AX.X, op=ALU.max, negate=True)
                    nc.vector.tensor_reduce(out=mneg[:, par, 1, :], in_=s1_bank.rearrange("p (h k) -> p h k", h=2),
                                            axis=AX.X, op=ALU.max, negate=True).then_inc(m_ready, 1)
                u = c_unit(n, VALUES_LAG, first, drain)
                if u is not None:
                    dve.wait_ge(pv_full, T_.up("values"))
                    v = pv_bank[:, 0:4 * (CD + 1)].rearrange("p (h q c) -> p h q c", h=2, q=QT)
                    own(nc.vector.reciprocal(rec[:], v[:, :, :, CD]))
                    nc.vector.tensor_tensor(att[:, :, P * u:P * u + P].rearrange("p q (h d) -> p h q d", h=2), v[:, :, :, 0:CD],
                                            rec[:].rearrange("p h (q a) -> p h q a", a=1).to_broadcast([P, 2, QT, CD]), ALU.mult)\
                        .then_inc(att_ready, 1)
                for it in c_items(n, first, drain):
                    item(*it, (B - 1 if drain else i))
                if n == 6 and not first:
                    finish(B - 1 if drain else i)
                u = c_unit(n, 0, first, drain)
                if u is not None:
                    v = T_.up("unit")
                    dve.wait_ge(proj_full, v)
                    wait(dve, turned_ready, T_.now("unit", 2))
                    for m, bank in enumerate((q_bank, k_bank)):
                        for w in range(2):
                            ins = nc.vector.scalar_tensor_tensor(out=turned[:, u % 2, m, w, :], in0=bank[:, w * T:(w + 1) * T],
                                                                 scalar=bias[:, m, w, u:u + 1], in1=tab[:, m, w, :],
                                                                 op0=ALU.add, op1=ALU.mult)
                    ins.then_inc(terms_ready, 1)

            program(dve, T_, norm, lambda: T_.up("item"), slot)

        @block.scalar
        def _(act):
            T_ = Tally(PER)

            def turn_x():
                act.wait_ge(item_full, T_.up("item"))
                nc.scalar.activation(xT[:], misc[:, 0:T], ACT.Copy).then_inc(item_free, 1)

            def slot(i, n, first, drain):
                u = c_unit(n, SCORES_LAG, first, drain)
                if u is not None:
                    act.wait_ge(m_ready, T_.up("scores"))
                    wait(act, tp_full, T_.now("scores", 2))
                    par = u % 2
                    for hh in range(2):
                        nc.scalar.activation(prob[:, par, hh, 0:P], s0_bank[:, hh * P:(hh + 1) * P], ACT.Exp,
                                             bias=mneg[:, par, 0, hh:hh + 1])
                        ins = nc.scalar.activation(prob[:, par, hh, P:3 * P], s1_bank[:, hh * 2 * P:(hh + 1) * 2 * P], ACT.Exp,
                                                   bias=mneg[:, par, 1, hh:hh + 1])
                    ins.then_inc(exp_done, 1)
                u = c_unit(n, TURN_LAG, first, drain)
                if u is not None:
                    act.wait_ge(tp_full, T_.up("turn"))
                    wait(act, pv_full, T_.now("turn", 2))
                    nc.scalar.activation(probT[:, u % 2, :, :], psum[:, 4:6, 0:3 * P], ACT.Copy).then_inc(probT_ready, 1)
                for kind, g in c_items(n, first, drain):
                    v = T_.up("item")
                    if kind == "c":
                        act.wait_ge(item_full, v)
                        nc.scalar.activation(attT[:, 2 * g:2 * g + 2, :].rearrange("p j t -> p (j t)"), misc, ACT.Copy)\
                            .then_inc(item_free, 1)

            program(act, T_, lambda b, n: None, turn_x, slot)

        @block.tensor
        def _(pe):
            T_ = Tally(PER)
            pe.wait_ge(w_loaded, N_W * 16)
            pe.wait_ge(cleared, 2)

            def item(kind, g):
                T_.up("item")
                wait(pe, item_free, T_.now("item", 1))
                if kind == "x":
                    pe.wait_ge(xr_ready, T_.up("batch"))
                    for q in range(QT):
                        last = nc.tensor.transpose(misc[:, q * P:(q + 1) * P], s["xr"][:, q, :], t["ident"][:])
                elif kind == "v":
                    q, half = g % 2, g // 2
                    if g == 0:
                        pe.wait_ge(item_free, T_.now("item", 1))
                    w = CH * CD // 2
                    last = nc.tensor.matmul(misc, xT[:, q * P:(q + 1) * P], vw[:, half * w:half * w + w], start=True, stop=True)
                elif kind == "c":
                    for j in range(2):
                        for q in range(QT):
                            last = nc.tensor.transpose(misc[:, (j * QT + q) * P:(j * QT + q + 1) * P],
                                                       att[:, q, (2 * g + j) * P:(2 * g + j + 1) * P], t["ident"][:])
                elif kind == "o":
                    for q in range(QT):
                        for j in range(UN):
                            last = nc.tensor.matmul(misc[:, q * D:(q + 1) * D], attT[:, j, q * P:(q + 1) * P], ow[:, j, :],
                                                    start=(j == 0), stop=(j == UN - 1))
                last.then_inc(item_full, 1)

            def turn_x():
                item("x", 0)

            def slot(i, n, first, drain):
                u = c_unit(n, SCORES_LAG, first, drain)
                if u is not None:
                    pe.wait_ge(turned_ready, T_.up("scores"))
                    wait(pe, exp_done, T_.now("scores", 1))
                    nc.tensor.matmul(s0_bank[:, 0:2 * P], t["identb"][:], t["mask_qk0"][:, 0:2].rearrange("p h k -> p (h k)"),
                                     start=True, stop=False)
                    nc.tensor.matmul(s1_bank, t["identb"][:], t["mask_qk1"][:].rearrange("p h k -> p (h k)"), start=True, stop=False)
                    for hh in range(2):
                        nc.tensor.matmul(s0_bank[:, hh * P:(hh + 1) * P], qz[:, 2 * u + hh, 0:P], kT[:, u, 0:P],
                                         start=False, stop=(hh == 1))
                        last = nc.tensor.matmul(s1_bank[:, hh * 2 * P:(hh + 1) * 2 * P], qz[:, 2 * u + hh, P:2 * P], kT[:, u, :],
                                                start=False, stop=(hh == 1))
                    last.then_inc(s_full, 1)
                u = c_unit(n, TURN_LAG, first, drain)
                if u is not None:
                    pe.wait_ge(exp_done, T_.up("turn"))
                    wait(pe, probT_ready, T_.now("turn", 1))
                    for hh in range(2):
                        for k in range(3):
                            last = nc.tensor.transpose(psum[:, 4 + hh, k * P:(k + 1) * P], prob[:, u % 2, hh, k * P:(k + 1) * P],
                                                       t["ident"][:])
                    last.then_inc(tp_full, 1)
                u = c_unit(n, VALUES_LAG, first, drain)
                if u is not None:
                    pe.wait_ge(probT_ready, T_.up("values"))
                    wait(pe, att_ready, T_.now("values", 1))
                    if u % 4 == 0:
                        pe.wait_ge(v_done, T_.up("v", 2))
                    for hh in range(2):
                        for q in range(QT):
                            c = (hh * QT + q) * (CD + 1)
                            for kt in range(q + 1):
                                last = nc.tensor.matmul(pv_bank[:, c:c + CD + 1], probT[:, u % 2, hh, (q + kt) * P:(q + kt + 1) * P],
                                                        v_aug[:, kt, 2 * u + hh, :], start=(kt == 0), stop=(kt == q))
                    last.then_inc(pv_full, 1)
                for kind, g in c_items(n, first, drain):
                    if kind == "c":
                        pe.wait_ge(att_ready, T_.now("values"))
                    item(kind, g)
                u = c_unit(n, 0, first, drain)
                if u is not None:
                    T_.up("unit")
                    if n == 0:
                        pe.wait_ge(item_free, T_.now("item") if not any(it == ("c", 1) for it in c_items(n, first, drain)) else T_.now("item", 1))
                    wait(pe, terms_ready, T_.now("unit", 1))
                    for m, bank in enumerate((q_bank, k_bank)):
                        for w, weights in enumerate((w1, w2)):
                            last = nc.tensor.matmul(bank[:, w * T:(w + 1) * T], weights[:, m, u * P:(u + 1) * P], xT[:],
                                                    start=True, stop=True)
                    last.then_inc(proj_full, 1)

            program(pe, T_, lambda b, n: None, turn_x, slot)


NE = 31
TOP = 3
GW = 4 * 32
WCH = 4
TW = B * T // WCH


def gates_of_experts(nc, a, t, psum, d):
    ctx = ExitStack()
    with ctx:
        def sb(name, shape, dt=F32):
            return ctx.enter_context(nc.sbuf_tensor(name, shape, dt))

        def sem(name):
            return ctx.enter_context(nc.semaphore(name))

        NT = B * QT
        PAD = 40
        rw, rb = sb("g_rw", [P, NE]), sb("g_rb", [P, NE])
        b1 = sb("g_b1", [32, P])
        lg = sb("g_lg", [P, NT, NE])
        mx, sm = sb("g_mx", [P, NT]), sb("g_sm", [P, NT])
        aff, cut = sb("g_aff", [P, NT, PAD]), sb("g_cut", [P, NT, PAD])
        top = sb("g_top", [P, NT, 8])
        gates, rest = sb("g_gates", [P, NT, 32]), sb("g_rest", [P, NT, 32])
        parts = sb("g_parts", [P, NT, 4, 32], BF16)
        sel1 = sb("g_sel1", [P, 32], BF16)
        loaded, own, pool_own = sem("g_loaded"), sem("g_own"), sem("g_pool_own")
        turned, copied, logits, sums = sem("g_turned"), sem("g_copied"), sem("g_logits"), sem("g_sums")
        exp_done, gates_ready, sel_ready = sem("g_exp_done"), sem("g_gates_ready"), sem("g_sel_ready")
        gates_turned, gates_copied = sem("g_gates_turned"), sem("g_gates_copied")
        N_W = 6
        block = ctx.enter_context(nc.Block())

        @block.sync
        def _(sp):
            sp.dma_start(rw[:], a["L0_ffn_router_w"]).then_inc(loaded, 16)
            sp.dma_start(rb[:], a["L0_ffn_router_b"].rearrange("(a e) -> a e", a=1).to_broadcast([P, NE])).then_inc(loaded, 16)
            for dst, name, shared in ((b1, "re_b1", "sh_b1"), (d["b2"], "re_b2", "sh_b2")):
                sp.dma_start(dst[0:NE, :], a["L0_ffn_" + name]).then_inc(loaded, 16)
                sp.dma_start(dst[NE:32, :], a["L0_ffn_" + shared].rearrange("(a d) -> a d", a=1)).then_inc(loaded, 16)
            sp.wait_ge(loaded, N_W * 16)

        @block.gpsimd
        def _(pool):
            nc.gpsimd.memset(sel1[:], 0.0).then_inc(pool_own, 1)
            for k in range(3):
                pool.wait_ge(pool_own, k + 1)
                nc.gpsimd.affine_select(out=sel1[:], in_=sel1[:], compare_op=ALU.not_equal, fill=1.0, base=-32 * k,
                                        pattern=[[-1, 32]], channel_multiplier=1).then_inc(pool_own, 1)

        @block.vector
        def _(dve):
            n = 0

            def link(ins):
                nonlocal n
                n += 1
                ins.then_inc(own, 1)
                dve.wait_ge(own, n)

            def wide(v, w):
                return v.rearrange("p (t a) -> p t a", a=1).to_broadcast([P, NT, w])

            nc.vector.memset(aff[:], -1.0)
            nc.vector.memset(parts[:], 0.0)
            dve.wait_ge(pool_own, 4)
            nc.vector.tensor_copy(d["sel"][:], sel1[:].rearrange("p (e a) -> p e a", a=1).to_broadcast([P, 32, P]))
            dve.wait_ge(loaded, N_W * 16)
            dve.wait_ge(logits, 1)
            link(nc.vector.tensor_tensor(lg[:], psum[:, 4, :].rearrange("p (t e) -> p t e", e=32)[:, :, 0:NE],
                                         rb[:].rearrange("p (a e) -> p a e", a=1).to_broadcast([P, NT, NE]), ALU.add))
            link(nc.vector.tensor_reduce(out=mx[:], in_=lg[:], axis=AX.X, op=ALU.max))
            link(nc.vector.tensor_tensor(lg[:], lg[:], wide(mx[:], NE), ALU.subtract))
            dve.sem_inc(sums, 1)
            dve.wait_ge(exp_done, 1)
            link(nc.vector.tensor_reduce(out=sm[:], in_=lg[:], axis=AX.X, op=ALU.add))
            link(nc.vector.reciprocal(sm[:], sm[:]))
            link(nc.vector.tensor_tensor(aff[:, :, 0:NE], lg[:], wide(sm[:], NE), ALU.mult))
            for k in range(NT):
                ins = nc.vector.max(top[:, k, :], aff[:, k, :])
            link(ins)
            link(nc.vector.memset(top[:, :, TOP:8], -1.0))
            for k in range(NT):
                ins = nc.vector.match_replace(out=cut[:, k, :], in_to_replace=top[:, k, :], in_values=aff[:, k, :], imm_value=-2.0)
            link(ins)
            link(nc.vector.tensor_tensor(cut[:, :, 0:NE], cut[:, :, 0:NE], aff[:, :, 0:NE], ALU.not_equal))
            link(nc.vector.tensor_tensor(gates[:, :, 0:NE], cut[:, :, 0:NE], aff[:, :, 0:NE], ALU.mult))
            link(nc.vector.memset(gates[:, :, NE:32], 1.0))
            split3(nc, dve, link, [parts[:, :, k, :] for k in range(3)], rest[:], gates[:]).then_inc(gates_ready, 1)

        @block.scalar
        def _(act):
            for c in range(WCH):
                act.wait_ge(turned, c + 1)
                nc.scalar.activation(d["anT"][:, c * TW:(c + 1) * TW], psum[:, c, :], ACT.Copy).then_inc(copied, 1)
            act.wait_ge(turned, WCH + 1)
            nc.scalar.activation(d["b1T"][:], psum[:, 5, 0:32], ACT.Copy).then_inc(copied, 1)
            act.wait_ge(sums, 1)
            nc.scalar.activation(lg[:], lg[:], ACT.Exp).then_inc(exp_done, 1)
            for c in range(WCH):
                act.wait_ge(gates_turned, c + 1)
                nc.scalar.activation(d["gatesT"][:, c * TW:(c + 1) * TW], psum[0:32, c, :], ACT.Copy)
                nc.scalar.activation(d["gparts"][:, c * TW:(c + 1) * TW], psum[:, 4 + c, :], ACT.Copy).then_inc(gates_copied, 1)

        @block.tensor
        def _(pe):
            per = NT // WCH
            for c in range(WCH):
                for k in range(per):
                    ins = nc.tensor.transpose(psum[:, c, k * P:(k + 1) * P], d["an"][:, c * per + k, :], t["ident"][:])
                ins.then_inc(turned, 1)
            pe.wait_ge(loaded, N_W * 16)
            nc.tensor.transpose(psum[:, 5, 0:32], b1[:], t["ident"][0:32, 0:32]).then_inc(turned, 1)
            for k in range(NT):
                if k % per == 0:
                    pe.wait_ge(copied, k // per + 1)
                ins = nc.tensor.matmul(psum[:, 4, k * 32:k * 32 + NE], d["anT"][:, k * P:(k + 1) * P], rw[:], start=True, stop=True)
            ins.then_inc(logits, 1)
            pe.wait_ge(copied, WCH + 1)
            pe.wait_ge(gates_ready, 1)
            for c in range(WCH):
                for k in range(c * per, (c + 1) * per):
                    cols = slice((k % per) * P, (k % per + 1) * P)
                    nc.tensor.transpose(psum[0:32, c, cols], gates[:, k, :], t["ident"][:])
                    ins = nc.tensor.matmul(psum[:, 4 + c, cols], parts[:, k, :, :].rearrange("p s e -> p (s e)"), t["identb"][:],
                                           start=True, stop=True)
                ins.then_inc(gates_turned, 1)


def experts(nc, a, t, psum, d, out):
    ctx = ExitStack()
    with ctx:
        def sb(name, shape, dt=F32):
            return ctx.enter_context(nc.sbuf_tensor(name, shape, dt))

        def sem(name):
            return ctx.enter_context(nc.semaphore(name))

        w = sb("e_w", [P, 2, 2, P])
        gl = sb("e_gl", [P, 2, TW])
        hg = sb("e_hg", [P, 2, TW])
        yT = sb("e_yT", [P, WCH, TW])
        h_full, gelu_done, passed = sem("e_h_full"), sem("e_gelu_done"), sem("e_passed")
        w_loaded = [sem("e_w_loaded0"), sem("e_w_loaded1")]
        g_full, hg_ready, y_done = sem("e_g_full"), sem("e_hg_ready"), sem("e_y_done")
        b2_done, y_copied, y_turned, x_done, stored = (sem("e_b2_done"), sem("e_y_copied"), sem("e_y_turned"),
                                                       sem("e_x_done"), sem("e_stored"))
        ROUNDS = NE // 2
        STEPS = 2 * WCH
        PER = dict(step=STEPS, y=STEPS, load=1)
        block = ctx.enter_context(nc.Block())

        def program(tally, eng, part):
            for k in range(STEPS):
                part(None, k)
            with eng.Fori(0, ROUNDS) as i:
                tally.enter(i)
                for k in range(STEPS):
                    part(i, k)
                tally.leave(ROUNDS)

        @block.sync
        def _(sp):
            T_ = Tally(PER)

            def load(e, j):
                for m in range(2):
                    if e is None:
                        src = a["L0_ffn_sh_w%d" % (m + 1)]
                    else:
                        v = a["L0_ffn_re_w%d" % (m + 1)]
                        src = v[e, :, :] if isinstance(e, int) else v[bass.ds(e, 1), :, :].rearrange("a p d -> p (a d)")
                    sp.dma_start(w[:, j, m, :], src).then_inc(w_loaded[j], 16)

            load(None, 0)
            load(0, 1)
            T_.n["y"] = 0
            with sp.Fori(0, ROUNDS) as i:
                T_.enter(i)
                for j in range(2):
                    sp.wait_ge(y_done, T_.up("y", WCH))
                    load(i * 2 + 1 + j, j)
                T_.leave(ROUNDS)
            for c in range(WCH):
                sp.wait_ge(x_done, c + 1)
                sp.dma_start(out.rearrange("b (q p) d -> p (b q) d", p=P)[:, c * 4:(c + 1) * 4, :], t["x"][:, c * 4:(c + 1) * 4, :])\
                    .then_inc(stored, 16)
            sp.wait_ge(stored, WCH * 16)

        @block.scalar
        def _(act):
            T_ = Tally(PER)

            def part(i, k):
                act.wait_ge(h_full, T_.up("step"))
                wait(act, hg_ready, T_.now("step", 2))
                act.sem_inc(passed, 1)
                j = k // WCH
                b1 = d["b1T"][:, (NE, 0)[j]:(NE, 0)[j] + 1] if i is None else d["b1T"][:, bass.ds(i * 2 + 1 + j, 1)]
                nc.scalar.activation(gl[:, k % 2, :], psum[:, 4 + k % 2, :], ACT.Gelu, bias=b1).then_inc(gelu_done, 1)

            program(T_, act, part)
            for c in range(WCH):
                act.wait_ge(b2_done, c + 1)
                nc.scalar.activation(yT[:, c, :], psum[:, c, :], ACT.Copy).then_inc(y_copied, 1)

        @block.vector
        def _(dve):
            T_ = Tally(PER)

            def part(i, k):
                v = T_.up("step")
                dve.wait_ge(gelu_done, v)
                dve.wait_ge(g_full, v)
                wait(dve, y_done, T_.now("step", 2))
                nc.vector.tensor_tensor(hg[:, k % 2, :], gl[:, k % 2, :], psum[:, 6 + k % 2, :], ALU.mult).then_inc(hg_ready, 1)

            program(T_, dve, part)
            for c in range(WCH):
                dve.wait_ge(y_turned, c + 1)
                x = t["x"][:, c * 4:(c + 1) * 4, :]
                nc.vector.tensor_tensor(x, x, psum[:, 4 + c, :].rearrange("p (q d) -> p q d", q=4), ALU.add).then_inc(x_done, 1)

        @block.tensor
        def _(pe):
            T_ = Tally(PER)

            def second(c, j, buf):
                pe.wait_ge(hg_ready, T_.up("y"))
                nc.tensor.matmul(psum[:, c, :], w[:, j, 1, :], hg[:, buf, :], start=second.start, stop=False).then_inc(y_done, 1)

            second.start = True

            def part(i, k):
                T_.up("step")
                j, c = divmod(k, WCH)
                if c == 0:
                    if j == 0:
                        T_.up("load")
                    pe.wait_ge(w_loaded[j], 32 * T_.now("load"))
                wait(pe, gelu_done, T_.now("step", 2))
                nc.tensor.matmul(psum[:, 4 + k % 2, :], w[:, j, 0, :], d["anT"][:, c * TW:(c + 1) * TW], start=True, stop=True)\
                    .then_inc(h_full, 1)
                wait(pe, hg_ready, T_.now("step", 2))
                e = (NE, 0)[j] if i is None else None
                sel = d["sel"][:, e, :] if i is None else d["sel"][:, bass.ds(i * 2 + 1 + j, 1), :].rearrange("p a m -> p (a m)")
                nc.tensor.matmul(psum[:, 6 + k % 2, :], sel, d["gparts"][:, c * TW:(c + 1) * TW], start=True, stop=True)\
                    .then_inc(g_full, 1)
                if not (i is None and k == 0):
                    second((c - 1) % WCH, ((k - 1) % STEPS) // WCH, (k - 1) % 2)
                if i is None and k == WCH:
                    second.start = False

            program(T_, pe, part)
            second(WCH - 1, 1, 1)
            for c in range(WCH):
                nc.tensor.matmul(psum[:, c, :], d["b2"][:], d["gatesT"][:, c * TW:(c + 1) * TW], start=False, stop=True)\
                    .then_inc(b2_done, 1)
            pe.wait_ge(hg_ready, T_.now("step"))
            for c in range(WCH):
                pe.wait_ge(y_copied, c + 1)
                for q in range(4):
                    ins = nc.tensor.transpose(psum[:, 4 + c, q * P:(q + 1) * P], yT[:, c, q * P:(q + 1) * P], t["ident"][:])
                ins.then_inc(y_turned, 1)


_NAMES = ['x', 'ctx_768', 'L0_attn_norm_w', 'L0_attn_Wq', 'L0_attn_bq', 'L0_attn_Wk', 'L0_attn_bk', 'L0_attn_Wv',
          'L0_attn_bv', 'L0_attn_Wo', 'L0_attn_bo', 'L0_xattn_Wq', 'L0_xattn_bq', 'L0_xattn_Wkv', 'L0_xattn_bkv',
          'L0_xattn_Wo', 'L0_xattn_bo', 'L0_ffn_theta', 'L0_ffn_gamma1', 'L0_ffn_gamma2', 'L0_ffn_q_w', 'L0_ffn_q_b',
          'L0_ffn_k_w', 'L0_ffn_k_b', 'L0_ffn_v_w', 'L0_ffn_v_b', 'L0_ffn_o_w', 'L0_ffn_o_b', 'L0_ffn_router_w',
          'L0_ffn_router_b', 'L0_ffn_sh_w1', 'L0_ffn_sh_b1', 'L0_ffn_sh_w2', 'L0_ffn_sh_b2', 'L0_ffn_re_w1',
          'L0_ffn_re_b1', 'L0_ffn_re_w2', 'L0_ffn_re_b2']


def kernel(**inputs):
    import numpy as _np
    import concourse.bacc as _bacc
    from concourse import mybir as _mybir
    from concourse.bass_utils import run_bass_kernel_spmd as _run

    nc = _bacc.Bacc("TRN2", target_bir_lowering=False, num_devices=1)
    arrays, args = {}, {}
    for name in _NAMES:
        v = _np.ascontiguousarray(inputs[name])
        arrays["in_" + name] = v
        args[name] = nc.dram_tensor("in_" + name, v.shape, _mybir.dt.from_np(v.dtype), kind="ExternalInput").ap()
    out = nc.dram_tensor("out_x", (B, T, D), F32, kind="ExternalOutput").ap()
    build(nc, args, out)
    r = _run(nc, [arrays], core_ids=[0])
    return r.results[0]["out_x"]
```

```python
import concourse.bass as bass
from concourse import mybir
from contextlib import ExitStack

F32 = mybir.dt.float32
BF16 = mybir.dt.bfloat16
ACT = mybir.ActivationFunctionType
ALU = mybir.AluOpType
AX = mybir.AxisListType

P = 128
B, T, D = 8, 256, 128
QT = T // P
H, HD = 16, D // 16
G, GH = 4, 4
SKV, DC = 1601, 96
MASKED = -1.0e30

PRODUCTS = [(0, 0), (0, 1), (0, 2), (1, 0), (1, 1), (2, 0)]
NP = len(PRODUCTS)
TWO_ONES = 1.0019378662109375
SHIFT_ROW = NP * HD


def build(nc, a, out):
    ctx = ExitStack()
    with ctx:
        def sb(name, shape, dt=F32):
            return ctx.enter_context(nc.sbuf_tensor(name, shape, dt))

        def sem(name):
            return ctx.enter_context(nc.semaphore(name))

        t = dict(
            x=sb("x_sb", [P, B * QT, D]),
            ident=sb("ident", [P, P]), identb=sb("identb", [P, P], BF16),
            mask_qk0=sb("mask_qk0", [P, 4, P], BF16), mask_qk1=sb("mask_qk1", [P, 2, 2 * P], BF16),
            mask_kq0=sb("mask_kq0", [P, 2, 2 * P], BF16), mask_kq1=sb("mask_kq1", [P, 2, P], BF16),
            neg_half=sb("neg_half", [P, QT]),
            qst=sb("q_stack", [P, H, T], BF16),
            kst=sb("k_stack", [P, H // 2, SKV + 1], BF16),
        )
        s = dict(stats=sb("stats", [P, QT, 6]), mv=sb("mv", [P, QT, 2]), ve=sb("ve", [P, QT]),
                 msq=sb("msq", [P, QT]), rstd=sb("rstd", [P, QT]), xn=sb("xn", [P, QT, D]),
                 xr=sb("xr", [P, QT, D]), spare=sb("spare", [P, 1]))
        psum = ctx.enter_context(nc.psum_tensor("psum", [P, 8, 512], F32))
        own = SelfLoads(a, sb, sem)
        setup(nc, a, t, sem, own)
        tables = RotaryTables(nc, a, sb, sem)
        cross = CrossLoads(a, sb, sem)
        self_attention(nc, a, t, psum, s, tables, cross, own)
        tables.allocate_weights(sb, sem)
        cross_attention(nc, a, t, psum, s, cross, tables)
        t["an_cur"] = sb("an_cur", [P, QT, D])
        an_all = sb("an_all", [P, B * QT, D])
        experts_pre = ExpertLoads(a, sb, sem)
        rotary_attention(nc, a, t, psum, s, an_all, tables, experts_pre)
        d = dict(an=an_all, anT=sb("anT", [P, B * T]), gatesT=sb("gatesT", [32, B * T]), b1T=sb("b1T", [P, 32]), b2=experts_pre.b2,
                 gates=nc.dram_tensor("gates", [32, B * T], F32, kind="Internal").ap(), stored=sem("gates_stored"))
        gates_of_experts(nc, a, t, psum, d, experts_pre)
        experts(nc, a, t, psum, d, out, experts_pre)


def setup(nc, a, t, sem, own):
    with nc.Block() as block:
        x_loaded, cleared, idents = sem("x_loaded"), sem("cleared"), sem("idents")

        @block.sync
        def _(sp):
            sp.dma_start(t["x"][:], a["x"].rearrange("b (q p) d -> p (b q) d", p=P)).then_inc(x_loaded, 16)
            own.load(sp)
            sp.wait_ge(x_loaded, 16)

        @block.vector
        def _(dve):
            for name in ("ident", "identb", "mask_qk0", "mask_qk1", "mask_kq0", "mask_kq1"):
                nc.vector.memset(t[name][:], 0.0).then_inc(cleared, 1)
            nc.vector.memset(t["neg_half"][:], -0.5)
            nc.vector.memset(t["qst"].bitcast(F32)[:], 0.0)
            nc.vector.memset(t["kst"].bitcast(F32)[:, :, 0:T], TWO_ONES)

        @block.gpsimd
        def _(pool):
            pool.wait_ge(cleared, 6)
            for name in ("ident", "identb"):
                nc.gpsimd.affine_select(out=t[name][:], in_=t[name][:], compare_op=ALU.not_equal, fill=1.0,
                                        base=0, pattern=[[-1, P]], channel_multiplier=1).then_inc(idents, 1)
            for name, part in (("mask_qk0", t["mask_qk0"][:]), ("mask_qk1", t["mask_qk1"][:, :, P:2 * P])):
                nc.gpsimd.affine_select(out=part, in_=part, compare_op=ALU.is_ge, fill=MASKED, base=0,
                                        pattern=[[0, part.shape[1]], [-1, P]], channel_multiplier=1).then_inc(idents, 1)
            for name, part in (("mask_kq0", t["mask_kq0"][:, :, 0:P]), ("mask_kq1", t["mask_kq1"][:])):
                nc.gpsimd.affine_select(out=part, in_=part, compare_op=ALU.is_ge, fill=MASKED, base=0,
                                        pattern=[[0, part.shape[1]], [1, P]], channel_multiplier=-1).then_inc(idents, 1)
            nc.gpsimd.memset(t["kst"].bitcast(F32)[:, :, T:(SKV + 1) // 2], TWO_ONES)


NORM_LINKS = 4
RMS_LINKS = 6


def layer_stats(nc, link, x, s, var_ready, eps=1e-5):
    for q in range(QT):
        link(nc.vector.bn_stats(s["stats"][:, q, :], x(q)))
    nc.vector.memset(s["spare"][:], 0.0)
    for q in range(QT):
        ins = nc.vector.bn_aggr(s["mv"][:, q, :], s["stats"][:, q, :])
    link(ins)
    nc.vector.tensor_scalar_add(s["ve"][:], s["mv"][:, :, 1], eps).then_inc(var_ready, 1)


def layer_scale(nc, dve, link, x, s, rstd_ready, ready_at):
    dve.wait_ge(rstd_ready, ready_at)
    for q in range(QT):
        ins = nc.vector.tensor_scalar(s["xn"][:, q, :], x(q), s["mv"][:, q, 0:1], s["rstd"][:, q:q + 1],
                                      ALU.subtract, ALU.mult)
    link(ins)


def rms_stats(nc, link, s, eps, var_ready):
    for q in range(QT):
        link(nc.vector.bn_stats(s["stats"][:, q, :], s["xn"][:, q, :]))
    nc.vector.memset(s["spare"][:], 0.0)
    for q in range(QT):
        ins = nc.vector.bn_aggr(s["mv"][:, q, :], s["stats"][:, q, :])
    link(ins)
    link(nc.vector.tensor_tensor(s["msq"][:], s["mv"][:, :, 0], s["mv"][:, :, 0], ALU.mult))
    link(nc.vector.tensor_tensor(s["msq"][:], s["msq"][:], s["mv"][:, :, 1], ALU.add))
    nc.vector.tensor_scalar_add(s["ve"][:], s["msq"][:], eps).then_inc(var_ready, 1)


def rms_scale(nc, dve, link, s, weight, rstd_ready, ready_at):
    dve.wait_ge(rstd_ready, ready_at)
    for q in range(QT):
        ins = nc.vector.scalar_tensor_tensor(out=s["xr"][:, q, :], in0=s["xn"][:, q, :],
                                             scalar=s["rstd"][:, q:q + 1], in1=weight, op0=ALU.mult, op1=ALU.mult)
    link(ins)


def split3(nc, dve, link, parts, rest, src):
    link(nc.vector.tensor_copy(parts[0], src))
    link(nc.vector.tensor_tensor(rest, src, parts[0], ALU.subtract))
    link(nc.vector.tensor_copy(parts[1], rest))
    return nc.vector.tensor_tensor(parts[2], rest, parts[1], ALU.subtract)


def unit_heads(u):
    per, v = (4, u) if u < 4 else (2, u - 4)
    return [2 * k + v % 2 for k in range(per * (v // 2), per * (v // 2) + per)]


def column(h):
    return (h % 2) * (H // 2) + h // 2


def queries_of(qst, h, cols):
    return qst[:, h, cols]


def keys_of(kst, h, cols):
    return kst[:, h // 2, cols]


def stack_rows(stack, which, i, row, count, tiles):
    rows = slice(64 * i + row, 64 * i + row + count)
    if which == 0:
        return stack[rows, slice(2 * tiles.start + i, 2 * tiles.stop, 2)]
    return stack[rows, tiles]


BOUNCES = 3


def bounce_parts(sp, scratch, parts, which, sem):
    n = parts.shape[2]
    if which == 0:
        copies = ((0, 3, parts[:, 0:1, :].to_broadcast([P, 3, n])), (3, 5, parts[:, 1:2, :].to_broadcast([P, 2, n])),
                  (5, 6, parts[:, 2:3, :]))
    else:
        copies = ((0, 3, parts), (3, 5, parts[:, 0:2, :]), (5, 6, parts[:, 0:1, :]))
    for lo, hi, src in copies:
        sp.dma_start(scratch[:, lo:hi, :], src).then_inc(sem, 16)


def load_stack(sp, stack, scratch, which, tiles, sem):
    n = scratch.shape[2]
    v = scratch.rearrange("(t i d) c n -> i (d c) t n", i=2, d=HD)
    for i in range(2):
        sp.dma_start(stack_rows(stack, which, i, 0, NP * HD, tiles)[:, :, 0:n], v[i, :, tiles]).then_inc(sem, 16)


CH, CD = 16, 64
UN = CH // 2


class RotaryTables:

    def __init__(self, nc, a, sb, sem):
        self.nc, self.a = nc, a
        self.w1, self.w2 = sb("c_w1", [P, 2, CH * CD]), sb("c_w2", [P, 2, CH * CD])
        self.tab = sb("c_tab", [P, 2, 2, T])
        self.bias, self.theta = sb("c_bias", [P, 2, 2, UN]), sb("c_theta", [P, 1])
        self.loaded, self.pos_set, self.own = sem("t_loaded"), sem("t_pos"), sem("t_own")
        self.reduced, self.made = sem("t_reduced"), sem("t_made")

    def allocate_weights(self, sb, sem):
        self.vw, self.ow = sb("c_vw", [D, CH * CD]), sb("c_ow", [P, UN, D])
        self.rows = sb("c_rows", [P, 3, D])
        self.vb = sb("c_vb", [P, CH * CD])
        self.w_loaded = sem("c_w_loaded")

    N_W = 6

    def load_weights(self, sp):
        a = self.a
        sp.dma_start(self.vw[:], a["L0_ffn_v_w"]).then_inc(self.w_loaded, 16)
        sp.dma_start(self.ow[:], a["L0_ffn_o_w"].rearrange("(j p) d -> p j d", p=P)).then_inc(self.w_loaded, 16)
        for n, name in enumerate(("gamma1", "gamma2", "o_b")):
            sp.dma_start(self.rows[:, n, :], a["L0_ffn_" + name].rearrange("(a d) -> a d", a=1).to_broadcast([P, D]))\
                .then_inc(self.w_loaded, 16)
        sp.dma_start(self.vb[:], a["L0_ffn_v_b"].rearrange("(a d) -> a d", a=1).to_broadcast([P, CH * CD])).then_inc(self.w_loaded, 16)

    def scratch(self, sb):
        self.raw = sb("t_raw", [P, 2, CH * CD])
        self.pos, self.posi = sb("t_pos", [P, T]), sb("t_posi", [P, T], mybir.dt.int32)
        self.ang, self.k, self.r = (sb("t_" + n, [P, 2, T]) for n in ("ang", "k", "r"))

    def load(self, sp):
        nc, a = self.nc, self.a
        for m, name in enumerate(("q_w", "k_w")):
            sp.dma_start(self.raw[:, m, :], a["L0_ffn_" + name]).then_inc(self.loaded, 16)
        with nc.allow_non_contiguous_dma(reason="biases are spread over partitions once"):
            for quarter in range(4):
                rows = slice(32 * quarter, 32 * quarter + 32)
                sp.dma_start(self.theta[rows, :], a["L0_ffn_theta"].rearrange("(p a) -> p a", a=1)).then_inc(self.loaded, 16)
                hh, par = quarter // 2, quarter % 2
                for m, name in enumerate(("q_b", "k_b")):
                    v = a["L0_ffn_" + name].rearrange("(j h f a) -> h a f j", j=UN, h=2, a=2)
                    for w in range(2):
                        sp.dma_start(self.bias[rows, m, w, :], v[hh, (par + w) % 2]).then_inc(self.loaded, 16)

    N_LOADS = 2 + 4 * 5

    def positions(self, pool):
        self.nc.gpsimd.iota(self.posi[:], pattern=[[1, T]], base=0, channel_multiplier=0).then_inc(self.pos_set, 1)

    def order_weights(self, pool):
        pool.wait_ge(self.loaded, 16 * self.N_LOADS)
        for m in range(2):
            v = self.raw[:, m, :].rearrange("p (g f a) -> p g a f", g=CH, a=2)
            for par in range(2):
                for dst, src in ((self.w1, par), (self.w2, 1 - par)):
                    self.nc.gpsimd.tensor_copy(dst[:, m, :].rearrange("p (g a f) -> p g a f", g=CH, a=2)[:, :, par], v[:, :, src])

    def angles(self, dve):
        import numpy as np
        nc, ang, k, r, tab = self.nc, self.ang, self.k, self.r, self.tab
        two_pi = 2 * np.pi
        c1 = 6.28125
        c2 = float(np.float32(np.uint32(np.float32(two_pi - c1).view(np.uint32) & 0xFFFFF000).view(np.float32)))
        c3 = float(np.float32(two_pi - c1 - c2))
        magic = 1.5 * 2 ** 23
        n = 0

        def link(ins):
            nonlocal n
            n += 1
            ins.then_inc(self.own, 1)
            dve.wait_ge(self.own, n)

        dve.wait_ge(self.pos_set, 1)
        link(nc.vector.tensor_copy(self.pos[:], self.posi[:]))
        dve.wait_ge(self.loaded, 16 * self.N_LOADS)
        for m in range(2):
            link(nc.vector.tensor_scalar(ang[:, m, :], self.pos[:], self.theta[:], None, ALU.mult))
        for m in range(2):
            link(nc.vector.tensor_scalar(k[:, m, :], ang[:, m, :], 1.0 / two_pi, 0.25 * (1 - m), ALU.mult, ALU.add))
        link(nc.vector.tensor_scalar_add(k[:], k[:], magic))
        link(nc.vector.tensor_scalar_add(k[:], k[:], -magic))
        for c in (c1, c2, c3):
            link(nc.vector.tensor_scalar(r[:], k[:], -c, None, ALU.mult))
            link(nc.vector.tensor_tensor(ang[:], ang[:], r[:], ALU.add))
        link(nc.vector.tensor_scalar_add(ang[:, 0, :], ang[:, 0, :], np.pi / 2))
        nc.vector.tensor_scalar(r[:], ang[:], 3.1415925, -3.1415925, ALU.min, ALU.max).then_inc(self.reduced, 1)
        dve.wait_ge(self.made, 1)
        for q in range(0, P, 64):
            link(nc.vector.tensor_scalar(tab[q:q + 32, 1, 1, :], tab[q:q + 32, 1, 1, :], -1.0, None, ALU.mult))
        nc.vector.tensor_scalar(tab[:, 0, :, :], tab[:, 1, :, :], CD ** -0.5, None, ALU.mult)

    def sines(self, act):
        act.wait_ge(self.reduced, 1)
        self.nc.scalar.activation(self.tab[:, 1, :, :], self.r[:], ACT.Sin).then_inc(self.made, 1)


class SelfLoads:

    def __init__(self, a, sb, sem):
        self.a = a
        self.w_nat = sb("a_w_nat", [P, 4, D])
        self.bqk = sb("a_bqk", [P, 2])
        self.rows = sb("a_rows", [P, 3, D])
        self.w_loaded = sem("a_w_loaded")

    def load(self, sp):
        a = self.a
        for n, name in enumerate(("norm_w", "bv", "bo")):
            sp.dma_start(self.rows[:, n, :], a["L0_attn_" + name].rearrange("(a d) -> a d", a=1).to_broadcast([P, D]))\
                .then_inc(self.w_loaded, 16)
        for n, name in enumerate(("Wq", "Wk", "Wv", "Wo")):
            sp.dma_start(self.w_nat[:, n, :], a["L0_attn_" + name]).then_inc(self.w_loaded, 16)
        for n, name in enumerate(("bq", "bk")):
            sp.dma_start(self.bqk[:, n:n + 1], a["L0_attn_" + name].rearrange("(p a) -> p a", a=1)).then_inc(self.w_loaded, 16)


def self_attention(nc, a, t, psum, s, tables, cross, pre):
    ctx = ExitStack()
    with ctx:
        def sb(name, shape, dt=F32):
            return ctx.enter_context(nc.sbuf_tensor(name, shape, dt))

        def sem(name):
            return ctx.enter_context(nc.semaphore(name))

        w_nat, bqk, rows = pre.w_nat, pre.bqk, pre.rows
        w_t = sb("a_w_t", [P, 4, D])
        resid = sb("a_resid", [P, 2, QT, D])
        xT = sb("a_xT", [P, T])
        qk = sb("a_qk", [P, 2 * T])
        rest = sb("a_rest", [P, 2 * T])
        parts = sb("a_parts", [P, 3, 2 * T], BF16)
        v_augs = [sb("a_v_aug%d" % j, [P, QT, H, 32]) for j in range(2)]
        mneg = sb("a_mneg", [P, QT, H])
        mparts = sb("a_mparts", [H, 2, T], BF16)
        prob = sb("a_prob", [P, 2, 4 * T])
        pvs = sb("a_pvs", [P, T])
        rec = sb("a_rec", [P, QT, GH])
        attn = sb("a_attn", [P, QT, D])
        attnT = sb("a_attnT", [P, T])
        tables.scratch(sb)
        scratch = [[nc.dram_tensor("a_scratch%d%d" % (j, n), [P, NP, T], BF16, kind="Internal").ap() for n in range(2)]
                   for j in range(2)]
        ident, identb = t["ident"], t["identb"]
        qsts = [t["qst"], sb("a_q_stack1", [P, H, T], BF16)]
        ksts = [t["kst"][:, :, j * T:(j + 1) * T] for j in range(2)]
        prep = psum[:, 0, :]
        pv = psum[:, 1, 0:T]

        UNITS = 4 + 8
        STEPS = 2 * G
        ITEMS_AT = {0: "v", 2: "x", 3: "pv", 4: "qk", 5: "pv", 7: "pv"}
        UNITS_AT = [range(n * UNITS // STEPS, (n + 1) * UNITS // STEPS) for n in range(STEPS)]

        w_loaded, wT_full, wT_free = pre.w_loaded, sem("a_wT_full"), sem("a_wT_free")
        var_ready, rstd_ready = sem("a_var_ready"), sem("a_rstd_ready")
        xr_ready, resid_ready = sem("a_xr_ready"), sem("a_resid_ready")
        dve_own, pool_own = sem("a_dve_own"), sem("a_pool_own")
        prep_full, prep_free = sem("a_prep_full"), sem("a_prep_free")
        parts_ready, bounced, stacked = sem("a_parts_ready"), sem("a_bounced"), sem("a_stacked")
        max_full, max_done = sem("a_max_full"), sem("a_max_done")
        m0_ready, m1_ready, m_stacked = sem("a_m0_ready"), sem("a_m1_ready"), sem("a_m_stacked")
        st_full, exp_done, pv_done, pv_copied = sem("a_st_full"), sem("a_exp_done"), sem("a_pv_done"), sem("a_pv_copied")
        attn_ready, x_done = sem("a_attn_ready"), sem("a_x_done")
        ones_set, stack_cleared, passed = sem("a_ones_set"), sem("a_stack_cleared"), sem("a_passed")

        PER = {name: 2 * n for name, n in dict(
            item=3 + 1 + G + 2, norm=2, next=1, batch=1, stack=1, m=1, qk=1, unit=UNITS, scores=STEPS, values=STEPS, group=G,
            dve_own=NORM_LINKS + RMS_LINKS + 3 + G + 2, pool_own=QT).items()}
        block = ctx.enter_context(nc.Block())

        def shown(kind, more, further):
            return {"v": more, "x": further, "qk": further, "m": more}.get(kind, True)

        def program(eng, tally, begin, attend):
            begin()
            with eng.Fori(0, B // 2 - 1) as i:
                tally.enter(i)
                for j in range(2):
                    attend(i * 2 + j, j, True, True)
                tally.leave(B // 2 - 1)
            for j in range(2):
                attend(B - 2 + j, j, j == 0, False)

        @block.sync
        def _(sp):
            T_ = Tally(PER)

            def bounce(j):
                sp.wait_ge(parts_ready, T_.up("next"))
                for which in range(2):
                    bounce_parts(sp, scratch[j][which], parts[:, :, which * T:which * T + T], which, bounced)

            def stack(j):
                sp.wait_ge(bounced, 2 * BOUNCES * 16 * T_.now("next"))
                for which, operand in enumerate((qsts[j], ksts[j])):
                    load_stack(sp, operand, scratch[j][which], which, slice(0, H // 2), stacked)

            def store_m(j):
                sp.wait_ge(m1_ready, T_.up("m"))
                for par in range(2):
                    for m in range(2):
                        sp.dma_start(stack_rows(qsts[j], 0, par, SHIFT_ROW + m, 1, slice(0, H // 2)), mparts[par * 8:par * 8 + 8, m, :])\
                            .then_inc(m_stacked, 16)

            def attend(b, j, more, further):
                T_.up("scores", STEPS)
                if further:
                    bounce(j)
                if more:
                    store_m(1 - j)
                if further:
                    sp.wait_ge(st_full, T_.now("scores"))
                    sp.sem_inc(passed, 1)
                    stack(j)

            def begin():
                bounce(0)
                stack(0)
                cross.load(sp)
                bounce(1)
                sp.wait_ge(stack_cleared, 1)
                stack(1)
                store_m(0)

            tables.load(sp)
            program(sp, T_, begin, attend)

        @block.gpsimd
        def _(pool):
            T_ = Tally(PER)
            pool.wait_ge(w_loaded, 9 * 16)

            def powers():
                for n in range(2):
                    pool.wait_ge(var_ready, T_.up("norm"))
                    nc.gpsimd.tensor_tensor(s["rstd"][:], s["ve"][:], t["neg_half"][:], ALU.pow).then_inc(rstd_ready, 1)

            def residual(b, j):
                pool.wait_ge(xr_ready, T_.up("next"))
                for q in range(QT):
                    nc.gpsimd.tensor_tensor(resid[:, j, q, :], s["xr"][:, q, :], rows[:, 2, :], ALU.add).then_inc(pool_own, 1)
                    pool.wait_ge(pool_own, T_.up("pool_own"))
                nc.gpsimd.tensor_tensor(resid[:, j], resid[:, j], t["x"][:, bass.ds(b * QT, QT), :], ALU.add)\
                    .then_inc(resid_ready, 1)

            def attend(b, j, more, further):
                T_.up("batch")
                if further:
                    powers()
                    pool.wait_ge(x_done, T_.now("batch"))
                    residual(b + 2, j)

            def begin():
                for j in range(2):
                    powers()
                    residual(j, j)
                    if j == 0:
                        nc.gpsimd.memset(qsts[1][:], 0.0).then_inc(stack_cleared, 1)
                tables.order_weights(pool)

            tables.positions(pool)
            program(pool, T_, begin, attend)

        @block.vector
        def _(dve):
            T_ = Tally(PER)
            dve.wait_ge(w_loaded, 9 * 16)

            def own(ins):
                ins.then_inc(dve_own, 1)
                dve.wait_ge(dve_own, T_.up("dve_own"))

            def norm(b, stage):
                def x(q):
                    return t["x"][:, bass.ds(b * QT + q, 1), :].rearrange("p a d -> p (a d)")

                if stage == 0:
                    layer_stats(nc, own, x, s, var_ready)
                elif stage == 1:
                    layer_scale(nc, dve, own, x, s, rstd_ready, T_.up("norm"))
                    rms_stats(nc, own, s, 1e-6, var_ready)
                elif stage == 2:
                    rms_scale(nc, dve, own, s, rows[:, 0, :], rstd_ready, T_.up("norm"))
                    dve.sem_inc(xr_ready, 1)

            def item(kind, g=0):
                n = T_.up("item")
                if kind == "qk":
                    dve.wait_ge(prep_free, n)
                    wait(dve, bounced, 2 * BOUNCES * 16 * (T_.up("qk") - 1))
                    split3(nc, dve, own, [parts[:, n, :] for n in range(3)], rest[:], qk[:]).then_inc(parts_ready, 1)
                elif kind == "m":
                    dve.wait_ge(m0_ready, T_.up("m"))
                    nc.vector.tensor_tensor(mparts[:, 1, :], prep[0:H, 0:T], mparts[:, 0, :], ALU.subtract)\
                        .then_inc(m1_ready, 1)
                    dve.wait_ge(m1_ready, T_.now("m"))
                    dve.sem_inc(prep_free, 1)
                elif kind == "pv":
                    dve.wait_ge(prep_full, n)
                    o = prep[:, 0:2 * P].rearrange("p (q h c) -> p q h c", q=QT, h=GH)
                    own(nc.vector.reciprocal(rec[:], o[:, :, :, HD]))
                    nc.vector.tensor_tensor(
                        attn[:, :, 32 * g:32 * g + 32].rearrange("p q (h d) -> p q h d", h=GH), o[:, :, :, 0:HD],
                        rec[:].rearrange("p q (h a) -> p q h a", a=1).to_broadcast([P, QT, GH, HD]), ALU.mult)\
                        .then_inc(prep_free, 1)
                    if g == G - 1:
                        dve.wait_ge(prep_free, n)
                        for q in range(QT):
                            own(nc.vector.tensor_tensor(attn[:, q, :], attn[:, q, :], rows[:, 1, :], ALU.add))
                        dve.sem_inc(attn_ready, 1)

            def begin():
                for b in range(2):
                    for stage in range(3):
                        norm(b, stage)
                    if b == 0:
                        for v_aug in v_augs:
                            nc.vector.memset(v_aug[:], 1.0).then_inc(ones_set, 1)
                    for kind in ("x", "qk", "v") if b == 0 else ("x", "qk"):
                        item(kind)
                maxima(range(UNITS))
                item("m")
                tables.angles(dve)

            def maxima(units):
                for u in units:
                    dve.wait_ge(max_full, T_.up("unit"))
                    heads = unit_heads(u)
                    c = column(heads[0])
                    dst = mneg[:, 0 if u < 4 else 1, c:c + len(heads)]
                    src = psum[:, 2 + u % 2, :].rearrange("p (h k) -> p h k", h=len(heads))
                    nc.vector.tensor_reduce(out=dst, in_=src, axis=AX.X, op=ALU.max, negate=True).then_inc(max_done, 1)

            def attend(b, j, more, further):
                T_.up("batch")
                for n in range(STEPS):
                    if further:
                        norm(b + 2, n)
                    if more:
                        maxima(UNITS_AT[n])
                    kind = ITEMS_AT.get(n)
                    if kind and shown(kind, more, further):
                        item(kind, (n - 3) // 2)
                if more:
                    item("m")
                item("pv", G - 1)
                item("attnT")
                n = T_.up("item")
                dve.wait_ge(resid_ready, T_.now("batch"))
                dve.wait_ge(prep_full, n)
                nc.vector.tensor_tensor(t["x"][:, bass.ds(b * QT, QT), :],
                                        prep[:, 0:2 * P].rearrange("p (q d) -> p q d", q=QT), resid[:, j], ALU.add)\
                    .then_inc(x_done, 1)
                dve.wait_ge(x_done, T_.now("batch"))
                dve.sem_inc(prep_free, 1)

            program(dve, T_, begin, attend)

        @block.scalar
        def _(act):
            T_ = Tally(PER)
            act.wait_ge(wT_full, 1)
            nc.scalar.activation(w_t[:].rearrange("p n d -> p (n d)"), prep, ACT.Copy).then_inc(wT_free, 1)

            def item(kind, j=0):
                n = T_.up("item")
                if kind == "x":
                    act.wait_ge(prep_full, n)
                    nc.scalar.activation(xT[:], prep[:, 0:T], ACT.Copy).then_inc(prep_free, 1)
                elif kind == "qk":
                    act.wait_ge(prep_full, n)
                    wait(act, parts_ready, T_.up("qk") - 1)
                    nc.scalar.activation(qk[:, 0:T], prep[:, 0:T], ACT.Identity, bias=bqk[:, 0:1])
                    nc.scalar.activation(qk[:, T:2 * T], prep[:, T:2 * T], ACT.Identity, bias=bqk[:, 1:2]).then_inc(prep_free, 1)
                elif kind == "v":
                    act.wait_ge(prep_full, n)
                    nc.scalar.activation(v_augs[j][:, :, :, 0:HD],
                                         prep[:, 0:2 * D].rearrange("p (q h d) -> p q h d", q=QT, h=H), ACT.Copy)\
                        .then_inc(prep_free, 1)
                elif kind == "m":
                    act.wait_ge(prep_full, n)
                    nc.scalar.activation(mparts[:, 0, :], prep[0:H, 0:T], ACT.Copy).then_inc(m0_ready, 1)
                elif kind == "attnT":
                    act.wait_ge(prep_full, n)
                    nc.scalar.activation(attnT[:], prep[:, 0:T], ACT.Copy).then_inc(prep_free, 1)

            def begin():
                for kind in ("x", "qk"):
                    item(kind)
                act.wait_ge(ones_set, 2)
                for kind in ("v", "x", "qk"):
                    item(kind, 0)
                item("m")
                tables.sines(act)

            def copy_pv():
                act.wait_ge(pv_done, T_.up("values", 2))
                wait(act, prep_full, T_.now("item"))
                nc.scalar.activation(pvs[:], pv, ACT.Copy).then_inc(pv_copied, 1)

            def attend(b, j, more, further):
                for n in range(STEPS):
                    act.wait_ge(st_full, T_.up("scores"))
                    w = 2 * T if n % 2 == 0 else T
                    nc.scalar.activation(prob[:, n % 2, 0:2 * w].rearrange("p (a c) -> p a c", a=2),
                                         psum[:, 4 + 2 * (n % 2):6 + 2 * (n % 2), 0:w], ACT.Exp, scale=HD ** -0.5)\
                        .then_inc(exp_done, 1)
                    if n >= 2 and n % 2 == 0:
                        copy_pv()
                    kind = ITEMS_AT.get(n)
                    if kind and shown(kind, more, further):
                        item(kind, 1 - j)
                if more:
                    item("m")
                copy_pv()
                for kind in ("pv", "attnT", "out"):
                    item(kind)

            program(act, T_, begin, attend)

        @block.tensor
        def _(pe):
            T_ = Tally(PER)
            pe.wait_ge(w_loaded, 9 * 16)
            for n in range(4):
                last = nc.tensor.transpose(prep[:, n * D:(n + 1) * D], w_nat[:, n, :], ident[:])
            last.then_inc(wT_full, 1)
            pe.wait_ge(wT_free, 1)

            def item(kind):
                T_.up("item")
                wait(pe, prep_free, T_.now("item", 1))
                if kind == "x":
                    pe.wait_ge(xr_ready, T_.up("next"))
                    for q in range(QT):
                        last = nc.tensor.transpose(prep[:, q * P:(q + 1) * P], s["xr"][:, q, :], ident[:])
                elif kind == "qk":
                    for n in range(2):
                        last = nc.tensor.matmul(prep[:, n * T:(n + 1) * T], w_t[:, n, :], xT[:], start=True, stop=True)
                elif kind == "v":
                    for q in range(QT):
                        last = nc.tensor.matmul(prep[:, q * D:(q + 1) * D], xT[:, q * P:(q + 1) * P], w_t[:, 2, :],
                                                start=True, stop=True)
                elif kind == "m":
                    pe.wait_ge(max_done, T_.now("unit"))
                    for q in range(QT):
                        last = nc.tensor.transpose(prep[0:H, q * P:(q + 1) * P], mneg[:, q, :], ident[:])
                elif kind == "pv":
                    pe.wait_ge(pv_copied, T_.up("group"))
                    for q in range(QT):
                        last = nc.tensor.transpose(prep[:, q * P:(q + 1) * P], pvs[:, q * P:(q + 1) * P], ident[:])
                elif kind == "attnT":
                    pe.wait_ge(attn_ready, T_.now("batch"))
                    for q in range(QT):
                        last = nc.tensor.transpose(prep[:, q * P:(q + 1) * P], attn[:, q, :], ident[:])
                elif kind == "out":
                    for q in range(QT):
                        last = nc.tensor.matmul(prep[:, q * D:(q + 1) * D], attnT[:, q * P:(q + 1) * P], w_t[:, 3, :],
                                                start=True, stop=True)
                last.then_inc(prep_full, 1)

            def scores_t(n, j):
                g, kt = n // 2, n % 2
                T_.up("scores")
                if n >= 2:
                    pe.wait_ge(exp_done, T_.now("scores", 2))
                w = T - kt * P
                for par in range(2):
                    nc.tensor.matmul(psum[:, 4 + 2 * (n % 2) + par, 0:2 * w], identb[:],
                                     t["mask_kq%d" % kt][:].rearrange("p h q -> p (h q)"), start=True, stop=False)
                for hh in range(GH):
                    h = g * GH + hh
                    dst = psum[:, 4 + 2 * (n % 2) + hh % 2, (hh // 2) * w:(hh // 2) * w + w]
                    last = nc.tensor.matmul(dst, keys_of(ksts[j], h, slice(kt * P, kt * P + P)),
                                            queries_of(qsts[j], h, slice(kt * P, T)), start=False, stop=(hh >= 2))
                last.then_inc(st_full, 1)

            def values(n, j):
                g, kt = n // 2, n % 2
                pe.wait_ge(exp_done, T_.up("values"))
                if kt == 0 and n > 0:
                    pe.wait_ge(pv_copied, T_.now("group", -1))
                w = T - kt * P
                for hh in range(GH):
                    c = (hh % 2) * 2 * w + (hh // 2) * w
                    last = nc.tensor.matmul(pv[32 * hh:32 * hh + 32, kt * P:T], v_augs[j][:, kt, g * GH + hh, :],
                                            prob[:, n % 2, c:c + w], start=(kt == 0), stop=(kt == 1),
                                            tile_position=(0, 32 * hh))
                last.then_inc(pv_done, 1)

            def maxima(units, j):
                for u in units:
                    if u == 0:
                        pe.wait_ge(stacked, T_.up("stack") * 4 * 16)
                    T_.up("unit")
                    wait(pe, max_done, T_.now("unit", 2))
                    bank = psum[:, 2 + u % 2, :]
                    q, keys, heads, mask = (0, P, unit_heads(u), "mask_qk0") if u < 4 else (1, 2 * P, unit_heads(u), "mask_qk1")
                    nc.tensor.matmul(bank, identb[:], t[mask][:].rearrange("p h k -> p (h k)"), start=True, stop=False)
                    for n, h in enumerate(heads):
                        last = nc.tensor.matmul(bank[:, n * keys:(n + 1) * keys], queries_of(qsts[j], h, slice(q * P, q * P + P)),
                                                keys_of(ksts[j], h, slice(0, keys)), start=False, stop=(n == len(heads) - 1))
                    last.then_inc(max_full, 1)

            def begin():
                for kind in ("x", "qk", "v", "x", "qk"):
                    item(kind)
                maxima(range(UNITS), 0)
                item("m")

            def attend(b, j, more, further):
                pe.wait_ge(m_stacked, T_.up("batch") * 4 * 16)
                for n in range(STEPS):
                    scores_t(n, j)
                    units = UNITS_AT[n] if more else range(0)
                    maxima(units[:1], 1 - j)
                    if n >= 1:
                        values(n - 1, j)
                    maxima(units[1:], 1 - j)
                    kind = ITEMS_AT.get(n)
                    if kind and shown(kind, more, further):
                        item(kind)
                if more:
                    item("m")
                values(STEPS - 1, j)
                for kind in ("pv", "attnT", "out"):
                    item(kind)

            program(pe, T_, begin, attend)


class Tally:

    def __init__(self, per):
        self.n, self.per, self.i = dict.fromkeys(per, 0), per, None

    def up(self, name, by=1):
        self.n[name] += by
        return self.now(name)

    def now(self, name, back=0):
        n = self.n[name] - back
        return n if self.i is None else self.i * self.per[name] + n

    def enter(self, i):
        self.i, self.start = i, dict(self.n)

    def leave(self, rounds):
        for name, n in self.n.items():
            assert n - self.start[name] in (0, self.per[name]), (name, n - self.start[name], self.per[name])
            if n != self.start[name]:
                self.n[name] = self.start[name] + rounds * self.per[name]
        self.i = None


def wait(eng, sem, value):
    if not isinstance(value, int) or value > 0:
        eng.wait_ge(sem, value)


KT = -(-SKV // P)
CHUNKS = [(c * SKV // 4, (c + 1) * SKV // 4) for c in range(4)]
CW = max(e - s for s, e in CHUNKS)
UNITS_B = QT * GH * 4
M_STEP = 9
HEAD = 21


def tile_rows(kt):
    return min(P, SKV - kt * P)


def units_of_step(n):
    head = HEAD
    if n < M_STEP:
        lo, k = UNITS_B - head, M_STEP
        return [lo + u for u in range(n * head // k, (n + 1) * head // k)]
    k, n, total = KT - M_STEP, n - M_STEP, UNITS_B - head
    return list(range(n * total // k, (n + 1) * total // k))


PREP_AT = {(0, 0): ("ctx", 0), (0, 1): ("k", 0), (0, 2): ("pv", 0), (0, 3): ("ctx", 1), (0, 4): ("k", 1),
           (0, 5): ("ctx", 2), (0, 6): ("k", 2), (0, 7): ("ctx", 3), (0, 8): ("k", 3), (0, 9): ("m", 2),
           (0, 10): ("x", 0), (0, 11): ("q", 0), (0, 12): ("v", 0), (1, 0): ("v", 1), (1, 1): ("v", 2),
           (1, 2): ("pv", 1), (1, 3): ("v", 3), (1, 9): ("m", 3), (2, 2): ("pv", 2), (2, 9): ("m", 0),
           (3, 2): ("pv", 3), (3, 4): ("attnT", 0), (3, 6): ("out", 0), (3, 9): ("m", 1)}
NEXT_BATCH = ("ctx", "k", "x", "q", "v")


def prep_item(r, n, first=False, last=False):
    item = PREP_AT.get((r, n))
    if item is None or (last and (item[0] in NEXT_BATCH or item == ("m", 0))):
        return None
    if first and item[0] in ("pv", "attnT", "out"):
        return None
    return item


def column4(hh):
    return hh % 2 * 2 + hh // 2


PROLOGUE_ITEMS = [("ctx", 0), ("k", 0), ("ctx", 1), ("x", 0), ("q", 0), ("k", 1), ("ctx", 2), ("k", 2), ("ctx", 3), ("k", 3),
                  ("v", 0), ("v", 1), ("v", 2), ("v", 3), ("m", 0)]


def units_left(r, n, last):
    return not (last and (r == 2 or (r == 1 and n >= M_STEP)))


class CrossLoads:

    def __init__(self, a, sb, sem):
        self.a = a
        self.wq, self.wo = sb("b_wq", [D, D]), sb("b_wo", [D, D])
        self.wkv = sb("b_wkv", [DC, 2 * D])
        self.bq, self.bk = sb("b_bq", [P, 1]), sb("b_bk", [P, 1])
        self.rows = sb("b_rows", [P, 2, D])
        self.ctx_sb = sb("b_ctx", [P, KT, DC])
        self.w_loaded, self.ctx_loaded = sem("b_w_loaded"), sem("b_ctx_loaded")

    N_W = 7

    def load(self, sp):
        a = self.a
        for dst, src in ((self.wq[:], a["L0_xattn_Wq"]), (self.wo[:], a["L0_xattn_Wo"]), (self.wkv[:], a["L0_xattn_Wkv"]),
                         (self.bq[:], a["L0_xattn_bq"].rearrange("(p a) -> p a", a=1)),
                         (self.bk[:], a["L0_xattn_bkv"][0:D].rearrange("(p a) -> p a", a=1)),
                         (self.rows[:, 0, :], a["L0_xattn_bkv"][D:2 * D].rearrange("(a d) -> a d", a=1).to_broadcast([P, D])),
                         (self.rows[:, 1, :], a["L0_xattn_bo"].rearrange("(a d) -> a d", a=1).to_broadcast([P, D]))):
            sp.dma_start(dst, src).then_inc(self.w_loaded, 16)
        self.load_ctx(sp, a["ctx_768"][0])

    def load_ctx(self, sp, src):
        sp.dma_start(self.ctx_sb[:, 0:KT - 1, :], src[0:(KT - 1) * P].rearrange("(k p) d -> p k d", p=P)).then_inc(self.ctx_loaded, 16)
        sp.dma_start(self.ctx_sb[0:tile_rows(KT - 1), KT - 1, :], src[(KT - 1) * P:SKV]).then_inc(self.ctx_loaded, 16)


def cross_attention(nc, a, t, psum, s, pre, tables):
    ctx = ExitStack()
    with ctx:
        def sb(name, shape, dt=F32):
            return ctx.enter_context(nc.sbuf_tensor(name, shape, dt))

        def sem(name):
            return ctx.enter_context(nc.semaphore(name))

        wq, wo, wkv, bq, bk, rows, ctx_sb = pre.wq, pre.wo, pre.wkv, pre.bq, pre.bk, pre.rows, pre.ctx_sb
        resid = sb("b_resid", [P, QT, D])
        xT = sb("b_xT", [P, T])
        qf, qrest = sb("b_qf", [P, T]), sb("b_qrest", [P, T])
        qparts = sb("b_qparts", [P, 3, T], BF16)
        ctxT = sb("b_ctxT", [DC, SKV])
        kf, krest = sb("b_kf", [P, 2, CW]), sb("b_krest", [P, 2, CW])
        zeros = sb("b_zeros", [P, CW])
        kparts = sb("b_kparts", [P, 3, SKV], BF16)
        v_new = sb("b_v_new", [P, KT, D])
        v_aug = sb("b_v_aug", [P, KT, H, 32])
        chunk_max = sb("b_chunk_max", [P, 2, QT, GH, 4])
        mneg = sb("b_mneg", [P, QT, GH])
        mparts = sb("b_mparts", [GH, 2, T], BF16)
        prob = sb("b_prob", [P, 2, GH * T])
        pvs = sb("b_pvs", [P, T])
        rec = sb("b_rec", [P, QT, GH])
        attn = sb("b_attn", [P, QT, D])
        attnT = sb("b_attnT", [P, T])
        q_scr = nc.dram_tensor("b_q_scratch", [P, NP, T], BF16, kind="Internal").ap()
        k_scr = nc.dram_tensor("b_k_scratch", [P, NP, SKV], BF16, kind="Internal").ap()
        qst, kst, ident = t["qst"], t["kst"], t["ident"]
        prep, pv = psum[:, 0, :], psum[:, 1, 0:T]

        w_loaded, ones_set, half_stacked = pre.w_loaded, sem("b_ones_set"), sem("b_half_stacked")
        chunks_bounced = sem("b_chunks_bounced")
        var_ready, rstd_ready, xn_ready = sem("b_var_ready"), sem("b_rstd_ready"), sem("b_xn_ready")
        dve_own, pool_own = sem("b_dve_own"), sem("b_pool_own")
        prep_full, prep_free = sem("b_prep_full"), sem("b_prep_free")
        ctx_loaded, ctx_used = pre.ctx_loaded, sem("b_ctx_used")
        kf_ready, k_split = sem("b_kf_ready"), sem("b_k_split")
        qf_ready, q_split = sem("b_qf_ready"), sem("b_q_split")
        q_bounced, k_bounced, stacked = sem("b_q_bounced"), sem("b_k_bounced"), sem("b_stacked")
        v_evacuated, v_placed = sem("b_v_evacuated"), sem("b_v_placed")
        max_full, max_done, mneg_ready = sem("b_max_full"), sem("b_max_done"), sem("b_mneg_ready")
        m0_ready, m1_ready, m_stacked = sem("b_m0_ready"), sem("b_m1_ready"), sem("b_m_stacked")
        st_full, exp_done, pv_done, pv_copied = sem("b_st_full"), sem("b_exp_done"), sem("b_pv_done"), sem("b_pv_copied")
        attn_ready, resid_ready, x_done = sem("b_attn_ready"), sem("b_resid_ready"), sem("b_x_done")

        passed = sem("b_passed")
        PER = dict(item=len(PREP_AT), step=4 * KT, unit=4 * UNITS_B, group=4, batch=1, kchunk=4, half=2,
                   stacked=8 * 16, m_stacked=4 * 64, dma=BOUNCES * 16, kdma=BOUNCES * 16, ctx=32, own_dve=NORM_LINKS + G + 2,
                   own_pool=4 * 2 + 2, mneg=4, vchunk=4, placed=2, out=1)
        N_W = pre.N_W
        block = ctx.enter_context(nc.Block())

        def parts_of_program(eng, tally, prologue, part):
            prologue()
            part(-1, 3, first=True, last=False)
            with eng.Fori(0, B - 2) as i:
                tally.enter(i)
                for r in range(4):
                    part(i, r, first=False, last=False)
                tally.leave(B - 2)
            for r in range(4):
                part(B - 2, r, first=False, last=False)
            for r in range(3):
                part(B - 1, r, first=False, last=True)

        @block.sync
        def _(sp):
            T_ = Tally(PER)
            def load_ctx(b):
                wait(sp, ctx_used, T_.now("batch"))
                sp.sem_inc(passed, 1)
                src = a["ctx_768"][b] if isinstance(b, int) else a["ctx_768"][bass.ds(b, 1)].rearrange("a s d -> (a s) d")
                pre.load_ctx(sp, src)

            def bounce():
                wait(sp, stacked, T_.now("stacked"))
                sp.sem_inc(passed, 1)
                sp.wait_ge(k_split, T_.up("kchunk", 4))
                bounce_parts(sp, k_scr, kparts[:], 1, k_bounced)
                sp.wait_ge(q_split, T_.up("batch"))
                bounce_parts(sp, q_scr, qparts[:], 0, q_bounced)
                sp.wait_ge(q_bounced, T_.up("dma", BOUNCES * 16))
                sp.wait_ge(k_bounced, T_.now("dma"))

            def load_operand(which, half, done):
                load_stack(sp, (qst, kst)[which], (q_scr, k_scr)[which], which, slice(4 * half, 4 * half + 4), done)

            def load_half(half):
                T_.up("stacked", 4 * 16)
                for which in range(2):
                    load_operand(which, half, stacked)

            def store_m(g):
                sp.wait_ge(m1_ready, T_.up("group"))
                for par in range(2):
                    for m in range(2):
                        sp.dma_start(stack_rows(qst, 0, par, SHIFT_ROW + m, 1, slice(2 * g, 2 * g + 2)), mparts[2 * par:2 * par + 2, m, :])\
                            .then_inc(m_stacked, 16)

            def prologue():
                sp.wait_ge(q_split, T_.up("batch"))
                bounce_parts(sp, q_scr, qparts[:], 0, q_bounced)
                sp.wait_ge(q_bounced, T_.up("dma", BOUNCES * 16))
                load_operand(0, 0, half_stacked)
                for c, (lo, hi) in enumerate(CHUNKS):
                    sp.wait_ge(k_split, T_.up("kchunk"))
                    bounce_parts(sp, k_scr[:, :, lo:hi], kparts[:, :, lo:hi], 1, k_bounced if c == 3 else chunks_bounced)
                load_operand(0, 1, stacked)
                sp.wait_ge(chunks_bounced, 3 * BOUNCES * 16)
                sp.wait_ge(k_bounced, T_.now("dma"))
                load_operand(1, 0, half_stacked)
                load_operand(1, 1, stacked)
                T_.up("stacked", 4 * 16)
                tables.load_weights(sp)
                store_m(0)

            def part(i, r, first, last):
                if r == 3:
                    if not first:
                        sp.wait_ge(st_full, T_.now("step"))
                        load_half(1)
                    if not isinstance(i, int) or i + 2 < B:
                        load_ctx(i + 2)
                if prep_item(r, M_STEP, first, last):
                    store_m(PREP_AT[(r, M_STEP)][1])
                T_.up("step", KT)
                if r == 0 and not last:
                    bounce()
                    sp.wait_ge(st_full, T_.now("step"))
                    load_half(0)

            parts_of_program(sp, T_, prologue, part)

        @block.gpsimd
        def _(pool):
            T_ = Tally(PER)

            def own(ins):
                ins.then_inc(pool_own, 1)
                pool.wait_ge(pool_own, T_.up("own_pool"))

            def power():
                pool.wait_ge(var_ready, T_.up("batch"))
                nc.gpsimd.tensor_tensor(s["rstd"][:], s["ve"][:], t["neg_half"][:], ALU.pow).then_inc(rstd_ready, 1)

            def split_k():
                wait(pool, k_bounced, T_.now("dma"))
                for c, (lo, hi) in enumerate(CHUNKS):
                    n = T_.up("kchunk")
                    pool.wait_ge(kf_ready, n)
                    own(nc.gpsimd.tensor_tensor(krest[:, c % 2, 0:hi - lo], kf[:, c % 2, 0:hi - lo], kparts[:, 0, lo:hi], ALU.subtract))
                    own(nc.gpsimd.tensor_tensor(kparts[:, 1, lo:hi], krest[:, c % 2, 0:hi - lo], zeros[:, 0:hi - lo], ALU.add))
                    nc.gpsimd.tensor_tensor(kparts[:, 2, lo:hi], krest[:, c % 2, 0:hi - lo], kparts[:, 1, lo:hi], ALU.subtract)\
                        .then_inc(k_split, 1)

            def split_q():
                wait(pool, q_bounced, T_.now("dma"))
                T_.up("dma", BOUNCES * 16)
                pool.wait_ge(qf_ready, T_.now("batch"))
                own(nc.gpsimd.tensor_tensor(qrest[:], qf[:], qparts[:, 0, :], ALU.subtract))
                own(nc.gpsimd.tensor_tensor(qparts[:, 1, :], qrest[:], zeros[:, 0:T], ALU.add))
                nc.gpsimd.tensor_tensor(qparts[:, 2, :], qrest[:], qparts[:, 1, :], ALU.subtract).then_inc(q_split, 1)

            def place_v(half):
                pool.wait_ge(v_evacuated, T_.now("kchunk"))
                wait(pool, pv_done, T_.now("step"))
                pool.sem_inc(passed, 1)
                c = half * H // 2
                for lo, hi, n in ((0, KT - 1, P), (KT - 1, KT, tile_rows(KT - 1))):
                    ins = nc.gpsimd.tensor_copy(v_aug[0:n, lo:hi, c:c + H // 2, 0:HD],
                                                v_new[0:n, lo:hi, c * HD:(c + H // 2) * HD].rearrange("p k (h d) -> p k h d", h=H // 2))
                ins.then_inc(v_placed, 1)

            def residual(b):
                wait(pool, x_done, T_.now("out"))
                T_.up("out")
                for q in range(QT):
                    ins = nc.gpsimd.tensor_tensor(
                        resid[:, q, :], t["x"][:, bass.ds(b * QT + q, 1), :].rearrange("p a d -> p (a d)"), rows[:, 1, :], ALU.add)
                ins.then_inc(resid_ready, 1)

            def prologue():
                pool.wait_ge(w_loaded, N_W * 16)
                pool.wait_ge(ones_set, 1)
                power()
                split_k()
                T_.up("dma", BOUNCES * 16)
                pool.wait_ge(ones_set, 2)
                place_v(0)
                place_v(1)

            def part(i, r, first, last):
                if r == 0 and not last:
                    power()
                    split_k()
                    split_q()
                T_.up("step", KT)
                if r == 1 and not last:
                    T_.up("step", -KT)
                    place_v(0)
                    T_.up("step", KT)
                if r == 2:
                    residual(B - 1 if last else i)
                    if not last:
                        place_v(1)

            parts_of_program(pool, T_, prologue, part)

        @block.vector
        def _(dve):
            T_ = Tally(PER)

            def own(ins):
                ins.then_inc(dve_own, 1)
                dve.wait_ge(dve_own, T_.up("own_dve"))

            def tile_of(b):
                return lambda q: t["x"][:, bass.ds(b * QT + q, 1), :].rearrange("p a d -> p (a d)")

            def norm_stats(b):
                T_.up("batch")
                layer_stats(nc, own, tile_of(b), s, var_ready)

            def norm_scale(b):
                layer_scale(nc, dve, own, tile_of(b), s, rstd_ready, T_.now("batch"))
                dve.sem_inc(xn_ready, 1)

            def unit(u):
                v = T_.up("unit")
                q, c, hh = u // (4 * GH), u // GH % 4, u % GH
                half = (T_.n["unit"] - 1) // UNITS_B % 2
                w = CHUNKS[c][1] - CHUNKS[c][0]
                dve.wait_ge(max_full, v)
                nc.vector.tensor_reduce(out=chunk_max[:, half, q, column4(hh), c:c + 1], in_=psum[:, 2 + u % 2, 0:w],
                                        axis=AX.X, op=ALU.max).then_inc(max_done, 1)
                if u == UNITS_B - 1:
                    dve.wait_ge(max_done, T_.now("unit"))
                    nc.vector.tensor_reduce(out=mneg[:], in_=chunk_max[:, half], axis=AX.X, op=ALU.max, negate=True)\
                        .then_inc(mneg_ready, 1)

            def item(kind, g, b):
                n = T_.up("item")
                if kind == "m":
                    dve.wait_ge(m0_ready, T_.up("group"))
                    nc.vector.tensor_tensor(mparts[:, 1, :], prep[0:GH, 0:T], mparts[:, 0, :], ALU.subtract)\
                        .then_inc(m1_ready, 1)
                    dve.wait_ge(m1_ready, T_.now("group"))
                    dve.sem_inc(prep_free, 1)
                elif kind == "pv":
                    dve.wait_ge(prep_full, n)
                    o = prep[:, 0:2 * P].rearrange("p (q h c) -> p q h c", q=QT, h=GH)
                    own(nc.vector.reciprocal(rec[:], o[:, :, :, HD]))
                    nc.vector.tensor_tensor(
                        attn[:, :, 32 * g:32 * g + 32].rearrange("p q (h d) -> p q h d", h=GH), o[:, :, :, 0:HD],
                        rec[:].rearrange("p q (h a) -> p q h a", a=1).to_broadcast([P, QT, GH, HD]), ALU.mult)\
                        .then_inc(prep_free, 1)
                    if g == G - 1:
                        dve.wait_ge(prep_free, n)
                        own(nc.vector.tensor_tensor(attn[:, 0, :], attn[:, 0, :], rows[:, 0, :], ALU.add))
                        own(nc.vector.tensor_tensor(attn[:, 1, :], attn[:, 1, :], rows[:, 0, :], ALU.add))
                        dve.sem_inc(attn_ready, 1)
                elif kind == "out":
                    dve.wait_ge(resid_ready, T_.up("out"))
                    dve.wait_ge(prep_full, n)
                    nc.vector.tensor_tensor(t["x"][:, bass.ds(b * QT, QT), :],
                                            prep[:, 0:2 * P].rearrange("p (q d) -> p q d", q=QT), resid[:], ALU.add)\
                        .then_inc(x_done, 1)
                    dve.wait_ge(x_done, T_.now("out"))
                    dve.sem_inc(prep_free, 1)

            def prologue():
                norm_stats(0)
                nc.vector.memset(zeros[:], 0.0).then_inc(ones_set, 1)
                norm_scale(0)
                dve.wait_ge(qf_ready, 1)
                own(nc.vector.tensor_tensor(qrest[:], qf[:], qparts[:, 0, :], ALU.subtract))
                own(nc.vector.tensor_copy(qparts[:, 1, :], qrest[:]))
                nc.vector.tensor_tensor(qparts[:, 2, :], qrest[:], qparts[:, 1, :], ALU.subtract).then_inc(q_split, 1)
                nc.vector.memset(v_aug[:], 1.0).then_inc(ones_set, 1)
                T_.up("item", 14)
                for u in range(UNITS_B):
                    unit(u)
                item("m", 0, 0)
                for u in range(UNITS_B - HEAD):
                    unit(u)

            def part(i, r, first, last):
                b = B - 1 if last else i
                for n in range(KT):
                    if r == 0 and n == 0 and not last:
                        norm_stats(i + 1)
                    if r == 0 and n == 2 and not last:
                        norm_scale(i + 1)
                    if units_left(r, n, last):
                        for u in units_of_step(n):
                            unit(u)
                    it = prep_item(r, n, first, last)
                    if it:
                        item(*it, b)

            parts_of_program(dve, T_, prologue, part)
            for it in (("pv", 3), ("attnT", 0), ("out", 0)):
                item(*it, B - 1)

        @block.scalar
        def _(act):
            T_ = Tally(PER)

            def item(kind, g):
                n = T_.up("item")
                if kind in ("pv", "out"):
                    return
                act.wait_ge(prep_full, n)
                if kind == "ctx":
                    cols = min(4 * P, SKV - 4 * P * g)
                    nc.scalar.activation(ctxT[:, 4 * P * g:4 * P * g + cols], prep[0:DC, 0:cols], ACT.Copy).then_inc(prep_free, 1)
                elif kind == "k":
                    lo, hi = CHUNKS[g]
                    v = T_.up("kchunk")
                    wait(act, k_split, T_.now("kchunk", 2))
                    wait(act, k_bounced, T_.now("kdma"))
                    if g == 3:
                        T_.up("kdma", BOUNCES * 16)
                    nc.scalar.activation(kf[:, g % 2, 0:hi - lo], prep[:, 0:hi - lo], ACT.Identity, bias=bk[:])
                    nc.scalar.activation(kparts[:, 0, lo:hi], prep[:, 0:hi - lo], ACT.Identity, bias=bk[:]).then_inc(kf_ready, 1)
                    act.wait_ge(kf_ready, v)
                    act.sem_inc(prep_free, 1)
                elif kind == "x":
                    nc.scalar.activation(xT[:], prep[:, 0:T], ACT.Copy).then_inc(prep_free, 1)
                elif kind == "q":
                    v = T_.up("batch")
                    wait(act, q_bounced, T_.now("dma"))
                    T_.up("dma", BOUNCES * 16)
                    nc.scalar.activation(qf[:], prep[:, 0:T], ACT.Identity, bias=bq[:])
                    nc.scalar.activation(qparts[:, 0, :], prep[:, 0:T], ACT.Identity, bias=bq[:]).then_inc(qf_ready, 1)
                    act.wait_ge(qf_ready, v)
                    act.sem_inc(prep_free, 1)
                elif kind == "v":
                    wait(act, v_placed, T_.now("half"))
                    if g == 3:
                        T_.up("half", 2)
                        nc.scalar.activation(v_new[0:tile_rows(KT - 1), KT - 1, :], prep[0:tile_rows(KT - 1), 0:D], ACT.Copy)\
                            .then_inc(v_evacuated, 1)
                    else:
                        nc.scalar.activation(v_new[:, 4 * g:4 * g + 4, :], prep[:, 0:4 * D].rearrange("p (k d) -> p k d", k=4),
                                             ACT.Copy).then_inc(v_evacuated, 1)
                    act.wait_ge(v_evacuated, T_.up("vchunk"))
                    act.sem_inc(prep_free, 1)
                elif kind == "m":
                    nc.scalar.activation(mparts[:, 0, :], prep[0:GH, 0:T], ACT.Copy).then_inc(m0_ready, 1)
                elif kind == "attnT":
                    nc.scalar.activation(attnT[:], prep[:, 0:T], ACT.Copy).then_inc(prep_free, 1)

            def copy_pv():
                act.wait_ge(pv_done, T_.now("step"))
                nc.scalar.activation(pvs[:], pv, ACT.Copy).then_inc(pv_copied, 1)

            def prologue():
                act.wait_ge(w_loaded, N_W * 16)
                for it in PROLOGUE_ITEMS:
                    item(*it)

            def part(i, r, first, last):
                for n in range(KT):
                    v = T_.up("step")
                    act.wait_ge(st_full, v)
                    wait(act, pv_done, T_.now("step", 2))
                    k, buf = tile_rows(n), (T_.n["step"] - 1) % 2
                    nc.scalar.activation(prob[0:k, buf, :].rearrange("p (a c) -> p a c", a=2),
                                         psum[0:k, 4 + 2 * buf:6 + 2 * buf, :], ACT.Exp, scale=HD ** -0.5)\
                        .then_inc(exp_done, 1)
                    if n == 0 and not first:
                        T_.up("step", -1)
                        copy_pv()
                        T_.up("step")
                    it = prep_item(r, n, first, last)
                    if it:
                        item(*it)

            parts_of_program(act, T_, prologue, part)
            copy_pv()
            for it in (("pv", 3), ("attnT", 0), ("out", 0)):
                item(*it)

        @block.tensor
        def _(pe):
            T_ = Tally(PER)
            pending = []

            def item(kind, g):
                n = T_.up("item")
                wait(pe, prep_free, T_.now("item", 1))
                if kind == "ctx":
                    if g == 0:
                        pe.wait_ge(ctx_loaded, T_.up("ctx", 32))
                    for j, kt in enumerate(range(4 * g, min(4 * g + 4, KT))):
                        k = tile_rows(kt)
                        last = nc.tensor.transpose(prep[0:DC, j * P:j * P + k], ctx_sb[0:k, kt, :], ident[0:k, 0:k])
                    last.then_inc(prep_full, 1)
                    if g == 3:
                        pe.wait_ge(prep_full, n)
                        pe.sem_inc(ctx_used, 1)
                elif kind == "k":
                    lo, hi = CHUNKS[g]
                    nc.tensor.matmul(prep[:, 0:hi - lo], wkv[:, 0:D], ctxT[:, lo:hi], start=True, stop=True).then_inc(prep_full, 1)
                elif kind == "x":
                    pe.wait_ge(xn_ready, T_.up("batch"))
                    for q in range(QT):
                        last = nc.tensor.transpose(prep[:, q * P:(q + 1) * P], s["xn"][:, q, :], ident[:])
                    last.then_inc(prep_full, 1)
                elif kind == "q":
                    nc.tensor.matmul(prep[:, 0:T], wq[:], xT[:], start=True, stop=True).then_inc(prep_full, 1)
                elif kind == "v":
                    for j, kt in enumerate(range(4 * g, min(4 * g + 4, KT))):
                        k = tile_rows(kt)
                        last = nc.tensor.matmul(prep[0:k, j * D:(j + 1) * D], ctxT[:, kt * P:kt * P + k], wkv[:, D:2 * D],
                                                start=True, stop=True)
                    last.then_inc(prep_full, 1)
                elif kind == "m":
                    pe.wait_ge(mneg_ready, T_.up("mneg"))
                    for q in range(QT):
                        last = nc.tensor.transpose(prep[0:GH, q * P:(q + 1) * P], mneg[:, q, :], ident[:])
                    last.then_inc(prep_full, 1)
                elif kind == "pv":
                    pe.wait_ge(pv_copied, T_.up("group"))
                    for q in range(QT):
                        last = nc.tensor.transpose(prep[:, q * P:(q + 1) * P], pvs[:, q * P:(q + 1) * P], ident[:])
                    last.then_inc(prep_full, 1)
                elif kind == "attnT":
                    pe.wait_ge(attn_ready, T_.up("out"))
                    for q in range(QT):
                        last = nc.tensor.transpose(prep[:, q * P:(q + 1) * P], attn[:, q, :], ident[:])
                    last.then_inc(prep_full, 1)
                elif kind == "out":
                    for q in range(QT):
                        last = nc.tensor.matmul(prep[:, q * D:(q + 1) * D], attnT[:, q * P:(q + 1) * P], wo[:],
                                                start=True, stop=True)
                    last.then_inc(prep_full, 1)

            def unit(g, u):
                T_.up("unit")
                wait(pe, max_done, T_.now("unit", 2))
                q, c, hh = u // (4 * GH), u // GH % 4, u % GH
                lo, hi = CHUNKS[c]
                h = g * GH + hh
                nc.tensor.matmul(psum[:, 2 + u % 2, 0:hi - lo], queries_of(qst, h, slice(q * P, q * P + P)),
                                 keys_of(kst, h, slice(lo, hi)), start=True, stop=True).then_inc(max_full, 1)

            def values():
                g, kt, buf, back = pending.pop()
                pe.wait_ge(exp_done, T_.now("step", back))
                k = tile_rows(kt)
                for hh in range(GH):
                    c = (hh % 2) * 2 * T + (hh // 2) * T
                    last = nc.tensor.matmul(pv[32 * hh:32 * hh + 32, :], v_aug[0:k, kt, g * GH + hh, :],
                                            prob[0:k, buf, c:c + T], start=(kt == 0), stop=(kt == KT - 1),
                                            tile_position=(0, 32 * hh))
                last.then_inc(pv_done, 1)

            def prologue():
                pe.wait_ge(w_loaded, N_W * 16)
                for it in PROLOGUE_ITEMS[:-1]:
                    item(*it)
                pe.wait_ge(half_stacked, 4 * 16)
                for u in range(UNITS_B):
                    unit(0, u)
                item(*PROLOGUE_ITEMS[-1])
                for u in range(UNITS_B - HEAD):
                    unit(1, u)

            def part(i, r, first, last):
                g = (r + 1) % 4
                for n in range(KT):
                    T_.up("step")
                    if n == 0:
                        pe.wait_ge(m_stacked, T_.up("m_stacked", 64))
                    wait(pe, exp_done, T_.now("step", 2))
                    k, buf = tile_rows(n), (T_.n["step"] - 1) % 2
                    for hh in range(GH):
                        h = g * GH + hh
                        lastmm = nc.tensor.matmul(psum[0:k, 4 + 2 * buf + hh % 2, (hh // 2) * T:(hh // 2) * T + T],
                                                  keys_of(kst, h, slice(n * P, n * P + k)),
                                                  queries_of(qst, h, slice(0, T)), start=True, stop=True)
                    lastmm.then_inc(st_full, 1)
                    units = units_of_step(n) if units_left(r, n, last) else []
                    for u in units[:1]:
                        unit_group = (g + 1) % 4 if n < M_STEP else (g + 2) % 4
                        if u == 0 and unit_group % 2 == 0:
                            pe.wait_ge(stacked, T_.up("stacked", 4 * 16))
                        unit(unit_group, u)
                    if n == 1 and not first:
                        pe.wait_ge(pv_copied, T_.now("group", -1))
                    if n == 1 and r == 3:
                        pe.wait_ge(v_placed, T_.up("placed", 2 if first else 1))
                    if n == 1 and r == 1:
                        pe.wait_ge(v_placed, T_.now("placed"))
                    for u in units[1:2]:
                        unit(unit_group, u)
                    it = prep_item(r, n, first, last)
                    if it:
                        item(*it)
                    if pending:
                        values()
                    pending.append((g, n, buf, 1))
                    for u in units[2:]:
                        unit(unit_group, u)
                if r == 3 and not first:
                    T_.up("placed")

            parts_of_program(pe, T_, prologue, part)
            pending[0] = pending[0][:3] + (0,)
            values()
            for it in (("pv", 3), ("attnT", 0), ("out", 0)):
                item(*it)


C_ITEMS = {0: [("c", 1)], 1: [("v", 0)], 2: [("c", 2), ("v", 1)], 4: [("c", 3), ("v", 2)],
           5: [("o", 0), ("v", 3)], 6: [("c", 0)]}
C_PREV = (("c", 1), ("c", 2), ("c", 3), ("o", 0))
SCORES_LAG, TURN_LAG, VALUES_LAG = 2, 3, 4


def c_items(slot, first, drain):
    return [it for it in C_ITEMS.get(slot, []) if not (first and it in C_PREV) and not (drain and it not in C_PREV)]


def c_unit(slot, lag, first, drain):
    n = slot - lag
    if (n < 0 and first) or (n >= 0 and drain):
        return None
    return n % UN


def rotary_attention(nc, a, t, psum, s, an_all, tables, experts_pre):
    ctx = ExitStack()
    with ctx:
        def sb(name, shape, dt=F32):
            return ctx.enter_context(nc.sbuf_tensor(name, shape, dt))

        def sem(name):
            return ctx.enter_context(nc.semaphore(name))

        w1, w2, tab, bias = tables.w1, tables.w2, tables.tab, tables.bias
        vw, ow, rows, vb, w_loaded = tables.vw, tables.ow, tables.rows, tables.vb, tables.w_loaded
        xT = sb("c_xT", [P, T])
        o = sb("c_o", [P, QT, D])
        turned = sb("c_turned", [P, 2, 2, 2, T])
        qz = sb("c_qz", [P, CH, T])
        kT = sb("c_kT", [P, UN, T])
        v_aug = sb("c_v_aug", [P, QT, CH, CD + 1])
        mneg = sb("c_mneg", [P, 2, QT, 2])
        prob = sb("c_prob", [P, 2, 2, 3 * P])
        probT = sb("c_probT", [P, 2, 2, 3 * P])
        rec = sb("c_rec", [P, 2, QT])
        att = sb("c_att", [P, QT, CH * CD])
        attT = sb("c_attT", [P, UN, T])
        item_full, item_free = sem("c_item_full"), sem("c_item_free")
        cleared = sem("c_cleared")
        var_ready, rstd_ready, xr_ready = sem("c_var_ready"), sem("c_rstd_ready"), sem("c_xr_ready")
        own_dve, own_pool = sem("c_own_dve"), sem("c_own_pool")
        proj_full, terms_ready, turned_ready = sem("c_proj_full"), sem("c_terms_ready"), sem("c_turned_ready")
        s_full, m_ready, exp_done = sem("c_s_full"), sem("c_m_ready"), sem("c_exp_done")
        tp_full, probT_ready, pv_full, att_ready = sem("c_tp_full"), sem("c_probT_ready"), sem("c_pv_full"), sem("c_att_ready")
        resid_ready, x_done = sem("c_resid_ready"), sem("c_x_done")
        v_done, passed = sem("c_v_done"), sem("c_passed")
        q_bank, k_bank, s0_bank, s1_bank = psum[:, 0, :], psum[:, 1, :], psum[:, 2, :], psum[:, 3, :]
        misc, pv_bank = psum[:, 6, :], psum[:, 7, :]
        PER = dict(unit=UN, scores=UN, turn=UN, values=UN, item=10, batch=1, norm=3, out=1, v=4, own_pool=2 * UN,
                   own_dve=(NORM_LINKS + RMS_LINKS) + RMS_LINKS + UN + 3)
        N_W = tables.N_W
        block = ctx.enter_context(nc.Block())

        def program(eng, tally, norm, turn_x, slot):
            def batch(i, b, first):
                for n in range(UN):
                    ahead = (lambda: norm(b, n)) if b is not None and 1 <= n <= 3 else (lambda: None)
                    slot(i, n, first, False, ahead)
                if b is not None:
                    turn_x()

            for n in range(1, 4):
                norm(0, n)
            turn_x()
            batch(0, 1, True)
            with eng.Fori(0, B - 2) as i:
                tally.enter(i)
                batch(i, i + 2, False)
                tally.leave(B - 2)
            batch(B - 2, None, False)
            for n in range(7):
                slot(B - 1, n, False, True, lambda: None)

        @block.sync
        def _(sp):
            experts_pre.load(sp)

        @block.gpsimd
        def _(pool):
            T_ = Tally(PER)
            pool.wait_ge(w_loaded, N_W * 16)

            def power():
                pool.wait_ge(var_ready, T_.up("norm"))
                nc.gpsimd.tensor_tensor(s["rstd"][:], s["ve"][:], t["neg_half"][:], ALU.pow).then_inc(rstd_ready, 1)

            def norm(b, stage):
                if stage < 3:
                    power()
                    return
                if T_.n["batch"] == 0:
                    nc.gpsimd.memset(qz[:], 0.0).then_inc(cleared, 1)
                    pool.wait_ge(cleared, 2)
                pool.wait_ge(xr_ready, T_.up("batch"))
                pool.sem_inc(passed, 1)
                for q in range(QT):
                    ins = nc.gpsimd.tensor_tensor(an_all[:, bass.ds(b * QT + q, 1), :].rearrange("p a d -> p (a d)"),
                                                  s["xr"][:, q, :], rows[:, 2, :], ALU.add)
                ins.then_inc(resid_ready, 1)

            def slot(i, n, first, drain, ahead):
                u = c_unit(n, 0, first, drain)
                if ("o", 0) in c_items(n, first, drain):
                    power()
                ahead()
                if u is not None:
                    pool.wait_ge(terms_ready, T_.up("unit"))
                    par = u % 2
                    for hh in range(2):
                        r = slice(64 * hh, 64 * hh + 64)
                        nc.gpsimd.tensor_tensor(qz[r, 2 * u + hh, :], turned[r, par, 0, 0, :], turned[r, par, 0, 1, :], ALU.add)\
                            .then_inc(own_pool, 1)
                        pool.wait_ge(own_pool, T_.up("own_pool"))
                    nc.gpsimd.tensor_tensor(kT[:, u, :], turned[:, par, 1, 0, :], turned[:, par, 1, 1, :], ALU.add)\
                        .then_inc(turned_ready, 1)
                    pool.wait_ge(turned_ready, T_.now("unit"))
            program(pool, T_, norm, lambda: None, slot)

        @block.vector
        def _(dve):
            T_ = Tally(PER)
            s2 = dict(s, xn=o, xr=t["an_cur"])

            def own(ins):
                ins.then_inc(own_dve, 1)
                dve.wait_ge(own_dve, T_.up("own_dve"))

            def item(kind, g, b):
                n = T_.up("item")
                if kind == "v":
                    dve.wait_ge(item_full, n)
                    q, half = g % 2, g // 2
                    w = CH * CD // 2
                    nc.vector.tensor_tensor(v_aug[:, q, 8 * half:8 * half + 8, 0:CD], misc.rearrange("p (h d) -> p h d", h=8),
                                            vb[:, half * w:half * w + w].rearrange("p (h d) -> p h d", h=8), ALU.add)\
                        .then_inc(v_done, 1)
                    dve.wait_ge(v_done, T_.up("v"))
                    dve.sem_inc(item_free, 1)
                elif kind == "o":
                    dve.wait_ge(resid_ready, T_.up("out"))
                    dve.wait_ge(item_full, n)
                    own(nc.vector.tensor_tensor(o[:], misc[:, 0:2 * D].rearrange("p (q d) -> p q d", q=QT),
                                                an_all[:, bass.ds(b * QT, QT), :], ALU.add))
                    dve.sem_inc(item_free, 1)
                    rms_stats(nc, own, s2, 1e-5, var_ready)

            def finish(b):
                rms_scale(nc, dve, own, s2, rows[:, 1, :], rstd_ready, T_.up("norm"))
                own(nc.vector.tensor_scalar(an_all[:, bass.ds(b * QT, QT), :], t["an_cur"][:], 1.0, None, ALU.mult))
                own(nc.vector.tensor_tensor(o[:], o[:], t["an_cur"][:], ALU.add))
                x = t["x"][:, bass.ds(b * QT, QT), :]
                nc.vector.tensor_tensor(x, x, o[:], ALU.add).then_inc(x_done, 1)

            def norm(b, stage):
                def x(q):
                    return t["x"][:, bass.ds(b * QT + q, 1), :].rearrange("p a d -> p (a d)")

                if stage == 1:
                    layer_stats(nc, own, x, s, var_ready)
                elif stage == 2:
                    layer_scale(nc, dve, own, x, s, rstd_ready, T_.up("norm"))
                    rms_stats(nc, own, s, 1e-5, var_ready)
                else:
                    rms_scale(nc, dve, own, s, rows[:, 0, :], rstd_ready, T_.up("norm"))
                    dve.sem_inc(xr_ready, 1)
                    if isinstance(b, int) and b == 0:
                        nc.vector.memset(v_aug[:], 1.0).then_inc(cleared, 1)

            def slot(i, n, first, drain, ahead):
                u = c_unit(n, SCORES_LAG, first, drain)
                if u is not None:
                    dve.wait_ge(s_full, T_.up("scores"))
                    par = u % 2
                    nc.vector.tensor_reduce(out=mneg[:, par, 0, :], in_=s0_bank[:, 0:2 * P].rearrange("p (h k) -> p h k", h=2),
                                            axis=AX.X, op=ALU.max, negate=True)
                    nc.vector.tensor_reduce(out=mneg[:, par, 1, :], in_=s1_bank.rearrange("p (h k) -> p h k", h=2),
                                            axis=AX.X, op=ALU.max, negate=True).then_inc(m_ready, 1)
                ahead()
                items = c_items(n, first, drain)
                if ("o", 0) in items:
                    item(*items.pop(0), B - 1 if drain else i)
                if n == 6 and not first:
                    finish(B - 1 if drain else i)
                u = c_unit(n, VALUES_LAG, first, drain)
                if u is not None:
                    dve.wait_ge(pv_full, T_.up("values"))
                    v = pv_bank[:, 0:4 * (CD + 1)].rearrange("p (h q c) -> p h q c", h=2, q=QT)
                    own(nc.vector.reciprocal(rec[:], v[:, :, :, CD]))
                    nc.vector.tensor_tensor(att[:, :, P * u:P * u + P].rearrange("p q (h d) -> p h q d", h=2), v[:, :, :, 0:CD],
                                            rec[:].rearrange("p h (q a) -> p h q a", a=1).to_broadcast([P, 2, QT, CD]), ALU.mult)\
                        .then_inc(att_ready, 1)
                for it in items:
                    item(*it, None)
                u = c_unit(n, 0, first, drain)
                if u is not None:
                    v = T_.up("unit")
                    dve.wait_ge(proj_full, v)
                    wait(dve, turned_ready, T_.now("unit", 2))
                    for m, bank in enumerate((q_bank, k_bank)):
                        for w in range(2):
                            ins = nc.vector.scalar_tensor_tensor(out=turned[:, u % 2, m, w, :], in0=bank[:, w * T:(w + 1) * T],
                                                                 scalar=bias[:, m, w, u:u + 1], in1=tab[:, m, w, :],
                                                                 op0=ALU.add, op1=ALU.mult)
                    ins.then_inc(terms_ready, 1)

            program(dve, T_, norm, lambda: T_.up("item"), slot)

        @block.scalar
        def _(act):
            T_ = Tally(PER)

            def turn_x():
                act.wait_ge(item_full, T_.up("item"))
                nc.scalar.activation(xT[:], misc[:, 0:T], ACT.Copy).then_inc(item_free, 1)

            def item(kind, g):
                v = T_.up("item")
                if kind == "c":
                    act.wait_ge(item_full, v)
                    nc.scalar.activation(attT[:, 2 * g:2 * g + 2, :].rearrange("p j t -> p (j t)"), misc, ACT.Copy)\
                        .then_inc(item_free, 1)

            def slot(i, n, first, drain, ahead):
                for it in c_items(n, first, drain):
                    item(*it)
                u = c_unit(n, SCORES_LAG, first, drain)
                if u is not None:
                    act.wait_ge(m_ready, T_.up("scores"))
                    wait(act, tp_full, T_.now("scores", 2))
                    par = u % 2
                    for hh in range(2):
                        nc.scalar.activation(prob[:, par, hh, 0:P], s0_bank[:, hh * P:(hh + 1) * P], ACT.Exp,
                                             bias=mneg[:, par, 0, hh:hh + 1])
                        ins = nc.scalar.activation(prob[:, par, hh, P:3 * P], s1_bank[:, hh * 2 * P:(hh + 1) * 2 * P], ACT.Exp,
                                                   bias=mneg[:, par, 1, hh:hh + 1])
                    ins.then_inc(exp_done, 1)
                u = c_unit(n, TURN_LAG, first, drain)
                if u is not None:
                    act.wait_ge(tp_full, T_.up("turn"))
                    wait(act, pv_full, T_.now("turn", 2))
                    nc.scalar.activation(probT[:, u % 2, :, :], psum[:, 4:6, 0:3 * P], ACT.Copy).then_inc(probT_ready, 1)

            program(act, T_, lambda b, n: None, turn_x, slot)

        @block.tensor
        def _(pe):
            T_ = Tally(PER)
            pe.wait_ge(w_loaded, N_W * 16)

            def item(kind, g):
                T_.up("item")
                wait(pe, item_free, T_.now("item", 1))
                if kind == "x":
                    pe.wait_ge(xr_ready, T_.up("batch"))
                    for q in range(QT):
                        last = nc.tensor.transpose(misc[:, q * P:(q + 1) * P], s["xr"][:, q, :], t["ident"][:])
                elif kind == "v":
                    q, half = g % 2, g // 2
                    if g == 0:
                        pe.wait_ge(item_free, T_.now("item", 1))
                    w = CH * CD // 2
                    last = nc.tensor.matmul(misc, xT[:, q * P:(q + 1) * P], vw[:, half * w:half * w + w], start=True, stop=True)
                elif kind == "c":
                    for j in range(2):
                        for q in range(QT):
                            last = nc.tensor.transpose(misc[:, (j * QT + q) * P:(j * QT + q + 1) * P],
                                                       att[:, q, (2 * g + j) * P:(2 * g + j + 1) * P], t["ident"][:])
                elif kind == "o":
                    for q in range(QT):
                        for j in range(UN):
                            last = nc.tensor.matmul(misc[:, q * D:(q + 1) * D], attT[:, j, q * P:(q + 1) * P], ow[:, j, :],
                                                    start=(j == 0), stop=(j == UN - 1))
                last.then_inc(item_full, 1)

            def turn_x():
                item("x", 0)

            def slot(i, n, first, drain, ahead):
                items = c_items(n, first, drain)
                if first and n == 1:
                    pe.wait_ge(cleared, 2)
                for kind, g in items[:1]:
                    if kind == "c":
                        pe.wait_ge(att_ready, T_.now("values"))
                    item(kind, g)
                u = c_unit(n, SCORES_LAG, first, drain)
                if u is not None:
                    pe.wait_ge(turned_ready, T_.up("scores"))
                    wait(pe, exp_done, T_.now("scores", 1))
                    nc.tensor.matmul(s0_bank[:, 0:2 * P], t["identb"][:], t["mask_qk0"][:, 0:2].rearrange("p h k -> p (h k)"),
                                     start=True, stop=False)
                    nc.tensor.matmul(s1_bank, t["identb"][:], t["mask_qk1"][:].rearrange("p h k -> p (h k)"), start=True, stop=False)
                    for hh in range(2):
                        nc.tensor.matmul(s0_bank[:, hh * P:(hh + 1) * P], qz[:, 2 * u + hh, 0:P], kT[:, u, 0:P],
                                         start=False, stop=(hh == 1))
                        last = nc.tensor.matmul(s1_bank[:, hh * 2 * P:(hh + 1) * 2 * P], qz[:, 2 * u + hh, P:2 * P], kT[:, u, :],
                                                start=False, stop=(hh == 1))
                    last.then_inc(s_full, 1)
                u = c_unit(n, TURN_LAG, first, drain)
                if u is not None:
                    pe.wait_ge(exp_done, T_.up("turn"))
                    wait(pe, probT_ready, T_.now("turn", 1))
                    for hh in range(2):
                        for k in range(3):
                            last = nc.tensor.transpose(psum[:, 4 + hh, k * P:(k + 1) * P], prob[:, u % 2, hh, k * P:(k + 1) * P],
                                                       t["ident"][:])
                    last.then_inc(tp_full, 1)
                u = c_unit(n, VALUES_LAG, first, drain)
                if u is not None:
                    pe.wait_ge(probT_ready, T_.up("values"))
                    wait(pe, att_ready, T_.now("values", 1))
                    if u % 4 == 0:
                        pe.wait_ge(v_done, T_.up("v", 2))
                    for hh in range(2):
                        for q in range(QT):
                            c = (hh * QT + q) * (CD + 1)
                            for kt in range(q + 1):
                                last = nc.tensor.matmul(pv_bank[:, c:c + CD + 1], probT[:, u % 2, hh, (q + kt) * P:(q + kt + 1) * P],
                                                        v_aug[:, kt, 2 * u + hh, :], start=(kt == 0), stop=(kt == q))
                    last.then_inc(pv_full, 1)
                for kind, g in items[1:]:
                    item(kind, g)
                u = c_unit(n, 0, first, drain)
                if u is not None:
                    T_.up("unit")
                    if n == 0:
                        pe.wait_ge(item_free, T_.now("item") if not any(it == ("c", 1) for it in c_items(n, first, drain)) else T_.now("item", 1))
                    wait(pe, terms_ready, T_.now("unit", 1))
                    for m, bank in enumerate((q_bank, k_bank)):
                        for w, weights in enumerate((w1, w2)):
                            last = nc.tensor.matmul(bank[:, w * T:(w + 1) * T], weights[:, m, u * P:(u + 1) * P], xT[:],
                                                    start=True, stop=True)
                    last.then_inc(proj_full, 1)

            program(pe, T_, lambda b, n: None, turn_x, slot)


NE = 31
TOP = 3
WCH = 4
TW = B * T // WCH


class ExpertLoads:

    def __init__(self, a, sb, sem):
        self.a = a
        self.rw, self.rb = sb("g_rw", [P, NE]), sb("g_rb", [P, NE])
        self.b1, self.b2 = sb("g_b1", [32, P]), sb("b2", [32, D])
        self.w = sb("e_w", [P, 2, 2, P])
        self.loaded, self.w_loaded = sem("g_loaded"), [sem("e_w_loaded0"), sem("e_w_loaded1")]

    N_W = 6

    def load(self, sp):
        a = self.a
        sp.dma_start(self.rw[:], a["L0_ffn_router_w"]).then_inc(self.loaded, 16)
        sp.dma_start(self.rb[:], a["L0_ffn_router_b"].rearrange("(a e) -> a e", a=1).to_broadcast([P, NE])).then_inc(self.loaded, 16)
        for dst, name, shared in ((self.b1, "re_b1", "sh_b1"), (self.b2, "re_b2", "sh_b2")):
            sp.dma_start(dst[0:NE, :], a["L0_ffn_" + name]).then_inc(self.loaded, 16)
            sp.dma_start(dst[NE:32, :], a["L0_ffn_" + shared].rearrange("(a d) -> a d", a=1)).then_inc(self.loaded, 16)
        for j, e in enumerate((None, 0)):
            self.load_expert(sp, e, j)

    def load_expert(self, sp, e, j):
        for m in range(2):
            if e is None:
                src = self.a["L0_ffn_sh_w%d" % (m + 1)]
            else:
                v = self.a["L0_ffn_re_w%d" % (m + 1)]
                src = v[e, :, :] if isinstance(e, int) else v[bass.ds(e, 1), :, :].rearrange("a p d -> p (a d)")
            sp.dma_start(self.w[:, j, m, :], src).then_inc(self.w_loaded[j], 16)


def gates_of_experts(nc, a, t, psum, d, pre):
    ctx = ExitStack()
    with ctx:
        def sb(name, shape, dt=F32):
            return ctx.enter_context(nc.sbuf_tensor(name, shape, dt))

        def sem(name):
            return ctx.enter_context(nc.semaphore(name))

        NT = B * QT
        PAD = 40
        rw, rb, b1, loaded = pre.rw, pre.rb, pre.b1, pre.loaded
        lg = sb("g_lg", [P, NT, NE])
        mx, sm = sb("g_mx", [P, NT]), sb("g_sm", [P, NT])
        aff, cut = sb("g_aff", [P, NT, PAD]), sb("g_cut", [P, NT, PAD])
        top = sb("g_top", [P, NT, 8])
        gates = sb("g_gates", [P, NT, 32])
        own = sem("g_own")
        turned, copied, logits, sums = sem("g_turned"), sem("g_copied"), sem("g_logits"), sem("g_sums")
        exp_done, gates_ready = sem("g_exp_done"), sem("g_gates_ready")
        gates_turned, gates_copied = sem("g_gates_turned"), sem("g_gates_copied")
        N_W = pre.N_W
        block = ctx.enter_context(nc.Block())

        @block.sync
        def _(sp):
            for c in range(WCH):
                cols = slice(c * TW, (c + 1) * TW)
                sp.wait_ge(gates_copied, c + 1)
                sp.dma_start(d["gates"][:, cols], d["gatesT"][:, cols]).then_inc(d["stored"], 16)

        @block.vector
        def _(dve):
            n = 0

            def link(ins):
                nonlocal n
                n += 1
                ins.then_inc(own, 1)
                dve.wait_ge(own, n)

            def wide(v, w):
                return v.rearrange("p (t a) -> p t a", a=1).to_broadcast([P, NT, w])

            nc.vector.memset(aff[:], -1.0)
            dve.wait_ge(loaded, N_W * 16)
            dve.wait_ge(logits, 1)
            link(nc.vector.tensor_tensor(lg[:], psum[:, 4, :].rearrange("p (t e) -> p t e", e=32)[:, :, 0:NE],
                                         rb[:].rearrange("p (a e) -> p a e", a=1).to_broadcast([P, NT, NE]), ALU.add))
            link(nc.vector.tensor_reduce(out=mx[:], in_=lg[:], axis=AX.X, op=ALU.max))
            link(nc.vector.tensor_tensor(lg[:], lg[:], wide(mx[:], NE), ALU.subtract))
            dve.sem_inc(sums, 1)
            dve.wait_ge(exp_done, 1)
            link(nc.vector.tensor_reduce(out=sm[:], in_=lg[:], axis=AX.X, op=ALU.add))
            link(nc.vector.reciprocal(sm[:], sm[:]))
            link(nc.vector.tensor_tensor(aff[:, :, 0:NE], lg[:], wide(sm[:], NE), ALU.mult))
            for k in range(NT):
                ins = nc.vector.max(top[:, k, :], aff[:, k, :])
            link(ins)
            link(nc.vector.memset(top[:, :, TOP:8], -1.0))
            for k in range(NT):
                ins = nc.vector.match_replace(out=cut[:, k, :], in_to_replace=top[:, k, :], in_values=aff[:, k, :], imm_value=-2.0)
            link(ins)
            link(nc.vector.tensor_tensor(cut[:, :, 0:NE], cut[:, :, 0:NE], aff[:, :, 0:NE], ALU.not_equal))
            link(nc.vector.memset(gates[:, :, NE:32], 1.0))
            nc.vector.tensor_tensor(gates[:, :, 0:NE], cut[:, :, 0:NE], aff[:, :, 0:NE], ALU.mult).then_inc(gates_ready, 1)

        @block.scalar
        def _(act):
            for c in range(WCH):
                act.wait_ge(turned, c + 1)
                nc.scalar.activation(d["anT"][:, c * TW:(c + 1) * TW], psum[:, c, :], ACT.Copy).then_inc(copied, 1)
            act.wait_ge(turned, WCH + 1)
            nc.scalar.activation(d["b1T"][:], psum[:, 5, 0:32], ACT.Copy).then_inc(copied, 1)
            act.wait_ge(sums, 1)
            nc.scalar.activation(lg[:], lg[:], ACT.Exp).then_inc(exp_done, 1)
            for c in range(WCH):
                act.wait_ge(gates_turned, c + 1)
                nc.scalar.activation(d["gatesT"][:, c * TW:(c + 1) * TW], psum[0:32, c, :], ACT.Copy).then_inc(gates_copied, 1)

        @block.tensor
        def _(pe):
            per = NT // WCH
            for c in range(WCH):
                for k in range(per):
                    ins = nc.tensor.transpose(psum[:, c, k * P:(k + 1) * P], d["an"][:, c * per + k, :], t["ident"][:])
                ins.then_inc(turned, 1)
            pe.wait_ge(loaded, N_W * 16)
            nc.tensor.transpose(psum[:, 5, 0:32], b1[:], t["ident"][0:32, 0:32]).then_inc(turned, 1)
            for k in range(NT):
                if k % per == 0:
                    pe.wait_ge(copied, k // per + 1)
                ins = nc.tensor.matmul(psum[:, 4, k * 32:k * 32 + NE], d["anT"][:, k * P:(k + 1) * P], rw[:], start=True, stop=True)
            ins.then_inc(logits, 1)
            pe.wait_ge(copied, WCH + 1)
            pe.wait_ge(gates_ready, 1)
            for c in range(WCH):
                for k in range(c * per, (c + 1) * per):
                    cols = slice((k % per) * P, (k % per + 1) * P)
                    ins = nc.tensor.transpose(psum[0:32, c, cols], gates[:, k, :], t["ident"][:])
                ins.then_inc(gates_turned, 1)


def experts(nc, a, t, psum, d, out, pre):
    ctx = ExitStack()
    with ctx:
        def sb(name, shape, dt=F32):
            return ctx.enter_context(nc.sbuf_tensor(name, shape, dt))

        def sem(name):
            return ctx.enter_context(nc.semaphore(name))

        w, w_loaded = pre.w, pre.w_loaded
        gate_row = [sb("e_gate_row%d" % j, [1, WCH * TW]) for j in range(2)]
        gate = [sb("e_gate%d" % j, [P, WCH * TW]) for j in range(2)]
        BUFS, LAG = 4, 2
        gl = sb("e_gl", [P, BUFS, TW])
        hg = sb("e_hg", [P, BUFS, TW])
        yT = sb("e_yT", [P, WCH, TW])
        h_full, gelu_done, passed = sem("e_h_full"), sem("e_gelu_done"), sem("e_passed")
        row_loaded = [sem("e_row_loaded0"), sem("e_row_loaded1")]
        g_full, hg_ready, y_done = sem("e_g_full"), sem("e_hg_ready"), sem("e_y_done")
        b2_done, y_copied, y_turned, x_done, stored = (sem("e_b2_done"), sem("e_y_copied"), sem("e_y_turned"),
                                                       sem("e_x_done"), sem("e_stored"))
        ROUNDS = NE // 2
        STEPS = 2 * WCH
        PER = dict(step=STEPS, y=STEPS, load=1, expert=2)
        block = ctx.enter_context(nc.Block())

        def program(tally, eng, part):
            for k in range(STEPS):
                part(None, k)
            with eng.Fori(0, ROUNDS) as i:
                tally.enter(i)
                for k in range(STEPS):
                    part(i, k)
                tally.leave(ROUNDS)

        @block.sync
        def _(sp):
            T_ = Tally(PER)

            def load_row(row, j):
                sp.dma_start(gate_row[j][:], d["gates"][row, :]).then_inc(row_loaded[j], 16)

            sp.wait_ge(d["stored"], WCH * 16)
            load_row(slice(NE, NE + 1), 0)
            load_row(slice(0, 1), 1)
            T_.n["y"] = 0
            with sp.Fori(0, ROUNDS) as i:
                T_.enter(i)
                for j in range(2):
                    sp.wait_ge(hg_ready, T_.up("y", WCH))
                    sp.sem_inc(passed, 1)
                    load_row(bass.ds(i * 2 + 1 + j, 1), j)
                    sp.wait_ge(y_done, T_.now("y"))
                    sp.sem_inc(passed, 1)
                    pre.load_expert(sp, i * 2 + 1 + j, j)
                T_.leave(ROUNDS)
            for c in range(WCH):
                sp.wait_ge(x_done, c + 1)
                sp.dma_start(out.rearrange("b (q p) d -> p (b q) d", p=P)[:, c * 4:(c + 1) * 4, :], t["x"][:, c * 4:(c + 1) * 4, :])\
                    .then_inc(stored, 16)
            sp.wait_ge(stored, WCH * 16)

        @block.gpsimd
        def _(pool):
            T_ = Tally(PER)

            def part(i, k):
                if k % WCH:
                    return
                j = k // WCH
                if j == 0:
                    T_.up("load")
                pool.wait_ge(row_loaded[j], 16 * T_.now("load"))
                pool.sem_inc(passed, 1)
                nc.gpsimd.partition_broadcast(gate[j][:], gate_row[j][:]).then_inc(g_full, 1)

            program(T_, pool, part)

        @block.scalar
        def _(act):
            T_ = Tally(PER)

            def part(i, k):
                act.wait_ge(h_full, T_.up("step"))
                wait(act, hg_ready, T_.now("step", BUFS))
                act.sem_inc(passed, 1)
                j = k // WCH
                b1 = d["b1T"][:, (NE, 0)[j]:(NE, 0)[j] + 1] if i is None else d["b1T"][:, bass.ds(i * 2 + 1 + j, 1)]
                nc.scalar.activation(gl[:, k % BUFS, :], psum[:, 4 + k % BUFS, :], ACT.Gelu, bias=b1).then_inc(gelu_done, 1)

            program(T_, act, part)
            for c in range(WCH):
                act.wait_ge(b2_done, c + 1)
                nc.scalar.activation(yT[:, c, :], psum[:, c, :], ACT.Copy).then_inc(y_copied, 1)

        @block.vector
        def _(dve):
            T_ = Tally(PER)

            def part(i, k):
                v = T_.up("step")
                j, c = divmod(k, WCH)
                if c == 0:
                    dve.wait_ge(g_full, T_.up("expert"))
                dve.wait_ge(gelu_done, v)
                wait(dve, y_done, T_.now("step", BUFS))
                nc.vector.tensor_tensor(hg[:, k % BUFS, :], gl[:, k % BUFS, :], gate[j][:, c * TW:(c + 1) * TW], ALU.mult)\
                    .then_inc(hg_ready, 1)

            program(T_, dve, part)
            for c in range(WCH):
                dve.wait_ge(y_turned, c + 1)
                x = t["x"][:, c * 4:(c + 1) * 4, :]
                nc.vector.tensor_tensor(x, x, psum[:, 4 + c, :].rearrange("p (q d) -> p q d", q=4), ALU.add).then_inc(x_done, 1)

        @block.tensor
        def _(pe):
            T_ = Tally(PER)

            def second(c, j, buf):
                pe.wait_ge(hg_ready, T_.up("y"))
                nc.tensor.matmul(psum[:, c, :], w[:, j, 1, :], hg[:, buf, :], start=second.start, stop=False).then_inc(y_done, 1)

            second.start = True

            def part(i, k):
                T_.up("step")
                j, c = divmod(k, WCH)
                if c == 0:
                    if j == 0:
                        T_.up("load")
                    pe.wait_ge(w_loaded[j], 32 * T_.now("load"))
                wait(pe, gelu_done, T_.now("step", BUFS))
                nc.tensor.matmul(psum[:, 4 + k % BUFS, :], w[:, j, 0, :], d["anT"][:, c * TW:(c + 1) * TW], start=True, stop=True)\
                    .then_inc(h_full, 1)
                if not (i is None and k < LAG):
                    second((c - LAG) % WCH, ((k - LAG) % STEPS) // WCH, (k - LAG) % BUFS)
                if i is None and k == WCH + LAG - 1:
                    second.start = False

            program(T_, pe, part)
            for c in range(WCH - LAG, WCH):
                second(c, 1, c % BUFS)
            for c in range(WCH):
                nc.tensor.matmul(psum[:, c, :], d["b2"][:], d["gatesT"][:, c * TW:(c + 1) * TW], start=False, stop=True)\
                    .then_inc(b2_done, 1)
            pe.wait_ge(hg_ready, T_.now("step"))
            for c in range(WCH):
                pe.wait_ge(y_copied, c + 1)
                for q in range(4):
                    ins = nc.tensor.transpose(psum[:, 4 + c, q * P:(q + 1) * P], yT[:, c, q * P:(q + 1) * P], t["ident"][:])
                ins.then_inc(y_turned, 1)


_NAMES = ['x', 'ctx_768', 'L0_attn_norm_w', 'L0_attn_Wq', 'L0_attn_bq', 'L0_attn_Wk', 'L0_attn_bk', 'L0_attn_Wv',
          'L0_attn_bv', 'L0_attn_Wo', 'L0_attn_bo', 'L0_xattn_Wq', 'L0_xattn_bq', 'L0_xattn_Wkv', 'L0_xattn_bkv',
          'L0_xattn_Wo', 'L0_xattn_bo', 'L0_ffn_theta', 'L0_ffn_gamma1', 'L0_ffn_gamma2', 'L0_ffn_q_w', 'L0_ffn_q_b',
          'L0_ffn_k_w', 'L0_ffn_k_b', 'L0_ffn_v_w', 'L0_ffn_v_b', 'L0_ffn_o_w', 'L0_ffn_o_b', 'L0_ffn_router_w',
          'L0_ffn_router_b', 'L0_ffn_sh_w1', 'L0_ffn_sh_b1', 'L0_ffn_sh_w2', 'L0_ffn_sh_b2', 'L0_ffn_re_w1',
          'L0_ffn_re_b1', 'L0_ffn_re_w2', 'L0_ffn_re_b2']


def kernel(**inputs):
    import numpy as _np
    import concourse.bacc as _bacc
    from concourse import mybir as _mybir
    from concourse.bass_utils import run_bass_kernel_spmd as _run

    nc = _bacc.Bacc("TRN2", target_bir_lowering=False, num_devices=1)
    arrays, args = {}, {}
    for name in _NAMES:
        v = _np.ascontiguousarray(inputs[name])
        arrays["in_" + name] = v
        args[name] = nc.dram_tensor("in_" + name, v.shape, _mybir.dt.from_np(v.dtype), kind="ExternalInput").ap()
    out = nc.dram_tensor("out_x", (B, T, D), F32, kind="ExternalOutput").ap()
    build(nc, args, out)
    r = _run(nc, [arrays], core_ids=[0])
    return r.results[0]["out_x"]
```
